# Optimizing a Trainium2 kernel written in Bass

```python
import numpy as np
import jax
import jax.numpy as jnp

def _softmax(x, axis=-1):
    return jax.nn.softmax(x, axis=axis)

def _gelu(x):
    return jax.nn.gelu(x, approximate=True)

def _silu(x):
    return jax.nn.silu(x)

def _sigmoid(x):
    return jax.nn.sigmoid(x)

def _layernorm(x, axis=-1, eps=1e-05):
    m = jnp.mean(x, axis=axis, keepdims=True)
    v = jnp.var(x, axis=axis, keepdims=True)
    return (x - m) / jnp.sqrt(v + eps)

def _scatter_add(tgt, idx, src, axis=0):
    return tgt.at[idx].add(src)

def _segment_sum(src, seg, n):
    return jax.ops.segment_sum(src, seg, n)
kernel_name = 'mk_decoder_postln_d1_seqx_r4_838ca9'

def setup_inputs(seed: int=0):
    np.random.seed(seed)
    _w = jnp.asarray

    def _rec_inputs():
        import jax
        import jax.numpy as jnp
        _rk = jax.random.key(seed)
        x = -0.0005207 + 1.001 * jax.random.normal(jax.random.fold_in(_rk, 1), (2, 512, 1024), jnp.float32)
        _lenS = 512 - jax.random.randint(jax.random.fold_in(_rk, 7), (2,), 0, max(1, 512 // 4) + 1, jnp.int32)
        _lenS2 = 1024 - jax.random.randint(jax.random.fold_in(_rk, 8), (2,), 0, max(1, 1024 // 4) + 1, jnp.int32)
        _ctx_4096P = jax.random.normal(jax.random.fold_in(_rk, 11), (2, 16, 1024), jnp.float32)
        _ctx_4096c = jax.random.dirichlet(jax.random.fold_in(_rk, 511), 0.3 * jnp.ones((16,), jnp.float32), (2, 1024))
        _ctx_4096t = jnp.einsum('bsk,bkd->bsd', _ctx_4096c, _ctx_4096P)
        _ctx_4096t = _ctx_4096t * jax.lax.rsqrt(jnp.mean(jnp.square(_ctx_4096t)) + 1e-12) * 0.953939
        ctx_4096 = -0.00010331 + 0.999899 * (_ctx_4096t + 0.3 * jax.random.normal(jax.random.fold_in(_rk, 611), (2, 1024, 1024), jnp.float32))
        return (x, ctx_4096)
    x, ctx_4096 = _rec_inputs()

    def _L0_attn_setup():
        import jax, jax.numpy as jnp
        import numpy as np
        from jax import lax
        H = 1024
        DIN = 2048
        N = 16
        K = 4
        R = 64
        B_SZ = 2
        L = 512
        EPS = 1e-06

        def rmsnorm(x, w):
            return x * lax.rsqrt(jnp.mean(x * x, axis=-1, keepdims=True) + EPS) * w

        def _selective_scan(x, dt, A, Bm, Cm):
            xT = jnp.transpose(x, (2, 0, 1))
            dtT = jnp.transpose(dt, (2, 0, 1))
            BT = jnp.transpose(Bm, (2, 0, 1))
            CT = jnp.transpose(Cm, (2, 0, 1))

            def step(h, inp):
                x_t, dt_t, B_t, C_t = inp
                dA = jnp.exp(dt_t[..., None] * A)
                dBx = dt_t[..., None] * B_t[:, None, :] * x_t[..., None]
                h = dA * h + dBx
                y = jnp.einsum('bdn,bn->bd', h, C_t)
                return (h, y)
            h0 = jnp.zeros((x.shape[0], x.shape[1], A.shape[1]), dtype=x.dtype)
            _, ys = lax.scan(step, h0, (xT, dtT, BT, CT))
            return jnp.transpose(ys, (1, 2, 0))
        key = jax.random.key(seed)
        ks = jax.random.split(key, 8)
        hidden_states = jax.random.normal(ks[0], (B_SZ, L, H), dtype=jnp.float32)
        s = 0.02
        in_proj_w = jax.random.normal(ks[1], (H, 2 * DIN), dtype=jnp.float32) * s
        conv_w = jax.random.normal(ks[2], (DIN, K), dtype=jnp.float32) * 0.2
        conv_b = jax.random.normal(ks[3], (DIN,), dtype=jnp.float32) * 0.02
        x_proj_w = jax.random.normal(ks[4], (R + 2 * N, DIN), dtype=jnp.float32) * s
        dt_proj_w = jax.random.normal(ks[5], (DIN, R), dtype=jnp.float32) * s
        dt_bias = jax.random.normal(ks[6], (DIN,), dtype=jnp.float32) * 0.5 - 4.0
        A_log = jnp.log(jnp.broadcast_to(jnp.arange(1, N + 1, dtype=jnp.float32)[None, :], (DIN, N)))
        D_param = jnp.ones((DIN,), dtype=jnp.float32)
        out_proj_w = jax.random.normal(ks[7], (H, DIN), dtype=jnp.float32) * s
        dt_ln_w = jnp.ones((R,), dtype=jnp.float32)
        B_ln_w = jnp.ones((N,), dtype=jnp.float32)
        C_ln_w = jnp.ones((N,), dtype=jnp.float32)
        return dict(hidden_states=hidden_states, in_proj_w=in_proj_w, conv_w=conv_w, conv_b=conv_b, x_proj_w=x_proj_w, dt_proj_w=dt_proj_w, dt_bias=dt_bias, A_log=A_log, D_param=D_param, out_proj_w=out_proj_w, dt_ln_w=dt_ln_w, B_ln_w=B_ln_w, C_ln_w=C_ln_w)
    _L0_attn_all = _L0_attn_setup()
    _L0_attn_in = {k: v for k, v in _L0_attn_all.items() if k in ('in_proj_w', 'conv_w', 'conv_b', 'x_proj_w', 'dt_proj_w', 'dt_bias', 'A_log', 'D_param', 'out_proj_w', 'dt_ln_w', 'B_ln_w', 'C_ln_w')}
    del _L0_attn_all

    def _L0_xattn_setup():
        import jax, jax.numpy as jnp
        import numpy as np
        B, Q, D = (8, 64, 1024)
        CTX = 1024
        H, KV, HD = (16, 4, 96)
        G = H // KV
        key = jax.random.key(seed)
        ks = jax.random.split(key, 6)
        s = 0.02
        return {'latents': jax.random.normal(ks[0], (B, Q, D), jnp.float32), 'context': jax.random.normal(ks[1], (B, CTX, D), jnp.float32), 'Wq': jax.random.normal(ks[2], (H * HD, D), jnp.float32) * s, 'Wk': jax.random.normal(ks[3], (KV * HD, D), jnp.float32) * s, 'Wv': jax.random.normal(ks[4], (KV * HD, D), jnp.float32) * s, 'Wo': jax.random.normal(ks[5], (D, H * HD), jnp.float32) * s}
    _L0_xattn_all = _L0_xattn_setup()
    _L0_xattn_in = {k: v for k, v in _L0_xattn_all.items() if k in ('Wq', 'Wk', 'Wv', 'Wo')}
    del _L0_xattn_all

    def _L0_ffn_setup():
        import jax, jax.numpy as jnp
        import numpy as np
        BS = 128
        FP8_MAX = 448.0

        def act_quant(x):
            T, K = x.shape
            xb = x.reshape(T, K // BS, BS)
            amax = jnp.max(jnp.abs(xb), axis=-1)
            scale = amax / FP8_MAX + 1e-12
            xq = (xb / scale[:, :, None]).reshape(T, K)
            return (xq, scale)

        def linear_dsv3(x, wq, w_scale):
            T, K = x.shape
            N = wq.shape[0]
            xq, xs = act_quant(x)
            xdq = (xq.reshape(T, K // BS, BS) * xs[:, :, None]).reshape(T, K)
            wdq = (wq.reshape(N // BS, BS, K // BS, BS) * w_scale[:, None, :, None]).reshape(N, K)
            return xdq @ wdq.T
        key = jax.random.key(seed)
        ks = jax.random.split(key, 4)
        DIM, INTER = (1024, 3584)

        def make_qweight(k, n, m):
            w = jax.random.normal(k, (n, m), dtype=jnp.float32) * 0.02
            wb = w.reshape(n // BS, BS, m // BS, BS)
            amax = jnp.max(jnp.abs(wb), axis=(1, 3))
            scale = amax / FP8_MAX + 1e-12
            wq = (wb / scale[:, None, :, None]).reshape(n, m)
            return (wq, scale)
        x = jax.random.normal(ks[0], (2, 256, DIM), dtype=jnp.float32)
        w1, w1_scale = make_qweight(ks[1], INTER, DIM)
        w3, w3_scale = make_qweight(ks[2], INTER, DIM)
        w2, w2_scale = make_qweight(ks[3], DIM, INTER)
        return {'x': x, 'w1': w1, 'w1_scale': w1_scale, 'w3': w3, 'w3_scale': w3_scale, 'w2': w2, 'w2_scale': w2_scale}
    _L0_ffn_all = _L0_ffn_setup()
    _L0_ffn_in = {k: v for k, v in _L0_ffn_all.items() if k in ('w1', 'w1_scale', 'w3', 'w3_scale', 'w2', 'w2_scale')}
    del _L0_ffn_all
    return {'x': x, 'ctx_4096': ctx_4096, 'L0_attn_in_proj_w': _L0_attn_in['in_proj_w'], 'L0_attn_conv_w': _L0_attn_in['conv_w'], 'L0_attn_conv_b': _L0_attn_in['conv_b'], 'L0_attn_x_proj_w': _L0_attn_in['x_proj_w'], 'L0_attn_dt_proj_w': _L0_attn_in['dt_proj_w'], 'L0_attn_dt_bias': _L0_attn_in['dt_bias'], 'L0_attn_A_log': _L0_attn_in['A_log'], 'L0_attn_D_param': _L0_attn_in['D_param'], 'L0_attn_out_proj_w': _L0_attn_in['out_proj_w'], 'L0_attn_dt_ln_w': _L0_attn_in['dt_ln_w'], 'L0_attn_B_ln_w': _L0_attn_in['B_ln_w'], 'L0_attn_C_ln_w': _L0_attn_in['C_ln_w'], 'L0_xattn_Wq': _L0_xattn_in['Wq'], 'L0_xattn_Wk': _L0_xattn_in['Wk'], 'L0_xattn_Wv': _L0_xattn_in['Wv'], 'L0_xattn_Wo': _L0_xattn_in['Wo'], 'L0_ffn_w1': _L0_ffn_in['w1'], 'L0_ffn_w1_scale': _L0_ffn_in['w1_scale'], 'L0_ffn_w3': _L0_ffn_in['w3'], 'L0_ffn_w3_scale': _L0_ffn_in['w3_scale'], 'L0_ffn_w2': _L0_ffn_in['w2'], 'L0_ffn_w2_scale': _L0_ffn_in['w2_scale']}

def reference(x, ctx_4096, L0_attn_in_proj_w, L0_attn_conv_w, L0_attn_conv_b, L0_attn_x_proj_w, L0_attn_dt_proj_w, L0_attn_dt_bias, L0_attn_A_log, L0_attn_D_param, L0_attn_out_proj_w, L0_attn_dt_ln_w, L0_attn_B_ln_w, L0_attn_C_ln_w, L0_xattn_Wq, L0_xattn_Wk, L0_xattn_Wv, L0_xattn_Wo, L0_ffn_w1, L0_ffn_w1_scale, L0_ffn_w3, L0_ffn_w3_scale, L0_ffn_w2, L0_ffn_w2_scale):
    import jax
    import jax.numpy as jnp

    def _L0_attn_ref(hidden_states, in_proj_w, conv_w, conv_b, x_proj_w, dt_proj_w, dt_bias, A_log, D_param, out_proj_w, dt_ln_w, B_ln_w, C_ln_w):
        import jax, jax.numpy as jnp
        import numpy as np
        from jax import lax
        H = 1024
        DIN = 2048
        N = 16
        K = 4
        R = 64
        B_SZ = 2
        L = 512
        EPS = 1e-06

        def rmsnorm(x, w):
            return x * lax.rsqrt(jnp.mean(x * x, axis=-1, keepdims=True) + EPS) * w

        def _selective_scan(x, dt, A, Bm, Cm):
            xT = jnp.transpose(x, (2, 0, 1))
            dtT = jnp.transpose(dt, (2, 0, 1))
            BT = jnp.transpose(Bm, (2, 0, 1))
            CT = jnp.transpose(Cm, (2, 0, 1))

            def step(h, inp):
                x_t, dt_t, B_t, C_t = inp
                dA = jnp.exp(dt_t[..., None] * A)
                dBx = dt_t[..., None] * B_t[:, None, :] * x_t[..., None]
                h = dA * h + dBx
                y = jnp.einsum('bdn,bn->bd', h, C_t)
                return (h, y)
            h0 = jnp.zeros((x.shape[0], x.shape[1], A.shape[1]), dtype=x.dtype)
            _, ys = lax.scan(step, h0, (xT, dtT, BT, CT))
            return jnp.transpose(ys, (1, 2, 0))
        proj = hidden_states @ in_proj_w
        x, z = jnp.split(proj, 2, axis=-1)
        x = jnp.transpose(x, (0, 2, 1))
        z = jnp.transpose(z, (0, 2, 1))
        Lq = x.shape[-1]
        xp = jnp.pad(x, ((0, 0), (0, 0), (K - 1, 0)))
        xc = conv_b[None, :, None]
        for k in range(K):
            xc = xc + conv_w[None, :, k:k + 1] * xp[:, :, k:k + Lq]
        xc = jax.nn.silu(xc)
        ssm_p = jnp.einsum('bdl,ed->ble', xc, x_proj_w)
        dt_r = rmsnorm(ssm_p[..., :R], dt_ln_w)
        Bm = rmsnorm(ssm_p[..., R:R + N], B_ln_w)
        Cm = rmsnorm(ssm_p[..., R + N:], C_ln_w)
        dt = jnp.einsum('blr,dr->bdl', dt_r, dt_proj_w)
        dt = jax.nn.softplus(dt + dt_bias[None, :, None])
        A = -jnp.exp(A_log)
        Bm = jnp.transpose(Bm, (0, 2, 1))
        Cm = jnp.transpose(Cm, (0, 2, 1))
        ys = _selective_scan(xc, dt, A, Bm, Cm)
        y = (ys + D_param[None, :, None] * xc) * jax.nn.silu(z)
        return jnp.einsum('bdl,hd->blh', y, out_proj_w)

    def _L0_xattn_ref(latents, context, Wq, Wk, Wv, Wo):
        import jax, jax.numpy as jnp
        import numpy as np
        B, Q, D = (8, 64, 1024)
        CTX = 1024
        H, KV, HD = (16, 4, 96)
        G = H // KV
        b, q_len, _ = latents.shape
        hidden = jnp.concatenate([context, latents], axis=1)
        s_len = hidden.shape[1]
        q = (latents @ Wq.T).reshape(b, q_len, H, HD)
        k = (hidden @ Wk.T).reshape(b, s_len, KV, HD)
        v = (hidden @ Wv.T).reshape(b, s_len, KV, HD)
        q = q.transpose(0, 2, 1, 3).reshape(b, KV, G, q_len, HD)
        k = k.transpose(0, 2, 1, 3)
        v = v.transpose(0, 2, 1, 3)
        scale = 1.0 / jnp.sqrt(jnp.asarray(HD, q.dtype))
        scores = jnp.einsum('bkgqd,bksd->bkgqs', q, k) * scale
        attn = jax.nn.softmax(scores.astype(jnp.float32), axis=-1).astype(q.dtype)
        out = jnp.einsum('bkgqs,bksd->bkgqd', attn, v)
        out = out.reshape(b, H, q_len, HD).transpose(0, 2, 1, 3).reshape(b, q_len, H * HD)
        return out @ Wo.T

    def _L0_ffn_ref(x, w1, w1_scale, w3, w3_scale, w2, w2_scale):
        import jax, jax.numpy as jnp
        import numpy as np
        BS = 128
        FP8_MAX = 448.0

        def act_quant(x):
            T, K = x.shape
            xb = x.reshape(T, K // BS, BS)
            amax = jnp.max(jnp.abs(xb), axis=-1)
            scale = amax / FP8_MAX + 1e-12
            xq = (xb / scale[:, :, None]).reshape(T, K)
            return (xq, scale)

        def linear_dsv3(x, wq, w_scale):
            T, K = x.shape
            N = wq.shape[0]
            xq, xs = act_quant(x)
            xdq = (xq.reshape(T, K // BS, BS) * xs[:, :, None]).reshape(T, K)
            wdq = (wq.reshape(N // BS, BS, K // BS, BS) * w_scale[:, None, :, None]).reshape(N, K)
            return xdq @ wdq.T
        B, S, D = x.shape
        xf = x.reshape(-1, D)
        g = linear_dsv3(xf, w1, w1_scale)
        u = linear_dsv3(xf, w3, w3_scale)
        h = jax.nn.silu(g) * u
        y = linear_dsv3(h, w2, w2_scale)
        return y.reshape(B, S, D)
    x = _layernorm(x + _L0_attn_ref(x, L0_attn_in_proj_w, L0_attn_conv_w, L0_attn_conv_b, L0_attn_x_proj_w, L0_attn_dt_proj_w, L0_attn_dt_bias, L0_attn_A_log, L0_attn_D_param, L0_attn_out_proj_w, L0_attn_dt_ln_w, L0_attn_B_ln_w, L0_attn_C_ln_w), axis=-1)
    x = _layernorm(x + _L0_xattn_ref(x, ctx_4096, L0_xattn_Wq, L0_xattn_Wk, L0_xattn_Wv, L0_xattn_Wo), axis=-1)
    x = _layernorm(x + _L0_ffn_ref(x, L0_ffn_w1, L0_ffn_w1_scale, L0_ffn_w3, L0_ffn_w3_scale, L0_ffn_w2, L0_ffn_w2_scale), axis=-1)
    return x

_drawn_inputs = setup_inputs


def setup_inputs(seed=0):
    import zlib

    import numpy as np

    out = dict(_drawn_inputs(seed))
    spreads = {'L0_attn_D_param': (1.0, 0.6),
     'L0_attn_dt_ln_w': (1.0, 0.6),
     'L0_attn_B_ln_w': (1.0, 0.6),
     'L0_attn_C_ln_w': (1.0, 0.6)}
    factors = {'L0_attn_conv_b': 8.0,
     'L0_attn_x_proj_w': 4.076,
     'L0_attn_dt_proj_w': 8.0,
     'L0_attn_dt_bias': 8.0,
     'L0_attn_A_log': 7.41,
     'L0_ffn_w1_scale': 2.839}
    for name, (base, spread) in spreads.items():
        noise = np.random.default_rng([zlib.crc32(name.encode()), seed]).standard_normal(out[name].shape)
        drawn = base * np.exp(spread * noise) if base else spread * noise
        out[name] = jnp.asarray(drawn.astype(out[name].dtype))
    for name, factor in factors.items():
        out[name] = (out[name] * factor).astype(out[name].dtype)
    return out
```

```python
from contextlib import ExitStack

import numpy as np

import concourse.bass as bass
from concourse import mybir

F32 = mybir.dt.float32
F32R = mybir.dt.float32r
ALU = mybir.AluOpType
ACT = mybir.ActivationFunctionType
AX_X = mybir.AxisListType.X

P = 128
B, L, H = 2, 512, 1024
TOK = B * L
HT = H // P
DIN, NS, R, KC = 2048, 16, 64, 4
IT = DIN // P
E = R + 2 * NS
CTX = 1024
NH, KV, HD = 16, 4, 96
G = NH // KV
S = CTX + L
ST = S // P
QT = L // P
FF = 3584
FT = FF // P
CF = 4
FC = FT // CF
RMS_EPS, LN_EPS = 1e-6, 1e-5
BASE = 16640
TOP = 229344


class Phase:

    def __init__(self, nc):
        self.nc, self.banks, self.sems = nc, ExitStack(), []

    def bank(self, name, shape):
        return self.banks.enter_context(self.nc.psum_tensor(name, shape, F32))

    def sem(self, name):
        self.sems.append(self.nc.alloc_semaphore(name))
        return self.sems[-1]

    def release(self):
        for s in self.sems:
            self.nc.sync.sem_clear(s)
            self.nc.release_semaphore(s)
        self.banks.close()


class Arena:

    def __init__(self, nc, phase, at=BASE):
        self.nc, self.phase, self.at = nc, phase, at

    def __call__(self, name, shape, dt=F32):
        size = 4
        for n in shape[1:]:
            size *= n
        size = (size + 31) // 32 * 32
        assert self.at + size <= TOP, (self.phase, name, self.at + size - TOP)
        t = self.nc.alloc_sbuf_tensor_at(f"{self.phase}_{name}", list(shape), dt, offset=self.at)
        self.at += size
        return t


def f32(ap):
    return ap.bitcast(F32)


def three_passes(nc, out, w_hi, w_lo, x_hi, x_lo, start, stop):
    nc.tensor.matmul(out, w_hi, x_hi, start=start, stop=False)
    nc.tensor.matmul(out, w_hi, x_lo, start=False, stop=False)
    return nc.tensor.matmul(out, w_lo, x_hi, start=False, stop=stop)


def mamba_in(nc, res, d, xc, ssm_n):
    sb = Arena(nc, "in")

    def sem(n):
        return res.sem("in_" + n)

    x = sb("x", [P, HT, TOK])
    x_hi = sb("x_hi", [P, HT, TOK], F32R)
    x_lo = Arena(nc, "in")("x_lo", [P, HT, TOK], F32R)
    w = [sb(f"w{s}", [P, HT, P]) for s in range(2)]
    w_hi = [sb(f"w_hi{s}", [P, HT, P], F32R) for s in range(2)]
    w_lo = [sb(f"w_lo{s}", [P, HT, P], F32R) for s in range(2)]
    xz = [sb(f"xz{s}", [P, B, L + KC - 1]) for s in range(2)]
    acc = [sb(f"acc{s}", [P, B, L]) for s in range(2)]
    pre = [sb(f"pre{s}", [P, B, L]) for s in range(2)]
    xpw = sb("xpw", [P, IT, E])
    xpw_hi = [sb(f"xpw_hi{s}", [P, E], F32R) for s in range(2)]
    xpw_lo = [sb(f"xpw_lo{s}", [P, E], F32R) for s in range(2)]
    cw = sb("cw", [P, IT, KC])
    cb = sb("cb", [P, IT])
    lnw = sb("lnw", [E, 1])
    eps = sb("eps", [E, 1])
    meanw = sb("meanw", [E, E])
    zero = sb("zero", [P, P], F32R)
    xc_hi = [sb(f"xc_hi{s}", [P, B, L], F32R) for s in range(2)]
    xc_lo = [sb(f"xc_lo{s}", [P, B, L], F32R) for s in range(2)]
    over = Arena(nc, "in_over")
    sq = over("sq", [E, B, L])
    rms = over("rms", [E, B, L])
    ssm = over("ssm", [E, B, L])
    assert sb.at <= TOP - 4 * 2 * IT * L - 4 * TOK

    ps = [res.bank(f"in_ps{s}", [P, B, L]) for s in range(2)]
    ps_xp = res.bank("in_ps_xp", [E, B, L])
    ps_ms = res.bank("in_ps_ms", [E, B, L])

    x_ld = [sem(f"x_ld{k}") for k in range(HT)]
    w_ld = [sem(f"w_ld{s}") for s in range(2)]
    par_ld, bc_st = sem("par_ld"), sem("bc_st")
    x_hi_done, x_lo_done = sem("x_hi_done"), sem("x_lo_done")
    w_hi_done, w_lo_done = sem("w_hi_done"), sem("w_lo_done")
    init_done, zeroed = sem("init_done"), sem("zeroed")
    main_done, xz_done, conv_step = sem("main_done"), sem("xz_done"), sem("conv_step")
    xc_done, xc_hi_done, xc_lo_done = sem("xc_done"), sem("xc_hi_done"), sem("xc_lo_done")
    xpw_hi_done, xpw_done, xproj_done = sem("xpw_hi_done"), sem("xpw_done"), sem("xproj_done")
    ssm_done, sq_done, ms_done = sem("ssm_done"), sem("sq_done"), sem("ms_done")
    rms_done, rr_done, n_done = sem("rms_done"), sem("rr_done"), sem("n_done")
    XP_LAST = IT + 1

    xc4 = xc[:].rearrange("p (b i) l -> p b i l", b=B)

    with nc.Block() as block:
        @block.sync
        def _(sp):
            for s in range(2):
                sp.dma_start(w[s][:], d["w_x"][s]).then_inc(w_ld[s], 16)
                for k in range(4 * s, 4 * s + 4):
                    sp.dma_start(x[:, k], d["x_t"][k]).then_inc(x_ld[k], 16)
            sp.dma_start(cw[:], d["conv_w"]).then_inc(par_ld, 16)
            sp.dma_start(cb[:], d["conv_b"]).then_inc(par_ld, 16)
            sp.dma_start(xpw[:], d["x_proj"]).then_inc(par_ld, 16)
            sp.dma_start(meanw[:], d["mean_w"]).then_inc(par_ld, 16)
            sp.dma_start(lnw[0:R], d["dt_ln"]).then_inc(par_ld, 16)
            sp.dma_start(lnw[R:R + NS], d["b_ln"]).then_inc(par_ld, 16)
            sp.dma_start(lnw[R + NS:E], d["c_ln"]).then_inc(par_ld, 16)
            with sp.Fori(0, IT // 2) as j:
                for s in range(2):
                    sp.wait_ge(w_lo_done, 2 * j + s + 1)
                    sp.dma_start(w[s][:], d["w_x"][(2 * j + s + 2) % IT]).then_inc(w_ld[s], 16)
            sp.wait_ge(n_done, 1)
            sp.dma_start(d["bc"].rearrange("b r l -> r b l"),
                         ssm_n[R:E].rearrange("r (b l) -> r b l", b=B)).then_inc(bc_st, 16)
            sp.wait_ge(bc_st, 16)
            for s in range(2):
                sp.wait_ge(w_ld[s], 16 * (IT // 2 + 1))

        @block.scalar
        def _(act):
            def split_w(s, load, tile):
                act.wait_ge(w_ld[s], load)
                nc.scalar.activation(w_hi[s][:], w[s][:], ACT.Copy).then_inc(w_hi_done, 1)

            act.sem_inc(xz_done, 1)
            split_w(0, 16, 0)
            for k in range(HT):
                act.wait_ge(x_ld[k], 16)
                nc.scalar.activation(x_hi[:, k], x[:, k], ACT.Copy).then_inc(x_hi_done, 1)
            act.wait_ge(init_done, 3)
            with act.Fori(0, IT // 2) as j:
                for s in range(2):
                    m = 2 * j + s
                    act.wait_ge(main_done, m)
                    split_w(1 - s, 16 * (j + 1 + s), m + 1)
                    act.wait_ge(main_done, m + 1)
                    act.wait_ge(conv_step, 8 * j)
                    nc.scalar.activation(xz[s][:, :, KC - 1:], ps[s][:], ACT.Copy).then_inc(xz_done, 1)
                    act.wait_ge(conv_step, 4 * m + 4)
                    nc.scalar.activation(xc4[:, :, m, :], pre[s][:], ACT.Silu).then_inc(xc_done, 1)
                    act.wait_ge(zeroed, 5)
                    act.wait_ge(xproj_done, m)
                    act.wait_ge(xc_done, m + 1)
                    nc.scalar.activation(xc_hi[s][:], xc4[:, :, m, :], ACT.Copy).then_inc(xc_hi_done, 1)
            act.wait_ge(xproj_done, XP_LAST)
            nc.scalar.activation(ssm[:], ps_xp[:], ACT.Copy).then_inc(ssm_done, 1)
            nc.scalar.activation(sq[:], ps_xp[:], ACT.Square).then_inc(sq_done, 1)
            act.wait_ge(ms_done, 1)
            nc.scalar.activation(rms[:], ps_ms[:], ACT.Sqrt, bias=eps[:, 0:1]).then_inc(rms_done, 1)

        @block.vector
        def _(dve):
            def split_w(s, n):
                dve.wait_ge(w_hi_done, n)
                nc.vector.tensor_tensor(w_lo[s][:], w[s][:], f32(w_hi[s][:]), ALU.subtract).then_inc(w_lo_done, 1)

            for s in range(2):
                nc.vector.memset(xz[s][:, :, 0:KC - 1], 0.0).then_inc(init_done, 1)
            nc.vector.memset(eps[:], RMS_EPS).then_inc(init_done, 1)
            nc.vector.memset(zero[:].bitcast(F32), 0.0).then_inc(zeroed, 1)
            nc.vector.memset(xpw_hi[1][:].bitcast(F32), 0.0).then_inc(zeroed, 1)
            nc.vector.memset(xpw_lo[1][:].bitcast(F32), 0.0).then_inc(zeroed, 1)
            nc.vector.memset(xc_hi[1][:].bitcast(F32), 0.0).then_inc(zeroed, 1)
            nc.vector.memset(xc_lo[1][:].bitcast(F32), 0.0).then_inc(zeroed, 1)
            split_w(0, 1)
            for k in range(HT):
                dve.wait_ge(x_hi_done, k + 1)
                nc.vector.tensor_tensor(x_lo[:, k], x[:, k], f32(x_hi[:, k]), ALU.subtract).then_inc(x_lo_done, 1)
            dve.wait_ge(par_ld, 16 * 7)
            with dve.Fori(0, IT // 2) as j:
                for s in range(2):
                    m = 2 * j + s
                    dve.wait_ge(main_done, m)
                    split_w(1 - s, m + 2)
                    dve.wait_ge(xpw_hi_done, m + 1)
                    nc.vector.tensor_tensor(xpw_lo[s][:], xpw[:, m, :], f32(xpw_hi[s][:]),
                                            ALU.subtract).then_inc(xpw_done, 1)
                    dve.wait_ge(xz_done, m + 2)
                    dve.wait_ge(xc_done, 2 * j)
                    nc.vector.tensor_scalar(acc[s][:], xz[s][:, :, 0:L], cw[:, m, 0:1], cb[:, bass.ds(m, 1)],
                                            ALU.mult, ALU.add).then_inc(conv_step, 1)
                    for t in range(1, KC):
                        a, o = (acc, pre) if t % 2 else (pre, acc)
                        dve.wait_ge(conv_step, 4 * m + t)
                        nc.vector.scalar_tensor_tensor(o[s][:], xz[s][:, :, t:t + L], cw[:, m, t:t + 1], a[s][:],
                                                       ALU.mult, ALU.add).then_inc(conv_step, 1)
                    dve.wait_ge(xc_hi_done, m + 1)
                    nc.vector.tensor_tensor(xc_lo[s][:], xc4[:, :, m, :], f32(xc_hi[s][:]),
                                            ALU.subtract).then_inc(xc_lo_done, 1)
            dve.wait_ge(rms_done, 1)
            nc.vector.reciprocal(sq[:], rms[:]).then_inc(rr_done, 1)
            dve.wait_ge(rr_done, 1)
            nc.vector.scalar_tensor_tensor(ssm_n[:], ssm[:].rearrange("e b l -> e (b l)"), lnw[:, 0:1],
                                           sq[:].rearrange("e b l -> e (b l)"),
                                           ALU.mult, ALU.mult).then_inc(n_done, 1)

        @block.gpsimd
        def _(pool):
            pool.wait_ge(par_ld, 16 * 7)
            pool.wait_ge(zeroed, 5)
            with pool.Fori(0, IT // 2) as j:
                for s in range(2):
                    m = 2 * j + s
                    pool.wait_ge(xproj_done, m)
                    nc.gpsimd.tensor_copy(xpw_hi[s][:], xpw[:, m, :]).then_inc(xpw_hi_done, 1)

        @block.tensor
        def _(pe):
            def main(m, s):
                pe.wait_ge(w_lo_done, m + 1)
                pe.wait_ge(xz_done, m)
                for k in range(HT):
                    pe.wait_ge(x_lo_done, k + 1)
                    for b in range(B):
                        c = slice(b * L, (b + 1) * L)
                        last = three_passes(nc, ps[s][:, b], w_hi[s][:, k], w_lo[s][:, k], x_hi[:, k, c], x_lo[:, k, c],
                                            k == 0, k == HT - 1)
                last.then_inc(main_done, 1)

            def xproj(s, ready, stop=False):
                pe.wait_ge(xc_lo_done, ready)
                pe.wait_ge(xpw_done, ready)
                for b in range(B):
                    last = three_passes(nc, ps_xp[:, b], xpw_hi[s][:], xpw_lo[s][:], xc_hi[s][:, b], xc_lo[s][:, b],
                                        False, stop)
                last.then_inc(xproj_done, 1)

            pe.wait_ge(zeroed, 5)
            pe.wait_ge(x_lo_done, 1)
            for b in range(B):
                nc.tensor.matmul(ps_xp[:, b], zero[:, 0:E], x_hi[:, 0, 0:L], start=True, stop=False)
            with pe.Fori(0, IT // 2) as j:
                for s in range(2):
                    main(2 * j + s, s)
                    xproj(1 - s, 2 * j + s)
            xproj(1, IT, stop=True)
            pe.wait_ge(sq_done, 1)
            pe.wait_ge(par_ld, 16 * 7)
            for b in range(B):
                last = nc.tensor.matmul(ps_ms[:, b], meanw[:], sq[:, b], start=True, stop=True)
            last.then_inc(ms_done, 1)


def mamba_scan(nc, res, d, xc, ssm_n):
    sb = Arena(nc, "scan")

    def sem(n):
        return res.sem("scan_" + n)

    NIT = B * IT
    NK = NS // 2
    CH = 4
    b_bc = sb("b_bc", [P, NS, L])
    c_bc = sb("c_bc", [P, NS, L])
    xb = sb("xb", [P, HT, L])
    wz = [sb(f"wz{s}", [P, HT, P]) for s in range(2)]
    dtw = [sb(f"dtw{s}", [R, P]) for s in range(2)]
    dbx = [sb(f"dbx{s}", [P, 2, L]) for s in range(2)]
    g = [sb(f"g{s}", [P, 2, L]) for s in range(2)]
    dt = [sb(f"dt{s}", [P, L]) for s in range(2)]
    u = [sb(f"u{s}", [P, L]) for s in range(2)]
    sz = [sb(f"sz{s}", [P, L]) for s in range(2)]
    yb = [sb(f"yb{s}", [P, L]) for s in range(2)]
    mag, rl, ee, ll, dd = (sb(n, [P, L]) for n in ("mag", "rl", "ee", "ll", "dd"))
    t1 = sb("t1", [P, L])
    a_neg = sb("a_neg", [P, NIT, NS])
    a_exp = mag[:].rearrange("p (i n) -> p i n", n=NS)
    dt_b = sb("dt_b", [P, NIT])
    d_p = sb("d_p", [P, NIT])
    ident = sb("ident", [P, P])
    zero = sb("zero", [P, P])
    assert sb.at <= TOP - 4 * NIT * L - 4 * TOK

    ps_a = [res.bank(f"scan_ps_a{s}", [P, 2, L]) for s in range(2)]
    ps_h = res.bank("scan_ps_h", [P, 2 * L])
    ps_y = res.bank("scan_ps_y", [P, L])
    ps_m = res.bank("scan_ps_m", [P, L])

    par_ld, x_ld = sem("par_ld"), sem("x_ld")
    bc_ld = [sem(f"bc_ld{c}") for c in range(NS // CH)]
    wz_ld = [sem(f"wz_ld{s}") for s in range(2)]
    y_st = [sem(f"y_st{s}") for s in range(2)]
    a_exp_done, a_done = sem("a_exp_done"), sem("a_done")
    init_done, y_init = sem("init_done"), sem("y_init")
    dt_mm, z_mm = sem("dt_mm"), sem("z_mm")
    mag_done, rl_done, e_done, l_done = sem("mag_done"), sem("rl_done"), sem("e_done"), sem("l_done")
    dd_done, cc_done, lr_done = sem("dd_done"), sem("cc_done"), sem("lr_done")
    dt_done, u_done, sz_done = sem("dt_done"), sem("u_done"), sem("sz_done")
    pair_free = sem("pair_free")
    g_free = sem("g_free")
    a_ready, dbx_ready, g_ready = sem("a_ready"), sem("dbx_ready"), sem("g_ready")
    t1_done, epi_done = sem("t1_done"), sem("epi_done")

    with nc.Block() as block:
        @block.sync
        def _(sp):
            sp.dma_start(a_exp[:, 0:IT, :], d["a_log"]).then_inc(par_ld, 16)
            sp.dma_start(a_exp[:, IT:NIT, :], d["a_log"]).then_inc(par_ld, 16)
            for b in range(B):
                sp.dma_start(dt_b[:, b * IT:(b + 1) * IT], d["dt_bias"]).then_inc(par_ld, 16)
                sp.dma_start(d_p[:, b * IT:(b + 1) * IT], d["d_param"]).then_inc(par_ld, 16)
            sp.dma_start(ident[:], d["ident"]).then_inc(par_ld, 16)

            def load_w(it, s):
                sp.wait_ge(z_mm, 2 * (it // 2))
                i = it % IT
                sp.dma_start(dtw[s][:], d["dt_w"][i]).then_inc(wz_ld[s], 16)
                sp.dma_start(wz[s][:], d["w_z"][i]).then_inc(wz_ld[s], 16)

            with sp.Fori(0, B) as b:
                sp.wait_ge(z_mm, IT * b)
                sp.dma_start(xb[:], d["x_tb"][b]).then_inc(x_ld, 16)
                for s in range(2):
                    load_w(IT * b + s, s)
                for c in range(NS // CH):
                    sp.wait_ge(dbx_ready, b * (NK * (IT - 1) + (c + 1) * CH // 2))
                    sp.wait_ge(g_ready, b * (NK * (IT - 1) + (c + 1) * CH // 2))
                    n = c * CH
                    sp.dma_start(b_bc[:, n:n + CH], d["bc"][b, n:n + CH].partition_broadcast(P)).then_inc(bc_ld[c], 16)
                    sp.dma_start(c_bc[:, n:n + CH],
                                 d["bc"][b, NS + n:NS + n + CH].partition_broadcast(P)).then_inc(bc_ld[c], 16)
                with sp.Fori(1, IT // 2) as j:
                    for s in range(2):
                        load_w(IT * b + 2 * j + s, s)
            load_w(NIT, 0)

        @block.scalar
        def _(act):
            def before(it, s):
                i = it % NIT
                act.wait_ge(dt_mm, it + 1)
                act.wait_ge(dt_done, it)
                nc.scalar.activation(mag[:], ps_m[:], ACT.Abs, bias=dt_b[:, bass.ds(i, 1)]).then_inc(mag_done, 1)
                nc.scalar.activation(rl[:], ps_m[:], ACT.Relu, bias=dt_b[:, bass.ds(i, 1)]).then_inc(rl_done, 1)
                act.wait_ge(mag_done, it + 1)
                nc.scalar.activation(ee[:], mag[:], ACT.Exp, scale=-1.0).then_inc(e_done, 1)
                act.wait_ge(e_done, it + 1)
                nc.scalar.activation(ll[:], ee[:], ACT.Ln, bias=1.0).then_inc(l_done, 1)

            def gate(it, s):
                act.wait_ge(z_mm, it + 1)
                act.wait_ge(epi_done, it)
                nc.scalar.activation(sz[s][:], ps_m[:], ACT.Silu).then_inc(sz_done, 1)

            act.wait_ge(par_ld, 16 * 7)
            nc.scalar.activation(a_exp, a_exp, ACT.Exp).then_inc(a_exp_done, 1)
            act.wait_ge(a_exp_done, 1)
            nc.scalar.activation(a_neg[:], a_exp, ACT.Copy, scale=-1.0).then_inc(a_done, 1)
            act.wait_ge(a_done, 1)
            before(0, 0)
            act.wait_ge(init_done, 1)
            gate(0, 0)
            with act.Fori(0, NIT // 2) as j:
                for s in range(2):
                    it = 2 * j + s
                    act.wait_ge(dt_done, it + 1)
                    for k in range(NK):
                        act.wait_ge(pair_free, NK * it + k + 1)
                        for n in range(2):
                            nc.scalar.activation(ps_a[k % 2][:, n, 1:], dt[s][:, 1:], ACT.Exp,
                                                 scale=a_neg[:, it, 2 * k + n:2 * k + n + 1]).then_inc(a_ready, 1)
                        if k == 3:
                            before(it + 1, 1 - s)
                        if k == 5:
                            act.wait_ge(epi_done, it + 1)
                            act.dma_start(d["y"][it], yb[1 - s][:]).then_inc(y_st[1 - s], 16)
                    gate(it + 1, 1 - s)
            act.wait_ge(epi_done, NIT + 1)
            act.dma_start(d["y"][NIT], yb[1][:]).then_inc(y_st[1], 16)
            act.wait_ge(y_st[1], 16 * (NIT // 2 + 1))
            act.wait_ge(y_st[0], 16 * (NIT // 2))

        @block.vector
        def _(dve):
            def after(it, s):
                i = (it + NIT - 1) % NIT
                dve.wait_ge(g_free, NK * it + 2)
                nc.vector.scalar_tensor_tensor(t1[:], xc[:, i, :], d_p[:, bass.ds(i, 1)], ps_y[:],
                                               ALU.mult, ALU.add).then_inc(t1_done, 1)
                dve.wait_ge(t1_done, it + 1)
                dve.wait_ge(sz_done, it)
                dve.wait_ge(y_st[1 - s], 16 * (it // 2))
                nc.vector.tensor_tensor(yb[1 - s][:], t1[:], sz[1 - s][:], ALU.mult).then_inc(epi_done, 1)

            def before1(it):
                dve.wait_ge(e_done, it + 1)
                nc.vector.tensor_scalar(dd[:], ee[:], 1.0, -1.0, ALU.add, ALU.add).then_inc(dd_done, 1)

            def before2(it, s):
                i = it % NIT
                dve.wait_ge(lr_done, it + 1)
                nc.vector.tensor_tensor(dt[s][:], dd[:], ll[:], ALU.add).then_inc(dt_done, 1)
                dve.wait_ge(dt_done, it + 1)
                nc.vector.tensor_tensor(u[s][:], dt[s][:], xc[:, i, :], ALU.mult).then_inc(u_done, 1)

            for s in range(2):
                nc.vector.memset(ps_a[s][:, :, 0:1], 0.0).then_inc(pair_free, 1)
            nc.vector.memset(zero[:], 0.0).then_inc(y_init, 1)
            nc.vector.memset(sz[1][:], 0.0).then_inc(init_done, 1)
            nc.vector.memset(dd[:], 0.0).then_inc(g_free, 1)
            nc.vector.memset(t1[:], 0.0).then_inc(g_free, 1)
            dve.wait_ge(par_ld, 16 * 7)
            dve.wait_ge(y_init, 2)
            dve.wait_ge(init_done, 1)
            dve.wait_ge(g_free, 2)
            before1(0)
            before2(0, 0)
            with dve.Fori(0, NIT // 2) as j:
                for s in range(2):
                    it = 2 * j + s
                    for k in range(NK):
                        n = NK * it + k
                        dve.wait_ge(a_ready, 2 * n + 2)
                        dve.wait_ge(dbx_ready, n + 1)
                        dve.wait_ge(g_ready, n)
                        nc.vector.tensor_tensor_scan(ps_h[:], ps_a[k % 2][:].rearrange("p n l -> p (n l)"),
                                                     dbx[k % 2][:].rearrange("p n l -> p (n l)"), 0.0,
                                                     ALU.mult, ALU.add).then_inc(pair_free, 1)
                        if k == 0:
                            after(it, s)
                        if k % 2 == 0:
                            dve.wait_ge(bc_ld[k // 2], 32 * (it // IT + 1))
                        dve.wait_ge(pair_free, n + 3)
                        dve.wait_ge(g_free, n + 1)
                        nc.vector.tensor_tensor(g[k % 2][:], ps_h[:].rearrange("p (n l) -> p n l", n=2),
                                                c_bc[:, 2 * k:2 * k + 2], ALU.mult).then_inc(g_ready, 1)
                        if k == 4:
                            before1(it + 1)
                        if k == 6:
                            before2(it + 1, 1 - s)
            after(NIT, 0)

        @block.gpsimd
        def _(pool):
            def before(it):
                pool.wait_ge(dd_done, it + 1)
                nc.gpsimd.tensor_tensor(dd[:], ee[:], dd[:], ALU.subtract).then_inc(cc_done, 1)
                pool.wait_ge(l_done, it + 1)
                pool.wait_ge(rl_done, it + 1)
                nc.gpsimd.tensor_tensor(ll[:], ll[:], rl[:], ALU.add).then_inc(lr_done, 1)

            before(0)
            with pool.Fori(0, NIT // 2) as j:
                for s in range(2):
                    it = 2 * j + s
                    pool.wait_ge(u_done, it + 1)
                    for k in range(NK):
                        if k % 2 == 0:
                            pool.wait_ge(bc_ld[k // 2], 32 * (it // IT + 1))
                        pool.wait_ge(pair_free, NK * it + k + 1)
                        nc.gpsimd.tensor_tensor(dbx[k % 2][:], u[s][:].unsqueeze(1).to_broadcast([P, 2, L]),
                                                b_bc[:, 2 * k:2 * k + 2], ALU.mult).then_inc(dbx_ready, 1)
                        if k == 5:
                            before(it + 1)

        @block.tensor
        def _(pe):
            def dt_product(it, s):
                b = (it // IT) % B
                pe.wait_ge(wz_ld[s], 32 * (it // 2 + 1))
                pe.wait_ge(sz_done, it)
                nc.tensor.matmul(ps_m[:], dtw[s][:], ssm_n[0:R, bass.ds(b * L, L)],
                                 start=True, stop=True).then_inc(dt_mm, 1)

            def z_product(it, s):
                pe.wait_ge(mag_done, it + 1)
                pe.wait_ge(rl_done, it + 1)
                for k in range(HT):
                    last = nc.tensor.matmul(ps_m[:], wz[s][:, k], xb[:, k], start=k == 0, stop=k == HT - 1)
                last.then_inc(z_mm, 1)

            pe.wait_ge(y_init, 1)
            pe.wait_ge(x_ld, 16)
            nc.tensor.matmul(ps_y[:], zero[:], xb[:, 0], start=True, stop=True).then_inc(y_init, 1)
            pe.wait_ge(par_ld, 16 * 7)
            dt_product(0, 0)
            z_product(0, 0)
            with pe.Fori(0, NIT // 2) as j:
                for s in range(2):
                    it = 2 * j + s
                    for k in range(NK):
                        pe.wait_ge(g_ready, NK * it + k + 1)
                        if k == 0:
                            pe.wait_ge(epi_done, it + 1)
                        for n in range(2):
                            last = nc.tensor.matmul(ps_y[:], ident[:], g[k % 2][:, n], start=k + n == 0,
                                                    stop=k == NK - 1 and n == 1)
                        last.then_inc(g_free, 1)
                        if k == 1:
                            dt_product(it + 1, 1 - s)
                        if k == 4:
                            pe.wait_ge(x_ld, 16 * (((it + 1) % NIT) // IT + 1))
                            z_product(it + 1, 1 - s)


class Norm:

    def __init__(self, nc, res, sb, phase, sq):
        def sem(n):
            return res.sem(f"{phase}_ln_{n}")

        self.nc = nc
        self.mean_w = sb("mean_w", [P, P])
        self.eps = sb("ln_eps", [P, 1])
        self.sq = sq
        self.std = sb("std", [P, B, L])
        self.rstd = sb("rstd", [P, B, L])
        self.ps_mean = res.bank(f"{phase}_ps_mean", [P, B, L])
        self.ps_var = res.bank(f"{phase}_ps_var", [P, B, L])
        self.set, self.mean_done, self.c_done, self.sq_done = sem("set"), sem("mean_done"), sem("c_done"), sem("sq_done")
        self.var_mm, self.std_done, self.rstd_done = sem("var_mm"), sem("std_done"), sem("rstd_done")
        self.out_done, self.stored = sem("out_done"), sem("stored")

    def setup(self):
        self.nc.vector.memset(self.mean_w[:], 1.0 / H).then_inc(self.set, 1)
        self.nc.vector.memset(self.eps[:], LN_EPS).then_inc(self.set, 1)

    def mean(self, v, m, start, stop):
        for b in range(B):
            last = self.nc.tensor.matmul(self.ps_mean[:, b], self.mean_w[:], v[:, m, bass.ds(b * L, L)],
                                         start=start, stop=stop)
        if stop:
            last.then_inc(self.mean_done, 1)

    def tensor(self, pe):
        for m in range(HT):
            pe.wait_ge(self.sq_done, m + 1)
            for b in range(B):
                last = self.nc.tensor.matmul(self.ps_var[:, b], self.mean_w[:], self.sq[m % 2][:, b],
                                             start=m == 0, stop=m == HT - 1)
            last.then_inc(self.var_mm, 1)

    def scalar(self, act):
        for m in range(HT):
            act.wait_ge(self.c_done, m + 1)
            if m >= 2:
                act.wait_ge(self.var_mm, m - 1)
            self.nc.scalar.activation(self.sq[m % 2][:], self.tile(m), ACT.Square).then_inc(self.sq_done, 1)
        act.wait_ge(self.var_mm, HT)
        act.wait_ge(self.set, 2)
        self.nc.scalar.activation(self.std[:], self.ps_var[:], ACT.Sqrt, bias=self.eps[:, 0:1]).then_inc(self.std_done, 1)

    def vector(self, dve):
        dve.wait_ge(self.mean_done, 1)
        for m in range(HT):
            self.nc.vector.tensor_tensor(self.tile(m), self.tile(m), self.ps_mean[:], ALU.subtract).then_inc(self.c_done, 1)
        dve.wait_ge(self.std_done, 1)
        self.nc.vector.reciprocal(self.rstd[:], self.std[:]).then_inc(self.rstd_done, 1)
        dve.wait_ge(self.rstd_done, 1)
        dve.wait_ge(self.sq_done, HT)
        dve.wait_ge(self.c_done, HT)
        for m in range(HT):
            self.nc.vector.tensor_tensor(self.tile(m), self.tile(m), self.rstd[:], ALU.mult).then_inc(self.out_done, 1)

    def sync(self, sp, v, out):
        for m in range(HT):
            sp.wait_ge(self.out_done, m + 1)
            sp.dma_start(out[m], v[:, m]).then_inc(self.stored, 16)
        sp.wait_ge(self.stored, 16 * HT)

    def over(self, v):
        self.v = v

    def tile(self, m):
        return self.v[:, m].rearrange("p (b l) -> p b l", b=B)


def project_add_norm(nc, res, phase, kt, act_src, w_dram, resid, out):
    sb = Arena(nc, phase)

    def sem(n):
        return res.sem(f"{phase}_{n}")

    KH = kt // 2
    NT = 2 * HT
    a = [sb(f"a{s}", [P, B, L]) for s in range(2)]
    a_hi = sb("a_hi", [P, kt, TOK], F32R)
    a_lo = sb("a_lo", [P, kt, TOK], F32R)
    w = [sb(f"w{s}", [P, KH, P]) for s in range(2)]
    w_hi = [sb(f"w_hi{s}", [P, KH, P], F32R) for s in range(2)]
    w_lo = [sb(f"w_lo{s}", [P, KH, P], F32R) for s in range(2)]
    v = sb("v", [P, HT, TOK])
    ln = Norm(nc, res, sb, phase, sq=a)
    ln.over(v)
    ps = res.bank(f"{phase}_ps", [P, 2, B, L])

    a_ld = [sem(f"a_ld{s}") for s in range(2)]
    w_ld = [sem(f"w_ld{s}") for s in range(2)]
    v_ld = sem("v_ld")
    a_hi_done, a_lo_done = sem("a_hi_done"), sem("a_lo_done")
    w_hi_done, w_lo_done, w_used = sem("w_hi_done"), sem("w_lo_done"), sem("w_used")
    v_done = sem("v_done")

    with nc.Block() as block:
        @block.sync
        def _(sp):
            for s in range(2):
                sp.dma_start(w[s][:], w_dram[s]).then_inc(w_ld[s], 16)
            with sp.Fori(0, kt // 2) as j:
                for s in range(2):
                    sp.wait_ge(a_lo_done, 2 * j)
                    sp.dma_start(a[s][:], act_src(2 * j + s)).then_inc(a_ld[s], 16)
            for m in range(HT):
                sp.dma_start(v[:, m], resid[m]).then_inc(v_ld, 16)
            with sp.Fori(0, HT - 1) as m:
                for s in range(2):
                    sp.wait_ge(w_lo_done, 2 * m + s + 1)
                    sp.dma_start(w[s][:], w_dram[2 * m + s + 2]).then_inc(w_ld[s], 16)
            ln.sync(sp, v, out)

        @block.scalar
        def _(act):
            def split_w(s, load):
                act.wait_ge(w_ld[s], load)
                nc.scalar.activation(w_hi[s][:], w[s][:], ACT.Copy).then_inc(w_hi_done, 1)

            split_w(0, 16)
            split_w(1, 16)
            with act.Fori(0, kt // 2) as j:
                for s in range(2):
                    act.wait_ge(a_ld[s], 16 * j + 16)
                    nc.scalar.activation(a_hi[:, 2 * j + s].rearrange("p (b l) -> p b l", b=B), a[s][:],
                                         ACT.Copy).then_inc(a_hi_done, 1)
            with act.Fori(0, HT - 1) as m:
                for s in range(2):
                    act.wait_ge(w_used, 2 * m + s + 1)
                    split_w(s, 16 * m + 32)
            ln.scalar(act)

        @block.vector
        def _(dve):
            def split_w(s, n):
                dve.wait_ge(w_hi_done, n)
                nc.vector.tensor_tensor(w_lo[s][:], w[s][:], f32(w_hi[s][:]), ALU.subtract).then_inc(w_lo_done, 1)

            def add(m):
                dve.wait_ge(w_used, 2 * m + 2)
                nc.vector.tensor_tensor(ln.tile(m), ln.tile(m), ps[:, m % 2], ALU.add).then_inc(v_done, 1)

            ln.setup()
            split_w(0, 1)
            split_w(1, 2)
            with dve.Fori(0, kt // 2) as j:
                for s in range(2):
                    dve.wait_ge(a_hi_done, 2 * j + s + 1)
                    nc.vector.tensor_tensor(a_lo[:, 2 * j + s].rearrange("p (b l) -> p b l", b=B), a[s][:],
                                            f32(a_hi[:, 2 * j + s]).rearrange("p (b l) -> p b l", b=B),
                                            ALU.subtract).then_inc(a_lo_done, 1)
            dve.wait_ge(v_ld, 16 * HT)
            with dve.Fori(0, HT - 1) as m:
                for s in range(2):
                    dve.wait_ge(w_used, 2 * m + s + 1)
                    split_w(s, 2 * m + s + 3)
                add(m)
            add(HT - 1)
            dve.wait_ge(v_done, HT)
            ln.vector(dve)

        @block.tensor
        def _(pe):
            def main(m, bank):
                for s in range(2):
                    pe.wait_ge(w_lo_done, 2 * m + s + 1)
                    for k in range(KH):
                        kk = s * KH + k
                        pe.wait_ge(a_lo_done, kk + 1)
                        for b in range(B):
                            c = slice(b * L, (b + 1) * L)
                            last = three_passes(nc, ps[:, bank, b], w_hi[s][:, k], w_lo[s][:, k],
                                                a_hi[:, kk, c], a_lo[:, kk, c], kk == 0, kk == kt - 1)
                    last.then_inc(w_used, 1)

            def mean(m, start=False, stop=False):
                pe.wait_ge(v_done, m + 1)
                ln.mean(v, m, start, stop)

            pe.wait_ge(ln.set, 2)
            main(0, 0)
            main(1, 1)
            mean(0, start=True)
            with pe.Fori(0, HT // 2 - 1) as j:
                for s in range(2):
                    main(2 * j + s + 2, s)
                    mean(2 * j + s + 1)
            mean(HT - 1, stop=True)
            ln.tensor(pe)


def kv_project(nc, res, d):
    sb = Arena(nc, "kv")

    def sem(n):
        return res.sem("kv_" + n)

    KW = KV * HD
    NCH = B * S // L
    CC = CTX // L
    wk_hi, wk_lo, wv_hi, wv_lo = (sb(n, [P, HT, KW], F32R) for n in ("wk_hi", "wk_lo", "wv_hi", "wv_lo"))
    h = [sb(f"h{s}", [P, HT, L]) for s in range(2)]
    h_hi = [sb(f"h_hi{s}", [P, HT, L], F32R) for s in range(2)]
    h_lo = [sb(f"h_lo{s}", [P, HT, L], F32R) for s in range(2)]
    kb = [sb(f"kb{s}", [HD, L]) for s in range(2)]
    vb = [sb(f"vb{s}", [P, KW]) for s in range(2)]
    wraw = [Arena(nc, f"kvw{s}", sb.at + s * 4 * HT * KW)("raw", [P, HT, KW]) for s in range(2)]
    ps_k = res.bank("kv_ps_k", [HD, 2, L])
    ps_v = res.bank("kv_ps_v", [P, 2, L])

    w_ld = [sem(f"w_ld{s}") for s in range(2)]
    h_ld = [sem(f"h_ld{s}") for s in range(2)]
    k_st = [sem(f"k_st{s}") for s in range(2)]
    v_st = [sem(f"v_st{s}") for s in range(2)]
    w_hi_done, w_lo_done = sem("w_hi_done"), sem("w_lo_done")
    h_hi_done, h_lo_done = sem("h_hi_done"), sem("h_lo_done")
    k_mm, v_mm, kb_done, vb_done = sem("k_mm"), sem("v_mm"), sem("kb_done"), sem("vb_done")
    x1 = d["x1"].rearrange("k p (b l) -> b p k l", b=B)
    NB4 = L // P

    def chunks(eng, body):
        with eng.Fori(0, B) as b:
            for c in range(CC):
                body(CC * b + c, c, b, c * L)
        for b in range(B):
            body(CC * B + b, b, b, CTX)

    with nc.Block() as block:
        @block.sync
        def _(sp):
            sp.dma_start(wraw[0][:], d["w_k"]).then_inc(w_ld[0], 16)
            sp.dma_start(h[0][:], d["ctx"][0]).then_inc(h_ld[0], 16)
            sp.dma_start(wraw[1][:], d["w_v"]).then_inc(w_ld[1], 16)
            sp.dma_start(h[1][:], d["ctx"][1]).then_inc(h_ld[1], 16)
            for q in range(2, NCH):
                sp.wait_ge(h_lo_done, q - 1)
                src = d["ctx"][q] if q < B * CC else x1[q - B * CC]
                sp.dma_start(h[q % 2][:], src).then_inc(h_ld[q % 2], 16)

        @block.scalar
        def _(act):
            def split(q, s):
                act.wait_ge(h_ld[s], 16 * (q // 2) + 16)
                act.wait_ge(v_mm, NB4 * q)
                nc.scalar.activation(h_hi[s][:], h[s][:], ACT.Copy).then_inc(h_hi_done, 1)

            def body(q, s, b, t0):
                split(q, s)
                for i in range(KV):
                    n = KV * q + i
                    act.wait_ge(k_mm, n + 1)
                    act.wait_ge(k_st[i % 2], 16 * (2 * q + i // 2))
                    nc.scalar.activation(kb[i % 2][:], ps_k[:, i % 2], ACT.Copy).then_inc(kb_done, 1)
                    act.wait_ge(kb_done, n + 1)
                    act.dma_start(d["k"][KV * b + i][:, t0:t0 + L], kb[i % 2][:]).then_inc(k_st[i % 2], 16)
                for i in range(NB4):
                    n = NB4 * q + i
                    act.wait_ge(v_mm, NB4 + n + 1)
                    act.wait_ge(v_st[i % 2], 16 * (2 * q + i // 2))
                    nc.scalar.activation(vb[i % 2][:], ps_v[:, i % 2, 0:KW], ACT.Copy).then_inc(vb_done, 1)
                    act.wait_ge(vb_done, n + 1)
                    act.dma_start(d["v"][b, :, :, t0 // P + i].rearrange("g p d -> p g d"),
                                  vb[i % 2][:].rearrange("p (g d) -> p g d", g=KV)).then_inc(v_st[i % 2], 16)

            for hi, s in ((wk_hi, 0), (wv_hi, 1)):
                act.wait_ge(w_ld[s], 16)
                nc.scalar.activation(hi[:], wraw[s][:], ACT.Copy).then_inc(w_hi_done, 1)
            chunks(act, body)
            for s in range(2):
                act.wait_ge(k_st[s], 16 * NCH * KV // 2)
                act.wait_ge(v_st[s], 16 * NCH * NB4 // 2)

        @block.vector
        def _(dve):
            def body(q, s, b, t0):
                dve.wait_ge(h_hi_done, q + 1)
                nc.vector.tensor_tensor(h_lo[s][:], h[s][:], f32(h_hi[s][:]), ALU.subtract).then_inc(h_lo_done, 1)

            for n, (hi, lo) in enumerate(((wk_hi, wk_lo), (wv_hi, wv_lo))):
                dve.wait_ge(w_hi_done, n + 1)
                nc.vector.tensor_tensor(lo[:], wraw[n][:], f32(hi[:]), ALU.subtract).then_inc(w_lo_done, 1)
            chunks(dve, body)

        @block.tensor
        def _(pe):
            def body(q, s, b, t0):
                pe.wait_ge(h_lo_done, q + 1)
                pe.wait_ge(w_lo_done, 2)
                for i in range(KV):
                    if i < 2:
                        pe.wait_ge(kb_done, KV * q)
                    else:
                        pe.wait_ge(kb_done, KV * q + i - 1)
                    c = slice(i * HD, (i + 1) * HD)
                    for k in range(HT):
                        last = three_passes(nc, ps_k[:, i % 2], wk_hi[:, k, c], wk_lo[:, k, c],
                                            h_hi[s][:, k], h_lo[s][:, k], k == 0, k == HT - 1)
                    last.then_inc(k_mm, 1)
                for i in range(NB4):
                    if i < 2:
                        pe.wait_ge(vb_done, NB4 * q)
                    else:
                        pe.wait_ge(vb_done, NB4 * q + i - 1)
                    c = slice(i * P, (i + 1) * P)
                    for k in range(HT):
                        last = three_passes(nc, ps_v[:, i % 2, 0:KW], h_hi[s][:, k, c], h_lo[s][:, k, c],
                                            wv_hi[:, k], wv_lo[:, k], k == 0, k == HT - 1)
                    last.then_inc(v_mm, 1)

            pe.sem_inc(v_mm, NB4)
            chunks(pe, body)


def attention(nc, res, d):
    sb = Arena(nc, "at")

    def sem(n):
        return res.sem("at_" + n)

    NHD = B * NH
    NW = B * KV
    SCALE = 1.0 / float(HD) ** 0.5
    NSL = 4
    LAG = 3
    x = [sb(f"x{s}", [P, TOK]) for s in range(2)]
    x_hi, x_lo = sb("x_hi", [P, HT, TOK], F32R), sb("x_lo", [P, HT, TOK], F32R)
    wq = [sb(f"wq{s}", [P, HT, HD]) for s in range(2)]
    wq_hi = [sb(f"wq_hi{s}", [P, HT, HD], F32R) for s in range(2)]
    wq_lo = [sb(f"wq_lo{s}", [P, HT, HD], F32R) for s in range(2)]
    k = sb("k", [HD, S])
    v = sb("v", [P, ST, HD])
    k_hi = [sb(f"k_hi{s}", [HD + 1, S], F32R) for s in range(2)]
    k_lo = [sb(f"k_lo{s}", [HD, S], F32R) for s in range(2)]
    v_hi = [sb(f"v_hi{s}", [P, ST, HD + 1], F32R) for s in range(2)]
    v_lo = [sb(f"v_lo{s}", [P, ST, HD + 1], F32R) for s in range(2)]
    q_hi = [sb(f"q_hi{s}", [HD + 1, L], F32R) for s in range(2)]
    q_lo = [sb(f"q_lo{s}", [HD, L], F32R) for s in range(2)]
    p = [sb(f"p{s}", [P, L]) for s in range(NSL)]
    p_hi = [sb(f"p_hi{s}", [P, L], F32R) for s in range(NSL)]
    p_lo = [sb(f"p_lo{s}", [P, L], F32R) for s in range(NSL)]
    neg_max = sb("neg_max", [P, QT, HD + 1])
    ident = sb("ident", [P, P])
    ones = sb("ones", [HD + 1, P])
    ao = sb("ao", [HD + 1, L])
    rs = sb("rs", [HD + 1, L])
    on = [sb(f"on{s}", [HD, L]) for s in range(2)]
    ones_l = sb("ones_l", [P, L])

    NB = S // L
    ps_mx = res.bank("at_ps_mx", [P, NB, L])
    ps_s = [res.bank(f"at_ps_s{s}", [P, L]) for s in range(2)]
    ps_o = res.bank("at_ps_o", [HD + 1, L])
    ps_t = res.bank("at_ps_t", [HD + 1, L])
    ps_q = res.bank("at_ps_q", [HD, L])

    x_ld = [sem(f"x_ld{s}") for s in range(2)]
    wq_ld = [sem(f"wq_ld{s}") for s in range(2)]
    on_st = [sem(f"on_st{s}") for s in range(2)]
    id_ld, kv_ld = sem("id_ld"), sem("kv_ld")
    set_done, before_done = sem("set_done"), sem("before_done")
    x_hi_done, x_lo_done = sem("x_hi_done"), sem("x_lo_done")
    wq_hi_done, wq_lo_done = sem("wq_hi_done"), sem("wq_lo_done")
    kv_hi_done, kv_lo_done = sem("kv_hi_done"), sem("kv_lo_done")
    q_mm, q_hi_done, q_lo_done = sem("q_mm"), sem("q_hi_done"), sem("q_lo_done")
    mx_mm, max_done, t_mm, row_done = sem("mx_mm"), sem("max_done"), sem("t_mm"), sem("row_done")
    s_mm, exp_done, p_hi_done, p_lo_done = sem("s_mm"), sem("exp_done"), sem("p_hi_done"), sem("p_lo_done")
    pv_mm, ao_done, rs_done, bc_mm, on_done = sem("pv_mm"), sem("ao_done"), sem("rs_done"), sem("bc_mm"), sem("on_done")

    def heads(eng, body):
        with eng.Fori(0, NW // 2) as j:
            for s in range(2):
                for g in range(G):
                    body(2 * G * j + G * s + g, 2 * j + s, g, s)

    with nc.Block() as block:
        @block.sync
        def _(sp):
            def load_kv(w):
                sp.dma_start(k[:], d["k"][w]).then_inc(kv_ld, 16)
                sp.dma_start(v[:], d["v"].rearrange("b g p t d -> (b g) p t d")[w]).then_inc(kv_ld, 16)

            def body(hd, w, g, s):
                if g == 0:
                    sp.wait_ge(kv_lo_done, 2 * w + 2)
                    load_kv((w + 1) % NW)
                sp.wait_ge(wq_lo_done, hd + 1)
                sp.dma_start(wq[g % 2][:], d["w_q"][(hd + 2) % NH]).then_inc(wq_ld[g % 2], 16)

            sp.dma_start(wq[0][:], d["w_q"][0]).then_inc(wq_ld[0], 16)
            sp.dma_start(wq[1][:], d["w_q"][1]).then_inc(wq_ld[1], 16)
            for m in range(HT):
                if m >= 2:
                    sp.wait_ge(x_lo_done, m - 1)
                sp.dma_start(x[m % 2][:], d["x1"][m]).then_inc(x_ld[m % 2], 16)
                if m == 1:
                    load_kv(0)
                    sp.dma_start(ident[:], d["ident"]).then_inc(id_ld, 16)
            heads(sp, body)
            for s in range(2):
                sp.wait_ge(wq_ld[s], 16 * (NHD // 2 + 1))
            sp.wait_ge(kv_ld, 32 * (NW + 1))

        @block.scalar
        def _(act):
            def split_wq(s, load):
                act.wait_ge(wq_ld[s], load)
                nc.scalar.activation(wq_hi[s][:], wq[s][:], ACT.Copy).then_inc(wq_hi_done, 1)

            def split_kv(w, s, used):
                act.wait_ge(kv_ld, 32 * (w + 1))
                act.wait_ge(pv_mm, NSL + used)
                nc.scalar.activation(k_hi[s][0:HD], k[:], ACT.Copy).then_inc(kv_hi_done, 1)
                nc.scalar.activation(v_hi[s][:, :, 0:HD], v[:], ACT.Copy).then_inc(kv_hi_done, 1)

            def queries(hd, s):
                act.wait_ge(q_mm, hd + 1)
                nc.scalar.activation(q_hi[s][0:HD], ps_q[:], ACT.Copy).then_inc(q_hi_done, 1)

            def leave(hd):
                act.wait_ge(pv_mm, NSL + ST * hd)
                act.wait_ge(on_done, hd)
                nc.scalar.activation(ao[:], ps_o[:], ACT.Copy).then_inc(ao_done, 1)

            def store(hd, s):
                act.wait_ge(on_done, hd + 1)
                act.dma_start(d["attn"][hd], on[s][:]).then_inc(on_st[s], 16)

            def body(hd, w, g, s):
                e = g % 2
                leave(hd)
                act.wait_ge(t_mm, hd + 1)
                nc.scalar.activation(q_hi[e][HD:HD + 1], ps_t[HD:HD + 1], ACT.Copy).then_inc(row_done, 1)
                for t in range(ST):
                    n = ST * hd + t
                    act.wait_ge(s_mm, n + 1)
                    act.wait_ge(p_lo_done, n + 1)
                    nc.scalar.activation(p[t % NSL][:], ps_s[t % 2][:], ACT.Exp, scale=SCALE).then_inc(exp_done, 1)
                    if t == 1:
                        queries(hd + 1, 1 - e)
                    if t == 3:
                        act.wait_ge(q_mm, hd + 1)
                        split_wq(e, 16 * (hd // 2) + 32)
                    if t == 5 and g == 1:
                        split_kv(w + 1, 1 - s, ST * G * w)
                    if t == 9:
                        store(hd, e)

            act.sem_inc(exp_done, 2)
            act.wait_ge(set_done, 6)
            split_wq(0, 16)
            for m in range(HT):
                act.wait_ge(x_ld[m % 2], 16 * (m // 2 + 1))
                nc.scalar.activation(x_hi[:, m], x[m % 2][:], ACT.Copy).then_inc(x_hi_done, 1)
                if m == 1:
                    split_kv(0, 0, 0)
            split_wq(1, 16)
            queries(0, 0)
            act.wait_ge(before_done, 1)
            heads(act, body)
            leave(NHD)
            store(NHD, 0)
            act.wait_ge(on_st[0], 16 * (NHD // 2 + 1))
            act.wait_ge(on_st[1], 16 * (NHD // 2))

        @block.vector
        def _(dve):
            def split_wq(s, n):
                dve.wait_ge(wq_hi_done, n)
                nc.vector.tensor_tensor(wq_lo[s][:], wq[s][:], f32(wq_hi[s][:]), ALU.subtract).then_inc(wq_lo_done, 1)

            def split_kv(w, s):
                dve.wait_ge(kv_hi_done, 2 * w + 2)
                nc.vector.tensor_tensor(k_lo[s][:], k[:], f32(k_hi[s][0:HD]), ALU.subtract).then_inc(kv_lo_done, 1)
                nc.vector.tensor_tensor(v_lo[s][:, :, 0:HD], v[:], f32(v_hi[s][:, :, 0:HD]),
                                        ALU.subtract).then_inc(kv_lo_done, 1)

            def queries(hd, s):
                dve.wait_ge(q_hi_done, hd + 1)
                nc.vector.tensor_tensor(q_lo[s][:], ps_q[:], f32(q_hi[s][0:HD]), ALU.subtract).then_inc(q_lo_done, 1)

            def maximum(hd, i):
                dve.wait_ge(mx_mm, QT * hd + i + 1)
                dve.wait_ge(t_mm, hd)
                nc.vector.tensor_reduce(neg_max[:, i, HD:HD + 1], ps_mx[:].rearrange("p n l -> p (n l)"), AX_X,
                                        ALU.max, negate=True).then_inc(max_done, 1)

            def divide1(hd):
                dve.wait_ge(ao_done, hd + 1)
                dve.wait_ge(bc_mm, hd)
                nc.vector.reciprocal(rs[HD:HD + 1], ao[HD:HD + 1]).then_inc(rs_done, 1)

            def divide2(hd, s):
                dve.wait_ge(bc_mm, hd + 1)
                dve.wait_ge(on_st[s], 16 * (hd // 2))
                nc.vector.tensor_tensor(on[s][:], ao[0:HD], ps_t[0:HD], ALU.mult).then_inc(on_done, 1)

            def body(hd, w, g, s):
                e = g % 2
                divide1(hd)
                for t in range(ST):
                    n = ST * hd + t
                    dve.wait_ge(exp_done, n + 3)
                    dve.wait_ge(pv_mm, ST * hd + t + 1)
                    nc.vector.tensor_copy(p_hi[t % NSL][:], p[t % NSL][:]).then_inc(p_hi_done, 1)
                    if t == 1:
                        queries(hd + 1, 1 - e)
                    if t == 2:
                        divide2(hd, e)
                    if t == 3:
                        split_wq(e, hd + 3)
                    if t == 5 and g == 1:
                        split_kv(w + 1, 1 - s)
                    if t in (4, 6, 8, 10):
                        maximum(hd + 1, t // 2 - 2)

            for s in range(2):
                nc.vector.memset(k_hi[s][HD:HD + 1].bitcast(F32), 1.0).then_inc(set_done, 1)
                nc.vector.memset(v_hi[s][:, :, HD:HD + 1].bitcast(F32), 1.0).then_inc(set_done, 1)
                nc.vector.memset(v_lo[s][:, :, HD:HD + 1].bitcast(F32), 0.0).then_inc(set_done, 1)
            nc.vector.memset(neg_max[:], 0.0).then_inc(set_done, 1)
            nc.vector.memset(ones[:], 1.0).then_inc(set_done, 1)
            nc.vector.memset(ones_l[:], 1.0).then_inc(set_done, 1)
            split_wq(0, 1)
            for m in range(HT):
                dve.wait_ge(x_hi_done, m + 1)
                nc.vector.tensor_tensor(x_lo[:, m], x[m % 2][:], f32(x_hi[:, m]), ALU.subtract).then_inc(x_lo_done, 1)
                if m == 1:
                    split_kv(0, 0)
            split_wq(1, 2)
            queries(0, 0)
            dve.wait_ge(set_done, 9)
            for i in range(QT):
                maximum(0, i)
            heads(dve, body)
            divide1(NHD)
            divide2(NHD, 0)

        @block.gpsimd
        def _(pool):
            def body(hd, w, g, s):
                for t in range(ST):
                    pool.wait_ge(p_hi_done, ST * hd + t + 1)
                    pool.wait_ge(pv_mm, ST * hd + t + 1)
                    nc.gpsimd.tensor_tensor(p_lo[t % NSL][:], p[t % NSL][:], f32(p_hi[t % NSL][:]),
                                            ALU.subtract).then_inc(p_lo_done, 1)

            pool.sem_inc(p_lo_done, NSL)
            heads(pool, body)

        @block.tensor
        def _(pe):
            def queries(hd, e):
                pe.wait_ge(wq_lo_done, hd + 1)
                pe.wait_ge(q_lo_done, hd)
                c = bass.ds(((hd // NH) % B) * L, L)
                for m in range(HT):
                    if isinstance(hd, int):
                        pe.wait_ge(x_lo_done, m + 1)
                    last = three_passes(nc, ps_q[:], wq_hi[e][:, m], wq_lo[e][:, m], x_hi[:, m, c], x_lo[:, m, c],
                                        m == 0, m == HT - 1)
                last.then_inc(q_mm, 1)

            def maximum(hd, w, e, s, i):
                if i == 0:
                    pe.wait_ge(q_hi_done, hd + 1)
                    pe.wait_ge(kv_hi_done, 2 * w + 1)
                pe.wait_ge(max_done, QT * hd + i)
                for c in range(NB):
                    last = nc.tensor.matmul(ps_mx[:, c], q_hi[e][0:HD, i * P:(i + 1) * P],
                                            k_hi[s][0:HD, c * L:(c + 1) * L], start=True, stop=True)
                last.then_inc(mx_mm, 1)

            def scores(hd, t, e, s):
                pe.wait_ge(exp_done, ST * hd + t + 1)
                c = slice(t * P, (t + 1) * P)
                nc.tensor.matmul(ps_s[t % 2][:], k_hi[s][:, c], q_hi[e][:], start=True, stop=False)
                nc.tensor.matmul(ps_s[t % 2][:], k_hi[s][0:HD, c], q_lo[e][:], start=False, stop=False)
                nc.tensor.matmul(ps_s[t % 2][:], k_lo[s][:, c], q_hi[e][0:HD], start=False, stop=True).then_inc(s_mm, 1)

            def values(hd, t, s):
                pe.wait_ge(p_lo_done, NSL + ST * hd + t + 1)
                three_passes(nc, ps_o[:], v_hi[s][:, t], v_lo[s][:, t], p_hi[t % NSL][:], p_lo[t % NSL][:],
                             t == 0, t == ST - 1).then_inc(pv_mm, 1)

            def broadcast():
                return nc.tensor.matmul(ps_t[0:HD], ones[HD:HD + 1, 0:HD], rs[HD:HD + 1], start=True, stop=True)

            def body(hd, w, g, s):
                e = g % 2
                pe.wait_ge(max_done, QT * hd + QT)
                pe.wait_ge(on_done, hd)
                for i in range(QT):
                    last = nc.tensor.transpose(ps_t[:, i * P:(i + 1) * P], neg_max[:, i], ident[:])
                last.then_inc(t_mm, 1)
                queries(hd + 1, 1 - e)
                pe.wait_ge(row_done, hd + 1)
                pe.wait_ge(q_lo_done, hd + 1)
                if g == 0:
                    pe.wait_ge(kv_lo_done, 2 * w + 2)
                for t in range(ST):
                    scores(hd, t, e, s)
                    if t == 1:
                        pe.wait_ge(rs_done, hd + 1)
                        broadcast().then_inc(bc_mm, 1)
                    if t >= LAG:
                        if t == LAG:
                            pe.wait_ge(ao_done, hd + 1)
                        values(hd, t - LAG, s)
                    if t in (3, 5, 7, 9):
                        nw = w + 1 if g == G - 1 else w
                        maximum(hd + 1, nw, 1 - e, 1 - s if g == G - 1 else s, t // 2 - 1)
                for t in range(ST - LAG, ST):
                    values(hd, t, s)

            pe.sem_inc(pv_mm, NSL)
            pe.wait_ge(id_ld, 16)
            pe.wait_ge(set_done, 9)
            nc.tensor.matmul(ps_o[:], ones_l[:, 0:HD + 1], ones_l[:], start=True, stop=True).then_inc(before_done, 1)
            queries(0, 0)
            for i in range(QT):
                maximum(0, 0, 0, 0, i)
            heads(pe, body)
            pe.wait_ge(rs_done, NHD + 1)
            pe.wait_ge(on_done, NHD)
            broadcast().then_inc(bc_mm, 1)


def feed_forward(nc, res, d, out):
    sb = Arena(nc, "ff")

    def sem(n):
        return res.sem("ff_" + n)

    x_hi, x_lo = sb("x_hi", [P, HT, TOK], F32R), sb("x_lo", [P, HT, TOK], F32R)
    y = sb("y", [P, HT, TOK])
    h_hi, h_lo = sb("h_hi", [P, CF, B, L], F32R), sb("h_lo", [P, CF, B, L], F32R)
    w = [sb(f"w{s}", [P, HT, P]) for s in range(4)]
    w_hi = [sb(f"w_hi{s}", [P, HT, P], F32R) for s in range(4)]
    w_lo = [sb(f"w_lo{s}", [P, HT, P], F32R) for s in range(4)]
    w2 = [sb(f"w2_{s}", [P, CF, P]) for s in range(2)]
    w2_hi = [sb(f"w2_hi{s}", [P, CF, P], F32R) for s in range(2)]
    w2_lo = [sb(f"w2_lo{s}", [P, CF, P], F32R) for s in range(2)]
    sg = sb("sg", [P, B, L])
    hf = sb("hf", [P, B, L])
    scales = [sb(f"scale{n}", [P, FT * HT]) for n in range(3)]
    ln = Norm(nc, res, sb, "ff", sq=[sg, hf])
    ln.over(y)
    ps_g, ps_u = res.bank("ff_ps_g", [P, B, L]), res.bank("ff_ps_u", [P, B, L])
    ps_y = [ln.ps_mean, ln.ps_var]

    y_ld, sc_ld = sem("y_ld"), sem("sc_ld")
    w_ld = [sem(f"w_ld{s}") for s in range(4)]
    w2_ld = [sem(f"w2_ld{s}") for s in range(2)]
    x_hi_done, x_lo_done = sem("x_hi_done"), sem("x_lo_done")
    ws_done, w_hi_done, w_lo_done = sem("ws_done"), sem("w_hi_done"), sem("w_lo_done")
    w2s_done, w2_hi_done, w2_lo_done = sem("w2s_done"), sem("w2_hi_done"), sem("w2_lo_done")
    g_mm, u_mm, y_mm = sem("g_mm"), sem("u_mm"), sem("y_mm")
    sg_done, hf_done, h_hi_done, h_lo_done, y_done = (sem("sg_done"), sem("hf_done"), sem("h_hi_done"),
                                                      sem("h_lo_done"), sem("y_done"))

    with nc.Block() as block:
        @block.sync
        def _(sp):
            def load_w(f, e):
                for i, name in enumerate(("w_1", "w_3")):
                    sp.dma_start(w[2 * i + e][:], d[name][f % FT]).then_inc(w_ld[2 * i + e], 16)

            for m in range(HT):
                sp.dma_start(y[:, m], d["x2"][m]).then_inc(y_ld, 16)
                if m == 0:
                    load_w(0, 0)
                    for n, name in enumerate(("s_1", "s_3", "s_2")):
                        sp.dma_start(scales[n][:], d[name].partition_broadcast(P)).then_inc(sc_ld, 16)
            load_w(1, 1)
            for s in range(2):
                sp.dma_start(w2[s][:], d["w_2"][s]).then_inc(w2_ld[s], 16)
            with sp.Fori(0, FC) as c:
                for f in range(CF):
                    sp.wait_ge(w_lo_done, 2 * (CF * c + f) + 2)
                    load_w(CF * c + f + 2, f % 2)
                with sp.Fori(0, HT // 2) as j:
                    for s in range(2):
                        sp.wait_ge(w2_lo_done, HT * c + 2 * j + s + 1)
                        sp.dma_start(w2[s][:], d["w_2"][(HT * c + 2 * j + s + 2) % (FC * HT)]).then_inc(w2_ld[s], 16)
            for s in range(4):
                sp.wait_ge(w_ld[s], 16 * (FT // 2 + 1))
            for s in range(2):
                sp.wait_ge(w2_ld[s], 16 * (FC * HT // 2 + 1))
            ln.sync(sp, y, out)

        @block.scalar
        def _(act):
            def split_w(f, e):
                for i in range(2):
                    n = 2 * f + i
                    act.wait_ge(ws_done, n + 1)
                    act.wait_ge((g_mm, u_mm)[i], f)
                    nc.scalar.activation(w_hi[2 * i + e][:], w[2 * i + e][:], ACT.Copy).then_inc(w_hi_done, 1)

            def split_w2(n, s):
                act.wait_ge(w2s_done, n + 1)
                act.wait_ge(y_mm, n)
                nc.scalar.activation(w2_hi[s][:], w2[s][:], ACT.Copy).then_inc(w2_hi_done, 1)

            act.wait_ge(ws_done, 1)
            nc.scalar.activation(w_hi[0][:], w[0][:], ACT.Copy).then_inc(w_hi_done, 1)
            act.wait_ge(y_ld, 16 * HT)
            for m in range(HT):
                nc.scalar.activation(x_hi[:, m], y[:, m], ACT.Copy).then_inc(x_hi_done, 1)
            act.wait_ge(ws_done, 2)
            nc.scalar.activation(w_hi[2][:], w[2][:], ACT.Copy).then_inc(w_hi_done, 1)
            with act.Fori(0, FC) as c:
                for f in range(CF):
                    ff = CF * c + f
                    if f < CF - 1:
                        split_w(ff + 1, 1 - f % 2)
                    else:
                        for s in range(2):
                            split_w2(HT * c + s, s)
                    act.wait_ge(g_mm, ff + 2)
                    act.wait_ge(hf_done, ff)
                    nc.scalar.activation(sg[:], ps_g[:], ACT.Silu).then_inc(sg_done, 1)
                    act.wait_ge(hf_done, ff + 1)
                    act.wait_ge(y_mm, HT * c + 1)
                    nc.scalar.activation(h_hi[:, f], hf[:], ACT.Copy).then_inc(h_hi_done, 1)
                with act.Fori(0, HT // 2 - 1) as j:
                    for s in range(2):
                        split_w2(HT * c + 2 * j + s + 2, s)
                split_w(CF * c + CF, 0)
            ln.scalar(act)

        @block.vector
        def _(dve):
            def scale_w(f, e):
                for i in range(2):
                    slot = 2 * i + e
                    dve.wait_ge(w_ld[slot], 16 * (f // 2 + 1))
                    sc = scales[i][:, bass.ds((f % FT) * HT, HT)].unsqueeze(2).to_broadcast([P, HT, P])
                    nc.vector.tensor_tensor(w[slot][:], w[slot][:], sc, ALU.mult).then_inc(ws_done, 1)

            def rest_w(f, e):
                for i in range(2):
                    slot = 2 * i + e
                    dve.wait_ge(w_hi_done, 2 * f + i + 1)
                    nc.vector.tensor_tensor(w_lo[slot][:], w[slot][:], f32(w_hi[slot][:]),
                                            ALU.subtract).then_inc(w_lo_done, 1)

            def scale_w2(n, s):
                dve.wait_ge(w2_ld[s], 16 * (n // 2 + 1))
                sc = scales[2][:, bass.ds(n * CF, CF)].unsqueeze(2).to_broadcast([P, CF, P])
                nc.vector.tensor_tensor(w2[s][:], w2[s][:], sc, ALU.mult).then_inc(w2s_done, 1)

            def rest_w2(n, s):
                dve.wait_ge(w2_hi_done, n + 1)
                nc.vector.tensor_tensor(w2_lo[s][:], w2[s][:], f32(w2_hi[s][:]), ALU.subtract).then_inc(w2_lo_done, 1)

            def add_y(c, m, s):
                dve.wait_ge(y_mm, HT * c + m + 2)
                nc.vector.tensor_tensor(ln.tile(m), ln.tile(m), ps_y[s][:], ALU.add).then_inc(y_done, 1)

            ln.setup()
            dve.sem_inc(y_done, 1)
            dve.wait_ge(sc_ld, 48)
            scale_w(0, 0)
            for m in range(HT):
                dve.wait_ge(x_hi_done, m + 1)
                nc.vector.tensor_tensor(x_lo[:, m], y[:, m], f32(x_hi[:, m]), ALU.subtract).then_inc(x_lo_done, 1)
            rest_w(0, 0)
            with dve.Fori(0, FC) as c:
                for f in range(CF):
                    ff = CF * c + f
                    if f < CF - 1:
                        scale_w(ff + 1, 1 - f % 2)
                        rest_w(ff + 1, 1 - f % 2)
                    else:
                        for s in range(2):
                            scale_w2(HT * c + s, s)
                            rest_w2(HT * c + s, s)
                    dve.wait_ge(sg_done, ff + 1)
                    dve.wait_ge(u_mm, ff + 2)
                    dve.wait_ge(h_lo_done, ff)
                    nc.vector.tensor_tensor(hf[:], sg[:], ps_u[:], ALU.mult).then_inc(hf_done, 1)
                    dve.wait_ge(h_hi_done, ff + 1)
                    nc.vector.tensor_tensor(h_lo[:, f], hf[:], f32(h_hi[:, f]), ALU.subtract).then_inc(h_lo_done, 1)
                with dve.Fori(0, HT // 2 - 1) as j:
                    for s in range(2):
                        n = HT * c + 2 * j + s
                        scale_w2(n + 2, s)
                        add_y(c, 2 * j + s, s)
                        rest_w2(n + 2, s)
                scale_w(CF * c + CF, 0)
                rest_w(CF * c + CF, 0)
                for s in range(2):
                    add_y(c, HT - 2 + s, s)
            dve.wait_ge(y_done, FC * HT + 1)
            ln.vector(dve)

        @block.tensor
        def _(pe):
            def product(ps, slot):
                for k in range(HT):
                    pe.wait_ge(x_lo_done, k + 1)
                    for b in range(B):
                        t = slice(b * L, (b + 1) * L)
                        last = three_passes(nc, ps[:, b], w_hi[slot][:, k], w_lo[slot][:, k], x_hi[:, k, t],
                                            x_lo[:, k, t], k == 0, k == HT - 1)
                return last

            def down(c, m, s):
                n = HT * c + m
                pe.wait_ge(w2_lo_done, n + 1)
                pe.wait_ge(y_done, n)
                for k in range(CF):
                    pe.wait_ge(h_lo_done, CF * c + k + 1)
                    for b in range(B):
                        last = three_passes(nc, ps_y[s][:, b], w2_hi[s][:, k], w2_lo[s][:, k], h_hi[:, k, b],
                                            h_lo[:, k, b], k == 0, k == CF - 1)
                last.then_inc(y_mm, 1)

            for free in (g_mm, u_mm, y_mm):
                pe.sem_inc(free, 1)
            with pe.Fori(0, FC) as c:
                for f in range(CF):
                    ff = CF * c + f
                    pe.wait_ge(w_lo_done, 2 * ff + 1)
                    pe.wait_ge(sg_done, ff)
                    product(ps_g, f % 2).then_inc(g_mm, 1)
                    pe.wait_ge(w_lo_done, 2 * ff + 2)
                    pe.wait_ge(hf_done, ff)
                    product(ps_u, 2 + f % 2).then_inc(u_mm, 1)
                with pe.Fori(0, HT // 2) as j:
                    for s in range(2):
                        down(c, 2 * j + s, s)
            pe.wait_ge(ln.set, 2)
            pe.wait_ge(y_done, FC * HT + 1)
            for m in range(HT):
                ln.mean(y, m, m == 0, m == HT - 1)
            ln.tensor(pe)


def decoder_layer(nc, d):
    for name, shape in (("bc", [B, 2 * NS, L]), ("y", [B * IT + 1, P, L]), ("x1", [HT, P, TOK]), ("x2", [HT, P, TOK]),
                        ("k", [B * KV, HD, S]), ("v", [B, KV, P, ST, HD]), ("attn", [B * NH + 1, HD, L])):
        d[name] = nc.dram_tensor(name, shape, F32, kind="Internal").ap()
    xc = nc.alloc_sbuf_tensor_at("xc", [P, B * IT, L], F32, offset=TOP - 4 * B * IT * L)
    ssm_n = nc.alloc_sbuf_tensor_at("ssm_n", [E, TOK], F32, offset=TOP - 4 * B * IT * L - 4 * TOK)
    y = d["y"][1:].rearrange("(b i) p l -> i p b l", b=B)
    attn = d["attn"][1:].rearrange("(b h) e l -> b (h e) l", b=B).rearrange("b (i p) l -> i p b l", p=P)

    def phase(f, *args):
        res = Phase(nc)
        f(nc, res, *args)
        res.release()

    phase(mamba_in, d, xc, ssm_n)
    phase(mamba_scan, d, xc, ssm_n)
    phase(project_add_norm, "mo", IT, lambda i: y[i], d["w_out"], d["x_t"], d["x1"])
    phase(kv_project, d)
    phase(attention, d)
    phase(project_add_norm, "ao", NH * HD // P, lambda i: attn[i], d["w_o"], d["x1"], d["x2"])
    phase(feed_forward, d, d["out"])


def kernel(**inputs):
    import concourse.bacc as bacc
    from concourse.bass_utils import run_bass_kernel_spmd

    a = {n: np.asarray(v) for n, v in inputs.items()}
    m, q, f = "L0_attn_", "L0_xattn_", "L0_ffn_"

    def tiles(w, mt, kt, width=P, split=1):
        w = w.reshape(mt, width, split, kt // split, -1).transpose(0, 2, 4, 3, 1)
        return w.reshape(mt * split, w.shape[2], kt // split, width)

    def cols(v):
        return v.reshape(-1, P).T

    x = a["x"].reshape(TOK, H).T
    w_in = a[m + "in_proj_w"].T
    group = np.repeat([0, 1, 2], [R, NS, NS])
    arrays = {
        "x_t": x.reshape(HT, P, TOK),
        "x_tb": x.reshape(HT, P, B, L).transpose(2, 1, 0, 3),
        "w_x": tiles(w_in[:DIN], IT, HT),
        "w_z": tiles(w_in[DIN:], IT, HT),
        "conv_w": a[m + "conv_w"].reshape(IT, P, KC).transpose(1, 0, 2),
        "conv_b": cols(a[m + "conv_b"]),
        "x_proj": a[m + "x_proj_w"].reshape(E, IT, P).transpose(2, 1, 0),
        "dt_w": a[m + "dt_proj_w"].reshape(IT, P, R).transpose(0, 2, 1),
        "dt_bias": cols(a[m + "dt_bias"]),
        "a_log": a[m + "A_log"].reshape(IT, P, NS).transpose(1, 0, 2),
        "d_param": cols(a[m + "D_param"]),
        "dt_ln": a[m + "dt_ln_w"].reshape(R, 1),
        "b_ln": a[m + "B_ln_w"].reshape(NS, 1),
        "c_ln": a[m + "C_ln_w"].reshape(NS, 1),
        "w_out": tiles(a[m + "out_proj_w"], HT, IT, split=2),
        "ctx": a["ctx_4096"].reshape(B, CTX // L, L, HT, P).transpose(0, 1, 4, 3, 2).reshape(-1, P, HT, L),
        "w_q": tiles(a[q + "Wq"], NH, HT, width=HD),
        "w_k": a[q + "Wk"].reshape(KV * HD, HT, P).transpose(2, 1, 0),
        "w_v": a[q + "Wv"].reshape(KV * HD, HT, P).transpose(2, 1, 0),
        "w_o": tiles(a[q + "Wo"], HT, NH * HD // P, split=2),
        "w_1": tiles(a[f + "w1"], FT, HT),
        "w_3": tiles(a[f + "w3"], FT, HT),
        "w_2": a[f + "w2"].reshape(HT, P, FC, CF, P).transpose(2, 0, 4, 3, 1).reshape(FC * HT, P, CF, P),
        "s_1": a[f + "w1_scale"].reshape(-1),
        "s_3": a[f + "w3_scale"].reshape(-1),
        "s_2": a[f + "w2_scale"].reshape(HT, FC, CF).transpose(1, 0, 2).reshape(-1),
        "ident": np.eye(P, dtype=np.float32),
        "mean_w": ((group[:, None] == group[None, :]) / np.repeat([R, NS, NS], [R, NS, NS])[:, None]).astype(np.float32),
    }
    nc = bacc.Bacc("TRN2", target_bir_lowering=False, num_devices=1)
    arrays = {f"in_{n}": np.ascontiguousarray(v) for n, v in arrays.items()}
    d = {n[3:]: nc.dram_tensor(n, v.shape, F32, kind="ExternalInput").ap() for n, v in arrays.items()}
    d["out"] = nc.dram_tensor("out", (HT, P, TOK), F32, kind="ExternalOutput").ap()
    decoder_layer(nc, d)
    r = run_bass_kernel_spmd(nc, [arrays], core_ids=[0])
    return r.results[0]["out"].reshape(H, TOK).T.reshape(B, L, H)
```

```python
from contextlib import ExitStack

import numpy as np

import concourse.bass as bass
from concourse import mybir

F32 = mybir.dt.float32
F32R = mybir.dt.float32r
ALU = mybir.AluOpType
ACT = mybir.ActivationFunctionType
AX_X = mybir.AxisListType.X

P = 128
B, L, H = 2, 512, 1024
TOK = B * L
HT = H // P
DIN, NS, R, KC = 2048, 16, 64, 4
IT = DIN // P
E = R + 2 * NS
CTX = 1024
NH, KV, HD = 16, 4, 96
G = NH // KV
S = CTX + L
ST = S // P
QT = L // P
FF = 3584
FT = FF // P
CF = 4
FC = FT // CF
RMS_EPS, LN_EPS = 1e-6, 1e-5
BASE = 16640
TOP = 229344


class Phase:

    def __init__(self, nc):
        self.nc, self.banks, self.sems = nc, ExitStack(), []

    def bank(self, name, shape):
        return self.banks.enter_context(self.nc.psum_tensor(name, shape, F32))

    def sem(self, name):
        self.sems.append(self.nc.alloc_semaphore(name))
        return self.sems[-1]

    def release(self):
        for s in self.sems:
            self.nc.sync.sem_clear(s)
            self.nc.release_semaphore(s)
        self.banks.close()


class Arena:

    def __init__(self, nc, phase, at=BASE):
        self.nc, self.phase, self.at = nc, phase, at

    def __call__(self, name, shape, dt=F32):
        size = 4
        for n in shape[1:]:
            size *= n
        size = (size + 31) // 32 * 32
        assert self.at + size <= TOP, (self.phase, name, self.at + size - TOP)
        t = self.nc.alloc_sbuf_tensor_at(f"{self.phase}_{name}", list(shape), dt, offset=self.at)
        self.at += size
        return t


def f32(ap):
    return ap.bitcast(F32)


def three_passes(nc, out, w_hi, w_lo, x_hi, x_lo, start, stop):
    nc.tensor.matmul(out, w_hi, x_hi, start=start, stop=False)
    nc.tensor.matmul(out, w_hi, x_lo, start=False, stop=False)
    return nc.tensor.matmul(out, w_lo, x_hi, start=False, stop=stop)


def mamba_in(nc, res, d, xc, ssm_n):
    sb = Arena(nc, "in")

    def sem(n):
        return res.sem("in_" + n)

    NT = 2 * IT
    x = sb("x", [P, HT, TOK])
    x_hi = sb("x_hi", [P, HT, TOK], F32R)
    x_lo = Arena(nc, "in")("x_lo", [P, HT, TOK], F32R)
    w = [sb(f"w{s}", [P, HT, P]) for s in range(2)]
    w_hi = [sb(f"w_hi{s}", [P, HT, P], F32R) for s in range(2)]
    w_lo = [sb(f"w_lo{s}", [P, HT, P], F32R) for s in range(2)]
    xz = [sb(f"xz{s}", [P, B, L + KC - 1]) for s in range(2)]
    acc = [sb(f"acc{s}", [P, B, L]) for s in range(2)]
    pre = [sb(f"pre{s}", [P, B, L]) for s in range(2)]
    xpw = sb("xpw", [P, IT, E])
    xpw_hi = [sb(f"xpw_hi{s}", [P, E], F32R) for s in range(2)]
    xpw_lo = [sb(f"xpw_lo{s}", [P, E], F32R) for s in range(2)]
    cw = sb("cw", [P, IT, KC])
    cb = sb("cb", [P, IT])
    lnw = sb("lnw", [E, 1])
    eps = sb("eps", [E, 1])
    meanw = sb("meanw", [E, E])
    zero = sb("zero", [P, P], F32R)
    xc_hi = [sb(f"xc_hi{s}", [P, B, L], F32R) for s in range(2)]
    xc_lo = [sb(f"xc_lo{s}", [P, B, L], F32R) for s in range(2)]
    ssm, sq, rms = acc[0][0:E], acc[1][0:E], pre[0][0:E]
    assert sb.at <= TOP - 4 * B * IT * L - 4 * TOK

    ps = [res.bank(f"in_ps{s}", [P, B, L]) for s in range(2)]
    ps_xp = res.bank("in_ps_xp", [E, B, L])
    ps_ms = res.bank("in_ps_ms", [E, B, L])

    x_ld = [sem(f"x_ld{k}") for k in range(HT)]
    w_ld = [sem(f"w_ld{s}") for s in range(2)]
    sz_st = [sem(f"sz_st{s}") for s in range(2)]
    par_ld, bc_st = sem("par_ld"), sem("bc_st")
    x_hi_done, x_lo_done = sem("x_hi_done"), sem("x_lo_done")
    w_hi_done, w_lo_done = sem("w_hi_done"), sem("w_lo_done")
    init_done, zeroed = sem("init_done"), sem("zeroed")
    main_done, conv_step = sem("main_done"), sem("conv_step")
    left = sem("left")
    xc_done, xc_hi_done, xc_lo_done = sem("xc_done"), sem("xc_hi_done"), sem("xc_lo_done")
    xpw_hi_done, xpw_done, xproj_done = sem("xpw_hi_done"), sem("xpw_done"), sem("xproj_done")
    ssm_done, sq_done, ms_done = sem("ssm_done"), sem("sq_done"), sem("ms_done")
    rms_done, rr_done, n_done = sem("rms_done"), sem("rr_done"), sem("n_done")
    XP_LAST = IT + 1

    xc4 = xc[:].rearrange("p (b i) l -> p b i l", b=B)
    sz = d["sz"].rearrange("(b i) p l -> i p b l", b=B)

    with nc.Block() as block:
        @block.sync
        def _(sp):
            def next_w(m, s):
                sp.wait_ge(w_lo_done, m + 1)
                sp.dma_start(w[s][:], d["w_in"][m + 2]).then_inc(w_ld[s], 16)

            def store_gate(m, s):
                sp.wait_ge(left, m + 2)
                sp.dma_start(sz[m - IT], xz[s][:, :, KC - 1:]).then_inc(sz_st[s], 16)

            for s in range(2):
                sp.dma_start(w[s][:], d["w_in"][s]).then_inc(w_ld[s], 16)
                for k in range(4 * s, 4 * s + 4):
                    sp.dma_start(x[:, k], d["x_t"][k]).then_inc(x_ld[k], 16)
            sp.dma_start(cw[:], d["conv_w"]).then_inc(par_ld, 16)
            sp.dma_start(cb[:], d["conv_b"]).then_inc(par_ld, 16)
            sp.dma_start(xpw[:], d["x_proj"]).then_inc(par_ld, 16)
            sp.dma_start(meanw[:], d["mean_w"]).then_inc(par_ld, 16)
            sp.dma_start(lnw[0:R], d["dt_ln"]).then_inc(par_ld, 16)
            sp.dma_start(lnw[R:R + NS], d["b_ln"]).then_inc(par_ld, 16)
            sp.dma_start(lnw[R + NS:E], d["c_ln"]).then_inc(par_ld, 16)
            with sp.Fori(0, IT // 2) as j:
                for s in range(2):
                    next_w(2 * j + s, s)
            with sp.Fori(IT // 2, IT - 1) as j:
                for s in range(2):
                    next_w(2 * j + s, s)
                    store_gate(2 * j + s, s)
            for s in range(2):
                store_gate(NT - 2 + s, s)
            sp.wait_ge(n_done, 1)
            sp.dma_start(d["bc"].rearrange("b r l -> r b l"),
                         ssm_n[R:E].rearrange("r (b l) -> r b l", b=B)).then_inc(bc_st, 16)
            sp.wait_ge(bc_st, 16)
            for s in range(2):
                sp.wait_ge(sz_st[s], 16 * IT // 2)

        @block.scalar
        def _(act):
            def split_w(s, load):
                act.wait_ge(w_ld[s], load)
                nc.scalar.activation(w_hi[s][:], w[s][:], ACT.Copy).then_inc(w_hi_done, 1)

            def next_w(m, s):
                act.wait_ge(main_done, m)
                split_w(1 - s, 16 * (m // 2 + 1 + s))

            def gate(m, s):
                act.wait_ge(main_done, m + 1)
                act.wait_ge(sz_st[s], 16 * ((m - IT) // 2))
                nc.scalar.activation(xz[s][:, :, KC - 1:], ps[s][:], ACT.Silu).then_inc(left, 1)

            act.sem_inc(left, 1)
            split_w(0, 16)
            for k in range(HT):
                act.wait_ge(x_ld[k], 16)
                nc.scalar.activation(x_hi[:, k], x[:, k], ACT.Copy).then_inc(x_hi_done, 1)
            act.wait_ge(init_done, 3)
            with act.Fori(0, IT // 2) as j:
                for s in range(2):
                    m = 2 * j + s
                    next_w(m, s)
                    act.wait_ge(main_done, m + 1)
                    act.wait_ge(conv_step, 8 * j)
                    nc.scalar.activation(xz[s][:, :, KC - 1:], ps[s][:], ACT.Copy).then_inc(left, 1)
                    act.wait_ge(conv_step, 4 * m + 4)
                    nc.scalar.activation(xc4[:, :, m, :], pre[s][:], ACT.Silu).then_inc(xc_done, 1)
                    act.wait_ge(zeroed, 5)
                    act.wait_ge(xproj_done, m)
                    act.wait_ge(xc_done, m + 1)
                    nc.scalar.activation(xc_hi[s][:], xc4[:, :, m, :], ACT.Copy).then_inc(xc_hi_done, 1)
            next_w(IT, 0)
            gate(IT, 0)
            act.wait_ge(xproj_done, XP_LAST)
            nc.scalar.activation(ssm, ps_xp[:], ACT.Copy).then_inc(ssm_done, 1)
            nc.scalar.activation(sq, ps_xp[:], ACT.Square).then_inc(sq_done, 1)
            next_w(IT + 1, 1)
            gate(IT + 1, 1)
            act.wait_ge(ms_done, 1)
            nc.scalar.activation(rms, ps_ms[:], ACT.Sqrt, bias=eps[:, 0:1]).then_inc(rms_done, 1)
            with act.Fori(IT // 2 + 1, IT - 1) as j:
                for s in range(2):
                    next_w(2 * j + s, s)
                    gate(2 * j + s, s)
            next_w(NT - 2, 0)
            gate(NT - 2, 0)
            gate(NT - 1, 1)

        @block.vector
        def _(dve):
            def split_w(s, n):
                dve.wait_ge(w_hi_done, n)
                nc.vector.tensor_tensor(w_lo[s][:], w[s][:], f32(w_hi[s][:]), ALU.subtract).then_inc(w_lo_done, 1)

            for s in range(2):
                nc.vector.memset(xz[s][:, :, 0:KC - 1], 0.0).then_inc(init_done, 1)
            nc.vector.memset(eps[:], RMS_EPS).then_inc(init_done, 1)
            nc.vector.memset(zero[:].bitcast(F32), 0.0).then_inc(zeroed, 1)
            nc.vector.memset(xpw_hi[1][:].bitcast(F32), 0.0).then_inc(zeroed, 1)
            nc.vector.memset(xpw_lo[1][:].bitcast(F32), 0.0).then_inc(zeroed, 1)
            nc.vector.memset(xc_hi[1][:].bitcast(F32), 0.0).then_inc(zeroed, 1)
            nc.vector.memset(xc_lo[1][:].bitcast(F32), 0.0).then_inc(zeroed, 1)
            split_w(0, 1)
            for k in range(HT):
                dve.wait_ge(x_hi_done, k + 1)
                nc.vector.tensor_tensor(x_lo[:, k], x[:, k], f32(x_hi[:, k]), ALU.subtract).then_inc(x_lo_done, 1)
            dve.wait_ge(par_ld, 16 * 7)
            with dve.Fori(0, IT // 2) as j:
                for s in range(2):
                    m = 2 * j + s
                    dve.wait_ge(main_done, m)
                    split_w(1 - s, m + 2)
                    dve.wait_ge(xpw_hi_done, m + 1)
                    nc.vector.tensor_tensor(xpw_lo[s][:], xpw[:, m, :], f32(xpw_hi[s][:]),
                                            ALU.subtract).then_inc(xpw_done, 1)
                    dve.wait_ge(left, m + 2)
                    dve.wait_ge(xc_done, 2 * j)
                    nc.vector.tensor_scalar(acc[s][:], xz[s][:, :, 0:L], cw[:, m, 0:1], cb[:, bass.ds(m, 1)],
                                            ALU.mult, ALU.add).then_inc(conv_step, 1)
                    for t in range(1, KC):
                        a, o = (acc, pre) if t % 2 else (pre, acc)
                        dve.wait_ge(conv_step, 4 * m + t)
                        nc.vector.scalar_tensor_tensor(o[s][:], xz[s][:, :, t:t + L], cw[:, m, t:t + 1], a[s][:],
                                                       ALU.mult, ALU.add).then_inc(conv_step, 1)
                    dve.wait_ge(xc_hi_done, m + 1)
                    nc.vector.tensor_tensor(xc_lo[s][:], xc4[:, :, m, :], f32(xc_hi[s][:]),
                                            ALU.subtract).then_inc(xc_lo_done, 1)
            for s in range(2):
                dve.wait_ge(main_done, IT + s)
                split_w(1 - s, IT + s + 2)
            dve.wait_ge(rms_done, 1)
            nc.vector.reciprocal(sq, rms).then_inc(rr_done, 1)
            dve.wait_ge(rr_done, 1)
            nc.vector.scalar_tensor_tensor(ssm_n[:].rearrange("e (b l) -> e b l", b=B), ssm, lnw[:, 0:1], sq,
                                           ALU.mult, ALU.mult).then_inc(n_done, 1)
            with dve.Fori(IT // 2 + 1, IT - 1) as j:
                for s in range(2):
                    dve.wait_ge(main_done, 2 * j + s)
                    split_w(1 - s, 2 * j + s + 2)
            dve.wait_ge(main_done, NT - 2)
            split_w(1, NT)

        @block.gpsimd
        def _(pool):
            pool.wait_ge(par_ld, 16 * 7)
            pool.wait_ge(zeroed, 5)
            with pool.Fori(0, IT // 2) as j:
                for s in range(2):
                    m = 2 * j + s
                    pool.wait_ge(xproj_done, m)
                    nc.gpsimd.tensor_copy(xpw_hi[s][:], xpw[:, m, :]).then_inc(xpw_hi_done, 1)

        @block.tensor
        def _(pe):
            def main(m, s):
                pe.wait_ge(w_lo_done, m + 1)
                pe.wait_ge(left, m)
                for k in range(HT):
                    pe.wait_ge(x_lo_done, k + 1)
                    for b in range(B):
                        c = slice(b * L, (b + 1) * L)
                        last = three_passes(nc, ps[s][:, b], w_hi[s][:, k], w_lo[s][:, k], x_hi[:, k, c], x_lo[:, k, c],
                                            k == 0, k == HT - 1)
                last.then_inc(main_done, 1)

            def xproj(s, ready, stop=False):
                pe.wait_ge(xc_lo_done, ready)
                pe.wait_ge(xpw_done, ready)
                for b in range(B):
                    last = three_passes(nc, ps_xp[:, b], xpw_hi[s][:], xpw_lo[s][:], xc_hi[s][:, b], xc_lo[s][:, b],
                                        False, stop)
                last.then_inc(xproj_done, 1)

            pe.wait_ge(zeroed, 5)
            pe.wait_ge(x_lo_done, 1)
            for b in range(B):
                nc.tensor.matmul(ps_xp[:, b], zero[:, 0:E], x_hi[:, 0, 0:L], start=True, stop=False)
            with pe.Fori(0, IT // 2) as j:
                for s in range(2):
                    main(2 * j + s, s)
                    xproj(1 - s, 2 * j + s)
            main(IT, 0)
            xproj(1, IT, stop=True)
            main(IT + 1, 1)
            pe.wait_ge(sq_done, 1)
            pe.wait_ge(par_ld, 16 * 7)
            for b in range(B):
                last = nc.tensor.matmul(ps_ms[:, b], meanw[:], sq[:, b], start=True, stop=True)
            last.then_inc(ms_done, 1)
            with pe.Fori(IT // 2 + 1, IT) as j:
                for s in range(2):
                    main(2 * j + s, s)


def mamba_scan(nc, res, d, xc, ssm_n):
    sb = Arena(nc, "scan")

    def sem(n):
        return res.sem("scan_" + n)

    NIT = B * IT
    NK = NS // 2
    CH = 4
    SL = 4
    b_bc = sb("b_bc", [P, NS, L])
    c_bc = sb("c_bc", [P, NS, L])
    dtw = [sb(f"dtw{s}", [R, P]) for s in range(2)]
    dbx = [sb(f"dbx{s}", [P, 2, L]) for s in range(SL)]
    g = [sb(f"g{s}", [P, 2, L]) for s in range(SL)]
    dt = [sb(f"dt{s}", [P, L]) for s in range(2)]
    u = [sb(f"u{s}", [P, L]) for s in range(2)]
    sz = [sb(f"sz{s}", [P, L]) for s in range(2)]
    yb = [sb(f"yb{s}", [P, L]) for s in range(2)]
    mag, rl, ee, one_e, back_e, ll, cc = (sb(n, [P, L]) for n in ("mag", "rl", "ee", "one_e", "back_e", "ll", "cc"))
    a_neg = sb("a_neg", [P, NIT, NS])
    a_exp = mag[:].rearrange("p (i n) -> p i n", n=NS)
    dt_b = sb("dt_b", [P, NIT])
    d_p = sb("d_p", [P, NIT])
    ident = sb("ident", [P, P])
    d_diag = [sb(f"d_diag{s}", [P, P]) for s in range(2)]
    assert sb.at <= TOP - 4 * NIT * L - 4 * TOK

    ps_a = [res.bank(f"scan_ps_a{s}", [P, 2, L]) for s in range(2)]
    ps_h = res.bank("scan_ps_h", [P, 2 * L])
    ps_y = res.bank("scan_ps_y", [P, L])
    ps_m = res.bank("scan_ps_m", [P, L])

    par_ld = sem("par_ld")
    bc_ld = [sem(f"bc_ld{c}") for c in range(NS // CH)]
    dtw_ld = [sem(f"dtw_ld{s}") for s in range(2)]
    sz_ld = [sem(f"sz_ld{s}") for s in range(2)]
    y_st = [sem(f"y_st{s}") for s in range(2)]
    a_exp_done, a_done, init_done = sem("a_exp_done"), sem("a_done"), sem("init_done")
    dt_mm, mag_done, rl_done, e_done = sem("dt_mm"), sem("mag_done"), sem("rl_done"), sem("e_done")
    one_done, back_done, l_done, cc_done = sem("one_done"), sem("back_done"), sem("l_done"), sem("cc_done")
    dt_sum, dt_done, u_done, diag_done = sem("dt_sum"), sem("dt_done"), sem("u_done"), sem("diag_done")
    scanned = sem("scanned")
    summed = sem("summed")
    a_ready, dbx_ready, g_ready, epi_done = sem("a_ready"), sem("dbx_ready"), sem("g_ready"), sem("epi_done")

    with nc.Block() as block:
        @block.sync
        def _(sp):
            sp.dma_start(a_exp[:, 0:IT, :], d["a_log"]).then_inc(par_ld, 16)
            sp.dma_start(a_exp[:, IT:NIT, :], d["a_log"]).then_inc(par_ld, 16)
            for b in range(B):
                sp.dma_start(dt_b[:, b * IT:(b + 1) * IT], d["dt_bias"]).then_inc(par_ld, 16)
                sp.dma_start(d_p[:, b * IT:(b + 1) * IT], d["d_param"]).then_inc(par_ld, 16)
            sp.dma_start(ident[:], d["ident"]).then_inc(par_ld, 16)
            for s in range(2):
                sp.dma_start(dtw[s][:], d["dt_w"][s]).then_inc(dtw_ld[s], 16)

            def block_loads(it, s):
                sp.wait_ge(epi_done, it)
                sp.dma_start(sz[s][:], d["sz"][it]).then_inc(sz_ld[s], 16)
                sp.wait_ge(dt_mm, it + 1)
                sp.dma_start(dtw[s][:], d["dt_w"][(it + 2) % IT]).then_inc(dtw_ld[s], 16)

            def store(it, s):
                sp.wait_ge(epi_done, it + 1)
                sp.dma_start(d["y"][it], yb[1 - s][:]).then_inc(y_st[1 - s], 16)

            sp.wait_ge(init_done, 3)
            with sp.Fori(0, B) as b:
                for c in range(NS // CH):
                    sp.wait_ge(dbx_ready, b * (NK * (IT - 1) + (c + 1) * CH // 2))
                    sp.wait_ge(g_ready, b * (NK * (IT - 1) + (c + 1) * CH // 2))
                    n = c * CH
                    sp.dma_start(b_bc[:, n:n + CH], d["bc"][b, n:n + CH].partition_broadcast(P)).then_inc(bc_ld[c], 16)
                    sp.dma_start(c_bc[:, n:n + CH],
                                 d["bc"][b, NS + n:NS + n + CH].partition_broadcast(P)).then_inc(bc_ld[c], 16)
                with sp.Fori(0, IT // 2) as j:
                    for s in range(2):
                        store(IT * b + 2 * j + s, s)
                        block_loads(IT * b + 2 * j + s, s)
            store(NIT, 0)
            sp.wait_ge(dtw_ld[0], 16 * (NIT // 2 + 1))
            sp.wait_ge(dtw_ld[1], 16 * (NIT // 2 + 1))
            sp.wait_ge(y_st[1], 16 * (NIT // 2 + 1))
            sp.wait_ge(y_st[0], 16 * (NIT // 2))

        @block.scalar
        def _(act):
            def before1(it):
                i = it % NIT
                act.wait_ge(dt_mm, it + 1)
                act.wait_ge(dt_sum, it)
                nc.scalar.activation(mag[:], ps_m[:], ACT.Abs, bias=dt_b[:, bass.ds(i, 1)]).then_inc(mag_done, 1)
                nc.scalar.activation(rl[:], ps_m[:], ACT.Relu, bias=dt_b[:, bass.ds(i, 1)]).then_inc(rl_done, 1)
                act.wait_ge(mag_done, it + 1)
                nc.scalar.activation(ee[:], mag[:], ACT.Exp, scale=-1.0).then_inc(e_done, 1)

            def before2(it):
                act.wait_ge(e_done, it + 1)
                nc.scalar.activation(one_e[:], ee[:], ACT.Copy, bias=1.0).then_inc(one_done, 1)
                act.wait_ge(one_done, it + 1)
                nc.scalar.activation(back_e[:], one_e[:], ACT.Copy, bias=-1.0).then_inc(back_done, 1)

            def logarithm(it):
                act.wait_ge(one_done, it + 1)
                nc.scalar.activation(ll[:], one_e[:], ACT.Ln).then_inc(l_done, 1)

            def before3(it, s):
                act.wait_ge(dt_sum, it + 1)
                act.wait_ge(u_done, it)
                nc.scalar.activation(dt[s][:], ps_m[:], ACT.Copy).then_inc(dt_done, 1)

            def diagonal(it, s):
                i = it % NIT
                nc.scalar.activation(d_diag[s][:], ident[:], ACT.Copy, scale=d_p[:, bass.ds(i, 1)]).then_inc(diag_done, 1)

            act.wait_ge(par_ld, 16 * 7)
            nc.scalar.activation(a_exp, a_exp, ACT.Exp).then_inc(a_exp_done, 1)
            act.wait_ge(a_exp_done, 1)
            nc.scalar.activation(a_neg[:], a_exp, ACT.Copy, scale=-1.0).then_inc(a_done, 1)
            act.wait_ge(a_done, 1)
            before1(0)
            before2(0)
            logarithm(0)
            before3(0, 0)
            diagonal(0, 0)
            before1(1)
            before2(1)
            act.wait_ge(init_done, 3)
            with act.Fori(0, NIT // 2) as j:
                for s in range(2):
                    it = 2 * j + s
                    act.wait_ge(dt_done, it + 1)
                    for k in range(NK):
                        n = NK * it + k
                        act.wait_ge(scanned, n + SL - 1)
                        for h in range(2):
                            nc.scalar.activation(ps_a[k % 2][:, h, 1:], dt[s][:, 1:], ACT.Exp,
                                                 scale=a_neg[:, it, 2 * k + h:2 * k + h + 1]).then_inc(a_ready, 1)
                        if k == 0:
                            logarithm(it + 1)
                        if k == 3:
                            before3(it + 1, 1 - s)
                        if k == 4:
                            act.wait_ge(summed, NK * it + 1)
                            diagonal(it + 1, 1 - s)
                        if k == 6:
                            before1(it + 2)
                        if k == 7:
                            before2(it + 2)

        @block.vector
        def _(dve):
            def after(it, s):
                dve.wait_ge(summed, NK * it + SL)
                if s == 0:
                    dve.wait_ge(sz_ld[1], 16 * (it // 2))
                else:
                    dve.wait_ge(sz_ld[0], 16 * (it // 2 + 1))
                dve.wait_ge(y_st[1 - s], 16 * (it // 2))
                nc.vector.tensor_tensor(yb[1 - s][:], ps_y[:], sz[1 - s][:], ALU.mult).then_inc(epi_done, 1)

            def before(it, s):
                i = it % NIT
                dve.wait_ge(dt_done, it + 1)
                nc.vector.tensor_tensor(u[s][:], dt[s][:], xc[:, i, :], ALU.mult).then_inc(u_done, 1)

            dve.sem_inc(scanned, SL)
            for s in range(2):
                nc.vector.memset(ps_a[s][:, :, 0:1], 0.0).then_inc(init_done, 1)
            nc.vector.memset(sz[1][:], 0.0).then_inc(init_done, 1)
            dve.wait_ge(init_done, 3)
            before(0, 0)
            with dve.Fori(0, NIT // 2) as j:
                for s in range(2):
                    it = 2 * j + s
                    for k in range(NK):
                        n = NK * it + k
                        dve.wait_ge(a_ready, 2 * n + 2)
                        dve.wait_ge(dbx_ready, n + 1)
                        dve.wait_ge(g_ready, n)
                        nc.vector.tensor_tensor_scan(ps_h[:], ps_a[k % 2][:].rearrange("p n l -> p (n l)"),
                                                     dbx[k % SL][:].rearrange("p n l -> p (n l)"), 0.0,
                                                     ALU.mult, ALU.add).then_inc(scanned, 1)
                        if k == 1:
                            after(it, s)
                        if k % 2 == 0:
                            dve.wait_ge(bc_ld[k // 2], 32 * (it // IT + 1))
                        dve.wait_ge(scanned, n + 1 + SL)
                        dve.wait_ge(summed, n + 1)
                        nc.vector.tensor_tensor(g[k % SL][:], ps_h[:].rearrange("p (n l) -> p n l", n=2),
                                                c_bc[:, 2 * k:2 * k + 2], ALU.mult).then_inc(g_ready, 1)
                        if k == 2:
                            dve.wait_ge(dbx_ready, NK * it)
                            before(it + 1, 1 - s)
            after(NIT, 0)

        @block.gpsimd
        def _(pool):
            def rest(it):
                pool.wait_ge(e_done, it + 1)
                pool.wait_ge(back_done, it + 1)
                nc.gpsimd.tensor_tensor(cc[:], ee[:], back_e[:], ALU.subtract).then_inc(cc_done, 1)

            rest(0)
            with pool.Fori(0, NIT // 2) as j:
                for s in range(2):
                    it = 2 * j + s
                    pool.wait_ge(u_done, it + 1)
                    for k in range(NK):
                        if k % 2 == 0:
                            pool.wait_ge(bc_ld[k // 2], 32 * (it // IT + 1))
                        pool.wait_ge(scanned, NK * it + k + 1)
                        nc.gpsimd.tensor_tensor(dbx[k % SL][:], u[s][:].unsqueeze(1).to_broadcast([P, 2, L]),
                                                b_bc[:, 2 * k:2 * k + 2], ALU.mult).then_inc(dbx_ready, 1)
                        if k == 1:
                            rest(it + 1)

        @block.tensor
        def _(pe):
            def dt_product(it, s):
                b = (it // IT) % B
                pe.wait_ge(dtw_ld[s], 16 * (it // 2 + 1))
                pe.wait_ge(dt_done, it)
                nc.tensor.matmul(ps_m[:], dtw[s][:], ssm_n[0:R, bass.ds(b * L, L)],
                                 start=True, stop=True).then_inc(dt_mm, 1)

            def dt_total(it):
                for n, (part, ready) in enumerate(((rl, rl_done), (ll, l_done), (cc, cc_done))):
                    pe.wait_ge(ready, it + 1)
                    last = nc.tensor.matmul(ps_m[:], ident[:], part[:], start=n == 0, stop=n == 2)
                last.then_inc(dt_sum, 1)

            pe.sem_inc(summed, SL)
            pe.wait_ge(par_ld, 16 * 7)
            nc.tensor.matmul(ps_y[:], ident[:], xc[:, 0], start=True, stop=True)
            dt_product(0, 0)
            dt_total(0)
            dt_product(1, 1)
            with pe.Fori(0, NIT // 2) as j:
                for s in range(2):
                    it = 2 * j + s
                    for k in range(NK):
                        if k == 0:
                            dt_total(it + 1)
                            pe.wait_ge(epi_done, it + 1)
                            pe.wait_ge(diag_done, it + 1)
                            nc.tensor.matmul(ps_y[:], d_diag[s][:], xc[:, it], start=True, stop=False)
                        pe.wait_ge(g_ready, NK * it + k + 1)
                        for h in range(2):
                            last = nc.tensor.matmul(ps_y[:], ident[:], g[k % SL][:, h], start=False,
                                                    stop=k == NK - 1 and h == 1)
                        last.then_inc(summed, 1)
                        if k == 2:
                            dt_product(it + 2, s)


class Norm:

    def __init__(self, nc, res, sb, phase, sq):
        def sem(n):
            return res.sem(f"{phase}_ln_{n}")

        self.nc = nc
        self.mean_w = sb("mean_w", [P, P])
        self.eps = sb("ln_eps", [P, 1])
        self.sq = sq
        self.std = sb("std", [P, B, L])
        self.rstd = sb("rstd", [P, B, L])
        self.ps_mean = res.bank(f"{phase}_ps_mean", [P, B, L])
        self.ps_var = res.bank(f"{phase}_ps_var", [P, B, L])
        self.set, self.mean_done, self.c_done, self.sq_done = sem("set"), sem("mean_done"), sem("c_done"), sem("sq_done")
        self.var_mm, self.std_done, self.rstd_done = sem("var_mm"), sem("std_done"), sem("rstd_done")
        self.out_done, self.stored = sem("out_done"), sem("stored")

    def setup(self):
        self.nc.vector.memset(self.mean_w[:], 1.0 / H).then_inc(self.set, 1)
        self.nc.vector.memset(self.eps[:], LN_EPS).then_inc(self.set, 1)

    def mean(self, v, m, start, stop):
        for b in range(B):
            last = self.nc.tensor.matmul(self.ps_mean[:, b], self.mean_w[:], v[:, m, bass.ds(b * L, L)],
                                         start=start, stop=stop)
        if stop:
            last.then_inc(self.mean_done, 1)

    def tensor(self, pe):
        for m in range(HT):
            pe.wait_ge(self.sq_done, m + 1)
            for b in range(B):
                last = self.nc.tensor.matmul(self.ps_var[:, b], self.mean_w[:], self.sq[m % 2][:, b],
                                             start=m == 0, stop=m == HT - 1)
            last.then_inc(self.var_mm, 1)

    def scalar(self, act):
        for m in range(HT):
            act.wait_ge(self.c_done, m + 1)
            if m >= 2:
                act.wait_ge(self.var_mm, m - 1)
            self.nc.scalar.activation(self.sq[m % 2][:], self.tile(m), ACT.Square).then_inc(self.sq_done, 1)
        act.wait_ge(self.var_mm, HT)
        act.wait_ge(self.set, 2)
        self.nc.scalar.activation(self.std[:], self.ps_var[:], ACT.Sqrt, bias=self.eps[:, 0:1]).then_inc(self.std_done, 1)

    def vector(self, dve):
        dve.wait_ge(self.mean_done, 1)
        for m in range(HT):
            self.nc.vector.tensor_tensor(self.tile(m), self.tile(m), self.ps_mean[:], ALU.subtract).then_inc(self.c_done, 1)
        dve.wait_ge(self.std_done, 1)
        self.nc.vector.reciprocal(self.rstd[:], self.std[:]).then_inc(self.rstd_done, 1)
        dve.wait_ge(self.rstd_done, 1)
        dve.wait_ge(self.sq_done, HT)
        dve.wait_ge(self.c_done, HT)
        for m in range(HT):
            self.nc.vector.tensor_tensor(self.tile(m), self.tile(m), self.rstd[:], ALU.mult).then_inc(self.out_done, 1)

    def sync(self, sp, v, out):
        for m in range(HT):
            sp.wait_ge(self.out_done, m + 1)
            sp.dma_start(out[m], v[:, m]).then_inc(self.stored, 16)
        sp.wait_ge(self.stored, 16 * HT)

    def over(self, v):
        self.v = v

    def tile(self, m):
        return self.v[:, m].rearrange("p (b l) -> p b l", b=B)


def project_add_norm(nc, res, phase, kt, act_src, w_dram, resid, out):
    sb = Arena(nc, phase)

    def sem(n):
        return res.sem(f"{phase}_{n}")

    KH = kt // 2
    NT = 2 * HT
    a = [sb(f"a{s}", [P, B, L]) for s in range(2)]
    a_hi = sb("a_hi", [P, kt, TOK], F32R)
    a_lo = sb("a_lo", [P, kt, TOK], F32R)
    w = [sb(f"w{s}", [P, KH, P]) for s in range(2)]
    w_hi = [sb(f"w_hi{s}", [P, KH, P], F32R) for s in range(2)]
    w_lo = [sb(f"w_lo{s}", [P, KH, P], F32R) for s in range(2)]
    v = sb("v", [P, HT, TOK])
    ln = Norm(nc, res, sb, phase, sq=a)
    ln.over(v)
    ps = res.bank(f"{phase}_ps", [P, 2, B, L])

    a_ld = [sem(f"a_ld{s}") for s in range(2)]
    w_ld = [sem(f"w_ld{s}") for s in range(2)]
    v_ld = sem("v_ld")
    a_hi_done, a_lo_done = sem("a_hi_done"), sem("a_lo_done")
    w_hi_done, w_lo_done, w_used = sem("w_hi_done"), sem("w_lo_done"), sem("w_used")
    v_done = sem("v_done")

    with nc.Block() as block:
        @block.sync
        def _(sp):
            for s in range(2):
                sp.dma_start(w[s][:], w_dram[s]).then_inc(w_ld[s], 16)
            with sp.Fori(0, kt // 2) as j:
                for s in range(2):
                    sp.wait_ge(a_lo_done, 2 * j)
                    sp.dma_start(a[s][:], act_src(2 * j + s)).then_inc(a_ld[s], 16)
            for m in range(HT):
                sp.dma_start(v[:, m], resid[m]).then_inc(v_ld, 16)
            with sp.Fori(0, HT - 1) as m:
                for s in range(2):
                    sp.wait_ge(w_lo_done, 2 * m + s + 1)
                    sp.dma_start(w[s][:], w_dram[2 * m + s + 2]).then_inc(w_ld[s], 16)
            ln.sync(sp, v, out)

        @block.scalar
        def _(act):
            def split_w(s, load):
                act.wait_ge(w_ld[s], load)
                nc.scalar.activation(w_hi[s][:], w[s][:], ACT.Copy).then_inc(w_hi_done, 1)

            split_w(0, 16)
            split_w(1, 16)
            with act.Fori(0, kt // 2) as j:
                for s in range(2):
                    act.wait_ge(a_ld[s], 16 * j + 16)
                    nc.scalar.activation(a_hi[:, 2 * j + s].rearrange("p (b l) -> p b l", b=B), a[s][:],
                                         ACT.Copy).then_inc(a_hi_done, 1)
            with act.Fori(0, HT - 1) as m:
                for s in range(2):
                    act.wait_ge(w_used, 2 * m + s + 1)
                    split_w(s, 16 * m + 32)
            ln.scalar(act)

        @block.vector
        def _(dve):
            def split_w(s, n):
                dve.wait_ge(w_hi_done, n)
                nc.vector.tensor_tensor(w_lo[s][:], w[s][:], f32(w_hi[s][:]), ALU.subtract).then_inc(w_lo_done, 1)

            def add(m):
                dve.wait_ge(w_used, 2 * m + 2)
                nc.vector.tensor_tensor(ln.tile(m), ln.tile(m), ps[:, m % 2], ALU.add).then_inc(v_done, 1)

            ln.setup()
            split_w(0, 1)
            split_w(1, 2)
            with dve.Fori(0, kt // 2) as j:
                for s in range(2):
                    dve.wait_ge(a_hi_done, 2 * j + s + 1)
                    nc.vector.tensor_tensor(a_lo[:, 2 * j + s].rearrange("p (b l) -> p b l", b=B), a[s][:],
                                            f32(a_hi[:, 2 * j + s]).rearrange("p (b l) -> p b l", b=B),
                                            ALU.subtract).then_inc(a_lo_done, 1)
            dve.wait_ge(v_ld, 16 * HT)
            with dve.Fori(0, HT - 1) as m:
                for s in range(2):
                    dve.wait_ge(w_used, 2 * m + s + 1)
                    split_w(s, 2 * m + s + 3)
                add(m)
            add(HT - 1)
            dve.wait_ge(v_done, HT)
            ln.vector(dve)

        @block.tensor
        def _(pe):
            def main(m, bank):
                for s in range(2):
                    pe.wait_ge(w_lo_done, 2 * m + s + 1)
                    for k in range(KH):
                        kk = s * KH + k
                        pe.wait_ge(a_lo_done, kk + 1)
                        for b in range(B):
                            c = slice(b * L, (b + 1) * L)
                            last = three_passes(nc, ps[:, bank, b], w_hi[s][:, k], w_lo[s][:, k],
                                                a_hi[:, kk, c], a_lo[:, kk, c], kk == 0, kk == kt - 1)
                    last.then_inc(w_used, 1)

            def mean(m, start=False, stop=False):
                pe.wait_ge(v_done, m + 1)
                ln.mean(v, m, start, stop)

            pe.wait_ge(ln.set, 2)
            main(0, 0)
            main(1, 1)
            mean(0, start=True)
            with pe.Fori(0, HT // 2 - 1) as j:
                for s in range(2):
                    main(2 * j + s + 2, s)
                    mean(2 * j + s + 1)
            mean(HT - 1, stop=True)
            ln.tensor(pe)


def qkv_project(nc, res, d):
    sb = Arena(nc, "kv")

    def sem(n):
        return res.sem("kv_" + n)

    KW = KV * HD
    KT = KW // P
    QF = NH * HD // P
    NCH = B * S // L
    CC = CTX // L
    VT = L // P
    wk_hi, wk_lo, wv_hi, wv_lo = (sb(n, [P, HT, KW], F32R) for n in ("wk_hi", "wk_lo", "wv_hi", "wv_lo"))
    h = [sb(f"h{s}", [P, HT, L]) for s in range(2)]
    h_hi = [sb(f"h_hi{s}", [P, HT, L], F32R) for s in range(2)]
    h_lo = [sb(f"h_lo{s}", [P, HT, L], F32R) for s in range(2)]
    kb = [sb(f"kb{s}", [P, L]) for s in range(2)]
    vb = [sb(f"vb{s}", [P, KW]) for s in range(2)]
    over = Arena(nc, "kv_over", sb.at)
    qb = [sb(f"qb{s}", [P, B, L]) for s in range(2)]
    wq = [sb(f"wq{s}", [P, HT, P]) for s in range(2)]
    wq_hi = [sb(f"wq_hi{s}", [P, HT, P], F32R) for s in range(2)]
    wq_lo = [sb(f"wq_lo{s}", [P, HT, P], F32R) for s in range(2)]
    wraw = [over(f"wraw{s}", [P, HT, KW]) for s in range(2)]
    ps_k = res.bank("kv_ps_k", [P, 2, L])
    ps_v = res.bank("kv_ps_v", [P, 2, L])
    ps_q = res.bank("kv_ps_q", [P, 2, B, L])

    w_ld = [sem(f"w_ld{s}") for s in range(2)]
    h_ld = [sem(f"h_ld{s}") for s in range(2)]
    wq_ld = [sem(f"wq_ld{s}") for s in range(2)]
    k_st = [sem(f"k_st{s}") for s in range(2)]
    v_st = [sem(f"v_st{s}") for s in range(2)]
    q_st = [sem(f"q_st{s}") for s in range(2)]
    w_hi_done, w_lo_done = sem("w_hi_done"), sem("w_lo_done")
    wq_hi_done, wq_lo_done = sem("wq_hi_done"), sem("wq_lo_done")
    h_hi_done, h_lo_done = sem("h_hi_done"), sem("h_lo_done")
    k_mm, v_mm, kb_done, vb_done = sem("k_mm"), sem("v_mm"), sem("kb_done"), sem("vb_done")
    q_mm, qb_done = sem("q_mm"), sem("qb_done")
    x1 = d["x1"].rearrange("k p (b l) -> b p k l", b=B)
    q_out = d["q"].rearrange("b (m p) l -> m p b l", p=P)

    def chunks(eng, body):
        with eng.Fori(0, B) as b:
            for c in range(CC):
                body(CC * b + c, c, b, c * L)
        for b in range(B):
            body(CC * B + b, b, b, CTX)

    with nc.Block() as block:
        @block.sync
        def _(sp):
            sp.dma_start(wraw[0][:], d["w_k"]).then_inc(w_ld[0], 16)
            sp.dma_start(h[0][:], d["ctx"][0]).then_inc(h_ld[0], 16)
            sp.dma_start(wraw[1][:], d["w_v"]).then_inc(w_ld[1], 16)
            sp.dma_start(h[1][:], d["ctx"][1]).then_inc(h_ld[1], 16)
            for q in range(2, NCH):
                sp.wait_ge(h_lo_done, q - 1)
                src = d["ctx"][q] if q < B * CC else x1[q - B * CC]
                sp.dma_start(h[q % 2][:], src).then_inc(h_ld[q % 2], 16)
            sp.wait_ge(w_lo_done, 2)
            for s in range(2):
                sp.dma_start(wq[s][:], d["w_q"][s]).then_inc(wq_ld[s], 16)
            def store_q(m, s):
                sp.wait_ge(qb_done, m + 3)
                sp.dma_start(q_out[m], qb[s][:]).then_inc(q_st[s], 16)

            with sp.Fori(0, QF // 2 - 1) as j:
                for s in range(2):
                    store_q(2 * j + s, s)
                    sp.wait_ge(wq_lo_done, 2 * j + s + 1)
                    sp.dma_start(wq[s][:], d["w_q"][2 * j + s + 2]).then_inc(wq_ld[s], 16)
            for s in range(2):
                store_q(QF - 2 + s, s)
            for s in range(2):
                sp.wait_ge(q_st[s], 16 * QF // 2)
                sp.wait_ge(k_st[s], 16 * NCH * KT // 2)
                sp.wait_ge(v_st[s], 16 * NCH * VT // 2)

        @block.scalar
        def _(act):
            def split(q, s):
                act.wait_ge(h_ld[s], 16 * (q // 2) + 16)
                nc.scalar.activation(h_hi[s][:], h[s][:], ACT.Copy).then_inc(h_hi_done, 1)

            def split_wq(m, s):
                act.wait_ge(wq_ld[s], 16 * (m // 2) + 16)
                nc.scalar.activation(wq_hi[s][:], wq[s][:], ACT.Copy).then_inc(wq_hi_done, 1)

            def body(q, s, b, t0):
                for i in range(KT):
                    n, e = KT * q + i, (s + i) % 2
                    act.wait_ge(k_mm, n + 1)
                    act.wait_ge(k_st[e], 16 * (n // 2))
                    nc.scalar.activation(kb[e][:], ps_k[:, e], ACT.Copy).then_inc(kb_done, 1)
                    act.wait_ge(kb_done, n + 3)
                    act.dma_start(d["k"][b, i * P:(i + 1) * P, t0:t0 + L], kb[e][:]).then_inc(k_st[e], 16)
                for i in range(VT):
                    n, e = VT * q + i, i % 2
                    act.wait_ge(v_mm, n + 1)
                    act.wait_ge(v_st[e], 16 * (n // 2))
                    nc.scalar.activation(vb[e][:], ps_v[:, e, 0:KW], ACT.Copy).then_inc(vb_done, 1)
                    act.wait_ge(vb_done, n + 3)
                    act.dma_start(d["v"][b, :, :, t0 // P + i].rearrange("g p d -> p g d"),
                                  vb[e][:].rearrange("p (g d) -> p g d", g=KV)).then_inc(v_st[e], 16)
                if isinstance(q, int) and q + 2 >= NCH:
                    split_wq(s, s)
                else:
                    split(q + 2, s)

            def query(m, s):
                act.wait_ge(q_mm, m + 1)
                act.wait_ge(q_st[s], 16 * (m // 2))
                nc.scalar.activation(qb[s][:], ps_q[:, s], ACT.Copy).then_inc(qb_done, 1)

            for free in (kb_done, vb_done, qb_done):
                act.sem_inc(free, 2)
            for n, hi in enumerate((wk_hi, wv_hi)):
                act.wait_ge(w_ld[n], 16)
                nc.scalar.activation(hi[:], wraw[n][:], ACT.Copy).then_inc(w_hi_done, 1)
                split(n, n)
            chunks(act, body)
            with act.Fori(0, QF // 2 - 1) as j:
                for s in range(2):
                    query(2 * j + s, s)
                    split_wq(2 * j + s + 2, s)
            for s in range(2):
                query(QF - 2 + s, s)

        @block.vector
        def _(dve):
            def split(q):
                dve.wait_ge(h_hi_done, q + 1)
                nc.vector.tensor_tensor(h_lo[q % 2][:], h[q % 2][:], f32(h_hi[q % 2][:]), ALU.subtract).then_inc(h_lo_done, 1)

            for n, (hi, lo) in enumerate(((wk_hi, wk_lo), (wv_hi, wv_lo))):
                dve.wait_ge(w_hi_done, n + 1)
                nc.vector.tensor_tensor(lo[:], wraw[n][:], f32(hi[:]), ALU.subtract).then_inc(w_lo_done, 1)
                split(n)
            for q in range(2, NCH):
                split(q)
            with dve.Fori(0, QF // 2) as j:
                for s in range(2):
                    dve.wait_ge(wq_hi_done, 2 * j + s + 1)
                    nc.vector.tensor_tensor(wq_lo[s][:], wq[s][:], f32(wq_hi[s][:]), ALU.subtract).then_inc(wq_lo_done, 1)

        @block.tensor
        def _(pe):
            def body(q, s, b, t0):
                pe.wait_ge(h_lo_done, q + 1)
                pe.wait_ge(w_lo_done, 1)
                for i in range(KT):
                    n, e = KT * q + i, (s + i) % 2
                    pe.wait_ge(kb_done, n + 1)
                    c = slice(i * P, (i + 1) * P)
                    for k in range(HT):
                        last = three_passes(nc, ps_k[:, e], wk_hi[:, k, c], wk_lo[:, k, c],
                                            h_hi[s][:, k], h_lo[s][:, k], k == 0, k == HT - 1)
                    last.then_inc(k_mm, 1)
                pe.wait_ge(w_lo_done, 2)
                for i in range(VT):
                    pe.wait_ge(vb_done, VT * q + i + 1)
                    c = slice(i * P, (i + 1) * P)
                    for k in range(HT):
                        last = three_passes(nc, ps_v[:, i % 2, 0:KW], h_hi[s][:, k, c], h_lo[s][:, k, c],
                                            wv_hi[:, k], wv_lo[:, k], k == 0, k == HT - 1)
                    last.then_inc(v_mm, 1)

            chunks(pe, body)
            with pe.Fori(0, QF // 2) as j:
                for s in range(2):
                    pe.wait_ge(wq_lo_done, 2 * j + s + 1)
                    pe.wait_ge(qb_done, 2 * j + s + 1)
                    for b in range(B):
                        for k in range(HT):
                            last = three_passes(nc, ps_q[:, s, b], wq_hi[s][:, k], wq_lo[s][:, k],
                                                h_hi[b][:, k], h_lo[b][:, k], k == 0, k == HT - 1)
                    last.then_inc(q_mm, 1)


def attention(nc, res, d):
    sb = Arena(nc, "at")

    def sem(n):
        return res.sem("at_" + n)

    NHD = B * NH
    NW = B * KV
    SCALE = 1.0 / float(HD) ** 0.5
    NSL = 6
    NQ = 4
    LAG = 4
    k = sb("k", [HD, S])
    v = sb("v", [P, ST, HD])
    q = [sb(f"q{s}", [HD, L]) for s in range(2)]
    k_hi = [sb(f"k_hi{s}", [HD + 1, S], F32R) for s in range(2)]
    k_lo = [sb(f"k_lo{s}", [HD, S], F32R) for s in range(2)]
    v_hi = [sb(f"v_hi{s}", [P, ST, HD + 1], F32R) for s in range(2)]
    v_lo = [sb(f"v_lo{s}", [P, ST, HD + 1], F32R) for s in range(2)]
    q_hi = [sb(f"q_hi{s}", [HD + 1, L], F32R) for s in range(NQ)]
    q_lo = [sb(f"q_lo{s}", [HD, L], F32R) for s in range(NQ)]
    p = [sb(f"p{s}", [P, L]) for s in range(NSL)]
    p_hi = [sb(f"p_hi{s}", [P, L], F32R) for s in range(NSL)]
    p_lo = [sb(f"p_lo{s}", [P, L], F32R) for s in range(NSL)]
    neg_max = sb("neg_max", [P, QT, HD + 1])
    ident = sb("ident", [P, P])
    ones = sb("ones", [P, P])
    ao = sb("ao", [HD + 1, L])
    rs = sb("rs", [P, QT])
    rs_diag = sb("rs_diag", [P, QT, P])
    on = [sb(f"on{s}", [HD, L]) for s in range(2)]

    NB = S // L
    ps_mx = res.bank("at_ps_mx", [P, NB, L])
    ps_s = [res.bank(f"at_ps_s{s}", [P, L]) for s in range(2)]
    ps_o = [res.bank(f"at_ps_o{s}", [HD + 1, L]) for s in range(2)]
    ps_t = res.bank("at_ps_t", [P, L])

    q_ld = [sem(f"q_ld{s}") for s in range(2)]
    on_st = [sem(f"on_st{s}") for s in range(2)]
    id_ld, kv_ld = sem("id_ld"), sem("kv_ld")
    set_done, before_done = sem("set_done"), sem("before_done")
    kv_hi_done, kv_lo_done = sem("kv_hi_done"), sem("kv_lo_done")
    q_hi_done, q_lo_done = sem("q_hi_done"), sem("q_lo_done")
    mx_mm, max_done, t_mm, row_done = sem("mx_mm"), sem("max_done"), sem("t_mm"), sem("row_done")
    s_mm, p_hi_done, pv_mm = sem("s_mm"), sem("p_hi_done"), sem("pv_mm")
    exp_done = sem("exp_done")
    p_lo_done = [sem("p_lo_even"), sem("p_lo_odd")]
    ao_done, sum_mm, rs_done, diag_done = sem("ao_done"), sem("sum_mm"), sem("rs_done"), sem("diag_done")
    bc_mm, on_done = sem("bc_mm"), sem("on_done")

    def heads(eng, body):
        with eng.Fori(0, NW // 2) as j:
            for s in range(2):
                for g in range(G):
                    body(2 * G * j + G * s + g, 2 * j + s, g, s)

    def lo_count(hd, t):
        return NSL // 2 + ST // 2 * hd + t // 2 + 1

    SET = 6 + 2 * LAG + 2

    def split_lo(eng, name, hd, t):
        eng.wait_ge(p_hi_done, ST * hd + t + 1)
        eng.wait_ge(pv_mm, ST * hd + t + 1)
        return name.tensor_tensor(p_lo[t % NSL][:], p[t % NSL][:], f32(p_hi[t % NSL][:]), ALU.subtract)

    with nc.Block() as block:
        @block.sync
        def _(sp):
            def load_kv(w):
                sp.dma_start(k[:], d["k"].rearrange("b (g e) s -> (b g) e s", g=KV)[w]).then_inc(kv_ld, 16)
                sp.dma_start(v[:], d["v"].rearrange("b g p t d -> (b g) p t d")[w]).then_inc(kv_ld, 16)

            def load_q(hd, s):
                sp.dma_start(q[s][:], d["q"].rearrange("b (h e) l -> (b h) e l", h=NH)[hd % NHD]).then_inc(q_ld[s], 16)

            def store(hd, s):
                sp.wait_ge(on_done, hd + 1)
                sp.dma_start(d["attn"][hd], on[s][:]).then_inc(on_st[s], 16)

            def body(hd, w, g, s):
                if g == 0:
                    sp.wait_ge(kv_lo_done, 2 * w + 2)
                    load_kv((w + 1) % NW)
                sp.wait_ge(q_lo_done, hd + 2)
                load_q(hd + 3, 1 - g % 2)
                store(hd, g % 2)

            load_q(0, 0)
            load_kv(0)
            load_q(1, 1)
            sp.dma_start(ident[:], d["ident"]).then_inc(id_ld, 16)
            sp.wait_ge(q_lo_done, 1)
            load_q(2, 0)
            heads(sp, body)
            store(NHD, 0)
            sp.wait_ge(on_st[0], 16 * (NHD // 2 + 1))
            sp.wait_ge(on_st[1], 16 * (NHD // 2))
            sp.wait_ge(q_ld[0], 16 * (NHD // 2 + 2))
            sp.wait_ge(q_ld[1], 16 * (NHD // 2 + 1))
            sp.wait_ge(kv_ld, 32 * (NW + 1))

        @block.scalar
        def _(act):
            def split_kv(w, s):
                act.wait_ge(kv_ld, 32 * (w + 1))
                nc.scalar.activation(k_hi[s][0:HD], k[:], ACT.Copy).then_inc(kv_hi_done, 1)
                nc.scalar.activation(v_hi[s][:, :, 0:HD], v[:], ACT.Copy).then_inc(kv_hi_done, 1)

            def queries(hd, s):
                act.wait_ge(q_ld[s % 2], 16 * (hd // 2 + 1))
                nc.scalar.activation(q_hi[s][0:HD], q[s % 2][:], ACT.Copy).then_inc(q_hi_done, 1)

            def row(hd, s):
                act.wait_ge(t_mm, hd + 1)
                nc.scalar.activation(q_hi[s][HD:HD + 1], ps_t[HD:HD + 1], ACT.Copy).then_inc(row_done, 1)

            def leave(hd, e):
                act.wait_ge(pv_mm, NSL + ST * hd)
                act.wait_ge(on_done, hd)
                nc.scalar.activation(ao[:], ps_o[1 - e][:], ACT.Copy).then_inc(ao_done, 1)

            def body(hd, w, g, s):
                for t in range(ST):
                    n = ST * hd + t
                    act.wait_ge(s_mm, n + 1)
                    act.wait_ge(p_lo_done[t % 2], ST // 2 * hd + t // 2 + 1)
                    nc.scalar.activation(p[t % NSL][:], ps_s[t % 2][:], ACT.Exp, scale=SCALE).then_inc(exp_done, 1)
                    act.wait_ge(exp_done, n + 3)
                    act.wait_ge(pv_mm, n + 1)
                    nc.scalar.activation(p_hi[t % NSL][:], p[t % NSL][:], ACT.Copy).then_inc(p_hi_done, 1)
                    if t == LAG:
                        leave(hd, g % 2)
                    if t == 6:
                        queries(hd + 2, (g + 2) % NQ)
                    if t == 7 and g == 1:
                        act.wait_ge(pv_mm, NSL + ST * G * w)
                        split_kv(w + 1, 1 - s)
                    if t == 10:
                        row(hd + 1, (g + 1) % NQ)

            act.sem_inc(exp_done, 2)
            act.wait_ge(set_done, 6)
            queries(0, 0)
            split_kv(0, 0)
            queries(1, 1)
            row(0, 0)
            act.wait_ge(before_done, 1)
            heads(act, body)
            leave(NHD, 0)

        @block.vector
        def _(dve):
            def split_kv(w, s):
                dve.wait_ge(kv_hi_done, 2 * w + 2)
                nc.vector.tensor_tensor(k_lo[s][:], k[:], f32(k_hi[s][0:HD]), ALU.subtract).then_inc(kv_lo_done, 1)
                nc.vector.tensor_tensor(v_lo[s][:, :, 0:HD], v[:], f32(v_hi[s][:, :, 0:HD]),
                                        ALU.subtract).then_inc(kv_lo_done, 1)

            def queries(hd, s):
                dve.wait_ge(q_hi_done, hd + 1)
                nc.vector.tensor_tensor(q_lo[s][:], q[s % 2][:], f32(q_hi[s][0:HD]), ALU.subtract).then_inc(q_lo_done, 1)

            def maximum(hd, i):
                dve.wait_ge(mx_mm, QT * hd + i + 1)
                dve.wait_ge(t_mm, hd)
                nc.vector.tensor_reduce(neg_max[:, i, HD:HD + 1], ps_mx[:].rearrange("p n l -> p (n l)"), AX_X,
                                        ALU.max, negate=True).then_inc(max_done, 1)

            def divide1(hd):
                dve.wait_ge(sum_mm, hd + 1)
                dve.wait_ge(bc_mm, hd)
                nc.vector.reciprocal(rs[:], ps_t[:, 0:QT]).then_inc(rs_done, 1)
                dve.wait_ge(rs_done, hd + 1)
                for i in range(QT):
                    nc.vector.tensor_scalar(rs_diag[:, i], ident[:], rs[:, i:i + 1], None,
                                            ALU.mult).then_inc(diag_done, 1)

            def divide2(hd, s):
                dve.wait_ge(bc_mm, hd + 1)
                dve.wait_ge(on_st[s], 16 * (hd // 2))
                nc.vector.tensor_tensor(on[s][:], ao[0:HD], ps_t[0:HD], ALU.mult).then_inc(on_done, 1)

            def body(hd, w, g, s):
                for t in range(ST):
                    if t % 2 == 0:
                        split_lo(dve, nc.vector, hd, t).then_inc(p_lo_done[0], 1)
                    if t in (1, 3, 5, 7):
                        maximum(hd + 1, t // 2)
                    if t == 6:
                        divide1(hd)
                    if t == 8:
                        divide2(hd, g % 2)
                    if t == 9:
                        queries(hd + 2, (g + 2) % NQ)
                    if t == 10 and g == 1:
                        split_kv(w + 1, 1 - s)

            dve.sem_inc(p_lo_done[0], NSL // 2)
            for s in range(2):
                nc.vector.memset(k_hi[s][HD:HD + 1].bitcast(F32), 1.0).then_inc(set_done, 1)
                nc.vector.memset(v_hi[s][:].bitcast(F32), 1.0).then_inc(set_done, 1)
                nc.vector.memset(v_lo[s][:].bitcast(F32), 0.0).then_inc(set_done, 1)
            for t in range(NSL - LAG, NSL):
                nc.vector.memset(p_hi[t][:].bitcast(F32), 1.0).then_inc(set_done, 1)
                nc.vector.memset(p_lo[t][:].bitcast(F32), 0.0).then_inc(set_done, 1)
            nc.vector.memset(neg_max[:], 0.0).then_inc(set_done, 1)
            nc.vector.memset(ones[:], 1.0).then_inc(set_done, 1)
            dve.wait_ge(set_done, SET)
            queries(0, 0)
            split_kv(0, 0)
            queries(1, 1)
            for i in range(QT):
                maximum(0, i)
            heads(dve, body)
            divide1(NHD)
            divide2(NHD, 0)

        @block.gpsimd
        def _(pool):
            def body(hd, w, g, s):
                for t in range(1, ST, 2):
                    split_lo(pool, nc.gpsimd, hd, t).then_inc(p_lo_done[1], 1)

            pool.sem_inc(p_lo_done[1], NSL // 2)
            heads(pool, body)

        @block.tensor
        def _(pe):
            def maximum(hd, w, e, s, i):
                if i == 0:
                    pe.wait_ge(q_hi_done, hd + 1)
                    pe.wait_ge(kv_hi_done, 2 * w + 1)
                pe.wait_ge(max_done, QT * hd + i)
                for c in range(NB):
                    last = nc.tensor.matmul(ps_mx[:, c], q_hi[e][0:HD, i * P:(i + 1) * P],
                                            k_hi[s][0:HD, c * L:(c + 1) * L], start=True, stop=True)
                last.then_inc(mx_mm, 1)

            def transposes(hd):
                pe.wait_ge(max_done, QT * hd + QT)
                pe.wait_ge(on_done, hd)
                for i in range(QT):
                    last = nc.tensor.transpose(ps_t[0:HD + 1, i * P:(i + 1) * P], neg_max[:, i], ident[:])
                last.then_inc(t_mm, 1)

            def scores(hd, t, e, s):
                pe.wait_ge(exp_done, ST * hd + t + 1)
                c = slice(t * P, (t + 1) * P)
                nc.tensor.matmul(ps_s[t % 2][:], k_hi[s][:, c], q_hi[e][:], start=True, stop=False)
                nc.tensor.matmul(ps_s[t % 2][:], k_hi[s][0:HD, c], q_lo[e][:], start=False, stop=False)
                nc.tensor.matmul(ps_s[t % 2][:], k_lo[s][:, c], q_hi[e][0:HD], start=False, stop=True).then_inc(s_mm, 1)

            def values(bank, t, s):
                three_passes(nc, ps_o[bank][:], v_hi[s][:, t], v_lo[s][:, t], p_hi[t % NSL][:], p_lo[t % NSL][:],
                             t == 0, t == ST - 1).then_inc(pv_mm, 1)

            def sums(hd):
                pe.wait_ge(ao_done, hd + 1)
                pe.wait_ge(on_done, hd)
                for i in range(QT):
                    last = nc.tensor.matmul(ps_t[:, i:i + 1], ao[HD:HD + 1, i * P:(i + 1) * P], ones[HD:HD + 1, 0:1],
                                            start=True, stop=True)
                last.then_inc(sum_mm, 1)

            def broadcast(hd):
                pe.wait_ge(diag_done, QT * hd + QT)
                for i in range(QT):
                    last = nc.tensor.matmul(ps_t[0:HD, i * P:(i + 1) * P], ones[:, 0:HD], rs_diag[:, i],
                                            start=True, stop=True)
                last.then_inc(bc_mm, 1)

            def body(hd, w, g, s):
                e = g % 2
                pe.wait_ge(row_done, hd + 1)
                pe.wait_ge(q_lo_done, hd + 1)
                if g == 0:
                    pe.wait_ge(kv_lo_done, 2 * w + 2)
                for t in range(ST):
                    scores(hd, t, g, s)
                    if t < LAG:
                        pe.wait_ge(p_lo_done[t % 2], lo_count(hd, t - LAG))
                        values(1 - e, ST + t - LAG, s if g else 1 - s)
                    else:
                        pe.wait_ge(p_lo_done[t % 2], lo_count(hd, t - LAG))
                        if t == LAG:
                            pe.wait_ge(ao_done, hd)
                        values(e, t - LAG, s)
                    if t in (0, 2, 4, 6):
                        nw = w + 1 if g == G - 1 else w
                        maximum(hd + 1, nw, (g + 1) % NQ, 1 - s if g == G - 1 else s, t // 2)
                    if t == 5:
                        sums(hd)
                    if t == 8:
                        broadcast(hd)
                    if t == 10:
                        transposes(hd + 1)

            pe.wait_ge(id_ld, 16)
            pe.wait_ge(set_done, SET)
            nc.tensor.matmul(ps_o[1][:], v_hi[1][:, 0], p_hi[NSL - 1][:], start=True, stop=False).then_inc(before_done, 1)
            pe.sem_inc(pv_mm, NSL - LAG)
            for i in range(QT):
                maximum(0, 0, 0, 0, i)
            transposes(0)
            heads(pe, body)
            for t in range(ST - LAG, ST):
                pe.wait_ge(p_lo_done[t % 2], lo_count(NHD - 1, t))
                values(1, t, 1)
            sums(NHD)
            broadcast(NHD)


def feed_forward(nc, res, d, out):
    sb = Arena(nc, "ff")

    def sem(n):
        return res.sem("ff_" + n)

    x_hi, x_lo = sb("x_hi", [P, HT, TOK], F32R), sb("x_lo", [P, HT, TOK], F32R)
    y = sb("y", [P, HT, TOK])
    h_hi, h_lo = sb("h_hi", [P, CF, B, L], F32R), sb("h_lo", [P, CF, B, L], F32R)
    w = [sb(f"w{s}", [P, HT, P]) for s in range(4)]
    w_hi = [sb(f"w_hi{s}", [P, HT, P], F32R) for s in range(4)]
    w_lo = [sb(f"w_lo{s}", [P, HT, P], F32R) for s in range(4)]
    w2 = [sb(f"w2_{s}", [P, CF, P]) for s in range(2)]
    w2_hi = [sb(f"w2_hi{s}", [P, CF, P], F32R) for s in range(2)]
    w2_lo = [sb(f"w2_lo{s}", [P, CF, P], F32R) for s in range(2)]
    sg = sb("sg", [P, B, L])
    hf = sb("hf", [P, B, L])
    scales = [sb(f"scale{n}", [P, FT * HT]) for n in range(3)]
    ln = Norm(nc, res, sb, "ff", sq=[sg, hf])
    ln.over(y)
    ps_g, ps_u = res.bank("ff_ps_g", [P, B, L]), res.bank("ff_ps_u", [P, B, L])
    ps_y = [ln.ps_mean, ln.ps_var]

    y_ld, sc_ld = sem("y_ld"), sem("sc_ld")
    w_ld = [sem(f"w_ld{s}") for s in range(4)]
    w2_ld = [sem(f"w2_ld{s}") for s in range(2)]
    x_hi_done, x_lo_done = sem("x_hi_done"), sem("x_lo_done")
    ws_done, w_hi_done, w_lo_done = sem("ws_done"), sem("w_hi_done"), sem("w_lo_done")
    w2s_done, w2_hi_done, w2_lo_done = sem("w2s_done"), sem("w2_hi_done"), sem("w2_lo_done")
    g_mm, u_mm, y_mm = sem("g_mm"), sem("u_mm"), sem("y_mm")
    sg_done, hf_done, h_hi_done, h_lo_done, y_done = (sem("sg_done"), sem("hf_done"), sem("h_hi_done"),
                                                      sem("h_lo_done"), sem("y_done"))

    with nc.Block() as block:
        @block.sync
        def _(sp):
            def load_w(f, e):
                for i, name in enumerate(("w_1", "w_3")):
                    sp.dma_start(w[2 * i + e][:], d[name][f % FT]).then_inc(w_ld[2 * i + e], 16)

            for m in range(HT):
                sp.dma_start(y[:, m], d["x2"][m]).then_inc(y_ld, 16)
                if m == 0:
                    load_w(0, 0)
                    for n, name in enumerate(("s_1", "s_3", "s_2")):
                        sp.dma_start(scales[n][:], d[name].partition_broadcast(P)).then_inc(sc_ld, 16)
            load_w(1, 1)
            for s in range(2):
                sp.dma_start(w2[s][:], d["w_2"][s]).then_inc(w2_ld[s], 16)
            with sp.Fori(0, FC) as c:
                for f in range(CF):
                    sp.wait_ge(w_lo_done, 2 * (CF * c + f) + 2)
                    load_w(CF * c + f + 2, f % 2)
                with sp.Fori(0, HT // 2) as j:
                    for s in range(2):
                        sp.wait_ge(w2_lo_done, HT * c + 2 * j + s + 1)
                        sp.dma_start(w2[s][:], d["w_2"][(HT * c + 2 * j + s + 2) % (FC * HT)]).then_inc(w2_ld[s], 16)
            for s in range(4):
                sp.wait_ge(w_ld[s], 16 * (FT // 2 + 1))
            for s in range(2):
                sp.wait_ge(w2_ld[s], 16 * (FC * HT // 2 + 1))
            ln.sync(sp, y, out)

        @block.scalar
        def _(act):
            def split_w(f, e):
                for i in range(2):
                    n = 2 * f + i
                    act.wait_ge(ws_done, n + 1)
                    act.wait_ge((g_mm, u_mm)[i], f)
                    nc.scalar.activation(w_hi[2 * i + e][:], w[2 * i + e][:], ACT.Copy).then_inc(w_hi_done, 1)

            def split_w2(n, s):
                act.wait_ge(w2s_done, n + 1)
                act.wait_ge(y_mm, n)
                nc.scalar.activation(w2_hi[s][:], w2[s][:], ACT.Copy).then_inc(w2_hi_done, 1)

            act.wait_ge(ws_done, 1)
            nc.scalar.activation(w_hi[0][:], w[0][:], ACT.Copy).then_inc(w_hi_done, 1)
            act.wait_ge(y_ld, 16 * HT)
            for m in range(HT):
                nc.scalar.activation(x_hi[:, m], y[:, m], ACT.Copy).then_inc(x_hi_done, 1)
            act.wait_ge(ws_done, 2)
            nc.scalar.activation(w_hi[2][:], w[2][:], ACT.Copy).then_inc(w_hi_done, 1)
            with act.Fori(0, FC) as c:
                for f in range(CF):
                    ff = CF * c + f
                    if f < CF - 1:
                        split_w(ff + 1, 1 - f % 2)
                    else:
                        for s in range(2):
                            split_w2(HT * c + s, s)
                    act.wait_ge(g_mm, ff + 2)
                    act.wait_ge(hf_done, ff)
                    nc.scalar.activation(sg[:], ps_g[:], ACT.Silu).then_inc(sg_done, 1)
                    act.wait_ge(hf_done, ff + 1)
                    act.wait_ge(y_mm, HT * c + 1)
                    nc.scalar.activation(h_hi[:, f], hf[:], ACT.Copy).then_inc(h_hi_done, 1)
                with act.Fori(0, HT // 2 - 1) as j:
                    for s in range(2):
                        split_w2(HT * c + 2 * j + s + 2, s)
                split_w(CF * c + CF, 0)
            ln.scalar(act)

        @block.vector
        def _(dve):
            def scale_w(f, e):
                for i in range(2):
                    slot = 2 * i + e
                    dve.wait_ge(w_ld[slot], 16 * (f // 2 + 1))
                    sc = scales[i][:, bass.ds((f % FT) * HT, HT)].unsqueeze(2).to_broadcast([P, HT, P])
                    nc.vector.tensor_tensor(w[slot][:], w[slot][:], sc, ALU.mult).then_inc(ws_done, 1)

            def rest_w(f, e):
                for i in range(2):
                    slot = 2 * i + e
                    dve.wait_ge(w_hi_done, 2 * f + i + 1)
                    nc.vector.tensor_tensor(w_lo[slot][:], w[slot][:], f32(w_hi[slot][:]),
                                            ALU.subtract).then_inc(w_lo_done, 1)

            def scale_w2(n, s):
                dve.wait_ge(w2_ld[s], 16 * (n // 2 + 1))
                sc = scales[2][:, bass.ds(n * CF, CF)].unsqueeze(2).to_broadcast([P, CF, P])
                nc.vector.tensor_tensor(w2[s][:], w2[s][:], sc, ALU.mult).then_inc(w2s_done, 1)

            def rest_w2(n, s):
                dve.wait_ge(w2_hi_done, n + 1)
                nc.vector.tensor_tensor(w2_lo[s][:], w2[s][:], f32(w2_hi[s][:]), ALU.subtract).then_inc(w2_lo_done, 1)

            def add_y(c, m, s):
                dve.wait_ge(y_mm, HT * c + m + 2)
                nc.vector.tensor_tensor(ln.tile(m), ln.tile(m), ps_y[s][:], ALU.add).then_inc(y_done, 1)

            ln.setup()
            dve.sem_inc(y_done, 1)
            dve.wait_ge(sc_ld, 48)
            scale_w(0, 0)
            for m in range(HT):
                dve.wait_ge(x_hi_done, m + 1)
                nc.vector.tensor_tensor(x_lo[:, m], y[:, m], f32(x_hi[:, m]), ALU.subtract).then_inc(x_lo_done, 1)
            rest_w(0, 0)
            with dve.Fori(0, FC) as c:
                for f in range(CF):
                    ff = CF * c + f
                    if f < CF - 1:
                        scale_w(ff + 1, 1 - f % 2)
                        rest_w(ff + 1, 1 - f % 2)
                    else:
                        for s in range(2):
                            scale_w2(HT * c + s, s)
                            rest_w2(HT * c + s, s)
                    dve.wait_ge(sg_done, ff + 1)
                    dve.wait_ge(u_mm, ff + 2)
                    dve.wait_ge(h_lo_done, ff)
                    nc.vector.tensor_tensor(hf[:], sg[:], ps_u[:], ALU.mult).then_inc(hf_done, 1)
                    dve.wait_ge(h_hi_done, ff + 1)
                    nc.vector.tensor_tensor(h_lo[:, f], hf[:], f32(h_hi[:, f]), ALU.subtract).then_inc(h_lo_done, 1)
                with dve.Fori(0, HT // 2 - 1) as j:
                    for s in range(2):
                        n = HT * c + 2 * j + s
                        scale_w2(n + 2, s)
                        add_y(c, 2 * j + s, s)
                        rest_w2(n + 2, s)
                scale_w(CF * c + CF, 0)
                rest_w(CF * c + CF, 0)
                for s in range(2):
                    add_y(c, HT - 2 + s, s)
            dve.wait_ge(y_done, FC * HT + 1)
            ln.vector(dve)

        @block.tensor
        def _(pe):
            def product(ps, slot):
                for k in range(HT):
                    pe.wait_ge(x_lo_done, k + 1)
                    for b in range(B):
                        t = slice(b * L, (b + 1) * L)
                        last = three_passes(nc, ps[:, b], w_hi[slot][:, k], w_lo[slot][:, k], x_hi[:, k, t],
                                            x_lo[:, k, t], k == 0, k == HT - 1)
                return last

            def down(c, m, s):
                n = HT * c + m
                pe.wait_ge(w2_lo_done, n + 1)
                pe.wait_ge(y_done, n)
                for k in range(CF):
                    pe.wait_ge(h_lo_done, CF * c + k + 1)
                    for b in range(B):
                        last = three_passes(nc, ps_y[s][:, b], w2_hi[s][:, k], w2_lo[s][:, k], h_hi[:, k, b],
                                            h_lo[:, k, b], k == 0, k == CF - 1)
                last.then_inc(y_mm, 1)

            for free in (g_mm, u_mm, y_mm):
                pe.sem_inc(free, 1)
            with pe.Fori(0, FC) as c:
                for f in range(CF):
                    ff = CF * c + f
                    pe.wait_ge(w_lo_done, 2 * ff + 1)
                    pe.wait_ge(sg_done, ff)
                    product(ps_g, f % 2).then_inc(g_mm, 1)
                    pe.wait_ge(w_lo_done, 2 * ff + 2)
                    pe.wait_ge(hf_done, ff)
                    product(ps_u, 2 + f % 2).then_inc(u_mm, 1)
                with pe.Fori(0, HT // 2) as j:
                    for s in range(2):
                        down(c, 2 * j + s, s)
            pe.wait_ge(ln.set, 2)
            pe.wait_ge(y_done, FC * HT + 1)
            for m in range(HT):
                ln.mean(y, m, m == 0, m == HT - 1)
            ln.tensor(pe)


def decoder_layer(nc, d):
    for name, shape in (("bc", [B, 2 * NS, L]), ("sz", [B * IT, P, L]), ("y", [B * IT + 1, P, L]), ("x1", [HT, P, TOK]), ("x2", [HT, P, TOK]),
                        ("q", [B, NH * HD, L]), ("k", [B, KV * HD, S]), ("v", [B, KV, P, ST, HD]), ("attn", [B * NH + 1, HD, L])):
        d[name] = nc.dram_tensor(name, shape, F32, kind="Internal").ap()
    xc = nc.alloc_sbuf_tensor_at("xc", [P, B * IT, L], F32, offset=TOP - 4 * B * IT * L)
    ssm_n = nc.alloc_sbuf_tensor_at("ssm_n", [E, TOK], F32, offset=TOP - 4 * B * IT * L - 4 * TOK)
    y = d["y"][1:].rearrange("(b i) p l -> i p b l", b=B)
    attn = d["attn"][1:].rearrange("(b h) e l -> b (h e) l", b=B).rearrange("b (i p) l -> i p b l", p=P)

    def phase(f, *args):
        res = Phase(nc)
        f(nc, res, *args)
        res.release()

    phase(mamba_in, d, xc, ssm_n)
    phase(mamba_scan, d, xc, ssm_n)
    phase(project_add_norm, "mo", IT, lambda i: y[i], d["w_out"], d["x_t"], d["x1"])
    phase(qkv_project, d)
    phase(attention, d)
    phase(project_add_norm, "ao", NH * HD // P, lambda i: attn[i], d["w_o"], d["x1"], d["x2"])
    phase(feed_forward, d, d["out"])


def kernel(**inputs):
    import concourse.bacc as bacc
    from concourse.bass_utils import run_bass_kernel_spmd

    a = {n: np.asarray(v) for n, v in inputs.items()}
    m, q, f = "L0_attn_", "L0_xattn_", "L0_ffn_"

    def tiles(w, mt, kt, split=1):
        w = w.reshape(mt, P, split, kt // split, -1).transpose(0, 2, 4, 3, 1)
        return w.reshape(mt * split, w.shape[2], kt // split, P)

    def cols(v):
        return v.reshape(-1, P).T

    x = a["x"].reshape(TOK, H).T
    group = np.repeat([0, 1, 2], [R, NS, NS])
    arrays = {
        "x_t": x.reshape(HT, P, TOK),
        "w_in": tiles(a[m + "in_proj_w"].T, 2 * IT, HT),
        "conv_w": a[m + "conv_w"].reshape(IT, P, KC).transpose(1, 0, 2),
        "conv_b": cols(a[m + "conv_b"]),
        "x_proj": a[m + "x_proj_w"].reshape(E, IT, P).transpose(2, 1, 0),
        "dt_w": a[m + "dt_proj_w"].reshape(IT, P, R).transpose(0, 2, 1),
        "dt_bias": cols(a[m + "dt_bias"]),
        "a_log": a[m + "A_log"].reshape(IT, P, NS).transpose(1, 0, 2),
        "d_param": cols(a[m + "D_param"]),
        "dt_ln": a[m + "dt_ln_w"].reshape(R, 1),
        "b_ln": a[m + "B_ln_w"].reshape(NS, 1),
        "c_ln": a[m + "C_ln_w"].reshape(NS, 1),
        "w_out": tiles(a[m + "out_proj_w"], HT, IT, split=2),
        "ctx": a["ctx_4096"].reshape(B, CTX // L, L, HT, P).transpose(0, 1, 4, 3, 2).reshape(-1, P, HT, L),
        "w_q": tiles(a[q + "Wq"], NH * HD // P, HT),
        "w_k": a[q + "Wk"].reshape(KV * HD, HT, P).transpose(2, 1, 0),
        "w_v": a[q + "Wv"].reshape(KV * HD, HT, P).transpose(2, 1, 0),
        "w_o": tiles(a[q + "Wo"], HT, NH * HD // P, split=2),
        "w_1": tiles(a[f + "w1"], FT, HT),
        "w_3": tiles(a[f + "w3"], FT, HT),
        "w_2": a[f + "w2"].reshape(HT, P, FC, CF, P).transpose(2, 0, 4, 3, 1).reshape(FC * HT, P, CF, P),
        "s_1": a[f + "w1_scale"].reshape(-1),
        "s_3": a[f + "w3_scale"].reshape(-1),
        "s_2": a[f + "w2_scale"].reshape(HT, FC, CF).transpose(1, 0, 2).reshape(-1),
        "ident": np.eye(P, dtype=np.float32),
        "mean_w": ((group[:, None] == group[None, :]) / np.repeat([R, NS, NS], [R, NS, NS])[:, None]).astype(np.float32),
    }
    nc = bacc.Bacc("TRN2", target_bir_lowering=False, num_devices=1)
    arrays = {f"in_{n}": np.ascontiguousarray(v) for n, v in arrays.items()}
    d = {n[3:]: nc.dram_tensor(n, v.shape, F32, kind="ExternalInput").ap() for n, v in arrays.items()}
    d["out"] = nc.dram_tensor("out", (HT, P, TOK), F32, kind="ExternalOutput").ap()
    decoder_layer(nc, d)
    r = run_bass_kernel_spmd(nc, [arrays], core_ids=[0])
    return r.results[0]["out"].reshape(H, TOK).T.reshape(B, L, H)
```

```python
from contextlib import ExitStack

import numpy as np

import concourse.bass as bass
from concourse import mybir

F32 = mybir.dt.float32
F32R = mybir.dt.float32r
ALU = mybir.AluOpType
ACT = mybir.ActivationFunctionType
AX_X = mybir.AxisListType.X

P = 128
B, L, H = 2, 512, 1024
TOK = B * L
HT = H // P
DIN, NS, R, KC = 2048, 16, 64, 4
IT = DIN // P
E = R + 2 * NS
CTX = 1024
NH, KV, HD = 16, 4, 96
G = NH // KV
S = CTX + L
ST = S // P
QT = L // P
FF = 3584
FT = FF // P
CF = 4
FC = FT // CF
RMS_EPS, LN_EPS = 1e-6, 1e-5
BASE = 16640
TOP = 229344


class Phase:

    def __init__(self, nc):
        self.nc, self.banks, self.sems = nc, ExitStack(), []

    def bank(self, name, shape):
        return self.banks.enter_context(self.nc.psum_tensor(name, shape, F32))

    def sem(self, name):
        self.sems.append(self.nc.alloc_semaphore(name))
        return self.sems[-1]

    def release(self):
        for s in self.sems:
            self.nc.sync.sem_clear(s)
            self.nc.release_semaphore(s)
        self.banks.close()


class Arena:

    def __init__(self, nc, phase, at=BASE):
        self.nc, self.phase, self.at = nc, phase, at

    def __call__(self, name, shape, dt=F32):
        size = 4
        for n in shape[1:]:
            size *= n
        size = (size + 31) // 32 * 32
        assert self.at + size <= TOP, (self.phase, name, self.at + size - TOP)
        t = self.nc.alloc_sbuf_tensor_at(f"{self.phase}_{name}", list(shape), dt, offset=self.at)
        self.at += size
        return t


def f32(ap):
    return ap.bitcast(F32)


def three_passes(nc, out, w_hi, w_lo, x_hi, x_lo, start, stop):
    nc.tensor.matmul(out, w_hi, x_hi, start=start, stop=False)
    nc.tensor.matmul(out, w_hi, x_lo, start=False, stop=False)
    return nc.tensor.matmul(out, w_lo, x_hi, start=False, stop=stop)


def mamba_in(nc, res, d, xc):
    sb = Arena(nc, "in")

    def sem(n):
        return res.sem("in_" + n)

    NT = 2 * IT
    x = sb("x", [P, HT, TOK])
    x_hi = sb("x_hi", [P, HT, TOK], F32R)
    x_lo = Arena(nc, "in")("x_lo", [P, HT, TOK], F32R)
    w = [sb(f"w{s}", [P, HT, P]) for s in range(2)]
    w_hi = [sb(f"w_hi{s}", [P, HT, P], F32R) for s in range(2)]
    w_lo = [sb(f"w_lo{s}", [P, HT, P], F32R) for s in range(2)]
    xz = [sb(f"xz{s}", [P, B, L + KC - 1]) for s in range(2)]
    acc = [sb(f"acc{s}", [P, B, L]) for s in range(2)]
    pre = [sb(f"pre{s}", [P, B, L]) for s in range(2)]
    xpw = sb("xpw", [P, IT, E])
    xpw_hi = [sb(f"xpw_hi{s}", [P, E], F32R) for s in range(2)]
    xpw_lo = [sb(f"xpw_lo{s}", [P, E], F32R) for s in range(2)]
    cw = sb("cw", [P, IT, KC])
    cb = sb("cb", [P, IT])
    lnw = sb("lnw", [E, 1])
    eps = sb("eps", [E, 1])
    meanw = sb("meanw", [E, E])
    zero = sb("zero", [P, P], F32R)
    over = Arena(nc, "in_over", sb.at)
    xc_hi = [sb(f"xc_hi{s}", [P, B, L], F32R) for s in range(2)]
    xc_lo = [sb(f"xc_lo{s}", [P, B, L], F32R) for s in range(2)]
    dtw = [sb(f"dtw{s}", [R, P]) for s in range(2)]
    dt_b = sb("dt_b", [P, IT])
    ssm, sq, rms, ssm_n = acc[0][0:E], acc[1][0:E], pre[0][0:E], pre[1][0:E]
    rl, ee = ([over(f"{n}{s}", [P, B, L]) for s in range(2)] for n in ("rl", "ee"))
    dd, ll = acc, [pre[0], sb("ll", [P, B, L])]
    assert sb.at <= TOP - 4 * B * IT * L

    ps = [res.bank(f"in_ps{s}", [P, B, L]) for s in range(2)]
    ps_dt = [res.bank(f"in_ps_dt{s}", [P, B, L]) for s in range(2)]
    ps_xp, ps_ms = ps_dt[0][0:E], ps_dt[1][0:E]

    x_ld = [sem(f"x_ld{k}") for k in range(HT)]
    w_ld = [sem(f"w_ld{s}") for s in range(2)]
    sz_st = [sem(f"sz_st{s}") for s in range(2)]
    par_ld, bc_st = sem("par_ld"), sem("bc_st")
    x_hi_done, x_lo_done = sem("x_hi_done"), sem("x_lo_done")
    w_hi_done, w_lo_done = sem("w_hi_done"), sem("w_lo_done")
    init_done, zeroed = sem("init_done"), sem("zeroed")
    main_done, conv_step = sem("main_done"), sem("conv_step")
    left = sem("left")
    xc_done, xc_hi_done, xc_lo_done = sem("xc_done"), sem("xc_hi_done"), sem("xc_lo_done")
    xpw_hi_done, xpw_done, xproj_done = sem("xpw_hi_done"), sem("xpw_done"), sem("xproj_done")
    ssm_done, sq_done, ms_done = sem("ssm_done"), sem("sq_done"), sem("ms_done")
    rms_done, rr_done, n_done = sem("rms_done"), sem("rr_done"), sem("n_done")
    dtw_ld = [sem(f"dtw_ld{s}") for s in range(2)]
    dt_st = [sem(f"dt_st{s}") for s in range(2)]
    dt_mm, part_done, e_done, l_done = sem("dt_mm"), sem("part_done"), sem("e_done"), sem("l_done")
    one_done, rest_done, ln_done, dt_done = sem("one_done"), sem("rest_done"), sem("ln_done"), sem("dt_done")
    XP_LAST = IT + 1

    xc4 = xc[:].rearrange("p (b i) l -> p b i l", b=B)
    sz, dt = (d[n].rearrange("(b i) p l -> i p b l", b=B) for n in ("sz", "dt"))

    with nc.Block() as block:
        @block.sync
        def _(sp):
            def next_w(m, s):
                sp.wait_ge(w_lo_done, m + 1)
                sp.dma_start(w[s][:], d["w_in"][m + 2]).then_inc(w_ld[s], 16)

            def store_gate(m, s):
                sp.wait_ge(left, m + 2)
                sp.dma_start(sz[m - IT], xz[s][:, :, KC - 1:]).then_inc(sz_st[s], 16)

            for s in range(2):
                sp.dma_start(w[s][:], d["w_in"][s]).then_inc(w_ld[s], 16)
                for k in range(4 * s, 4 * s + 4):
                    sp.dma_start(x[:, k], d["x_t"][k]).then_inc(x_ld[k], 16)
            sp.dma_start(cw[:], d["conv_w"]).then_inc(par_ld, 16)
            sp.dma_start(cb[:], d["conv_b"]).then_inc(par_ld, 16)
            sp.dma_start(xpw[:], d["x_proj"]).then_inc(par_ld, 16)
            sp.dma_start(meanw[:], d["mean_w"]).then_inc(par_ld, 16)
            sp.dma_start(lnw[0:R], d["dt_ln"]).then_inc(par_ld, 16)
            sp.dma_start(lnw[R:R + NS], d["b_ln"]).then_inc(par_ld, 16)
            sp.dma_start(lnw[R + NS:E], d["c_ln"]).then_inc(par_ld, 16)
            sp.dma_start(dt_b[:], d["dt_bias"]).then_inc(par_ld, 16)
            for s in range(2):
                sp.dma_start(dtw[s][:], d["dt_w"][s]).then_inc(dtw_ld[s], 16)
            with sp.Fori(0, IT // 2) as j:
                for s in range(2):
                    next_w(2 * j + s, s)
            for s in range(2):
                next_w(IT + s, s)
                store_gate(IT + s, s)

            def store_dt(i, s):
                sp.wait_ge(dt_done, i + 1)
                sp.dma_start(dt[i], dd[s][:]).then_inc(dt_st[s], 16)

            with sp.Fori(IT // 2 + 1, IT - 1) as j:
                next_w(2 * j, 0)
                store_gate(2 * j, 0)
                next_w(2 * j + 1, 1)
                i = 2 * j - IT - 2
                for s in range(2):
                    sp.wait_ge(dt_mm, i + s + 1)
                    sp.dma_start(dtw[s][:], d["dt_w"][i + s + 2]).then_inc(dtw_ld[s], 16)
                store_gate(2 * j + 1, 1)
                for s in range(2):
                    store_dt(i + s, s)
            for s in range(2):
                sp.wait_ge(dt_mm, IT - 3 + s)
                sp.dma_start(dtw[s][:], d["dt_w"][IT - 2 + s]).then_inc(dtw_ld[s], 16)
            for s in range(2):
                store_dt(IT - 4 + s, s)
            store_gate(NT - 2, 0)
            for s in range(2):
                store_dt(IT - 2 + s, s)
            store_gate(NT - 1, 1)
            sp.wait_ge(n_done, 1)
            sp.dma_start(d["bc"].rearrange("b r l -> r b l"),
                         ssm_n[R:E]).then_inc(bc_st, 16)
            sp.wait_ge(bc_st, 16)
            for s in range(2):
                sp.wait_ge(sz_st[s], 16 * IT // 2)
                sp.wait_ge(dt_st[s], 16 * IT // 2)

        @block.scalar
        def _(act):
            def split_w(s, load):
                act.wait_ge(w_ld[s], load)
                nc.scalar.activation(w_hi[s][:], w[s][:], ACT.Copy).then_inc(w_hi_done, 1)

            def next_w(m, s):
                act.wait_ge(main_done, m)
                split_w(1 - s, 16 * (m // 2 + 1 + s))

            def gate(m, s):
                act.wait_ge(main_done, m + 1)
                act.wait_ge(sz_st[s], 16 * ((m - IT) // 2))
                nc.scalar.activation(xz[s][:, :, KC - 1:], ps[s][:], ACT.Silu).then_inc(left, 1)

            act.sem_inc(left, 1)
            split_w(0, 16)
            for k in range(HT):
                act.wait_ge(x_ld[k], 16)
                nc.scalar.activation(x_hi[:, k], x[:, k], ACT.Copy).then_inc(x_hi_done, 1)
            act.wait_ge(init_done, 3)
            with act.Fori(0, IT // 2) as j:
                for s in range(2):
                    m = 2 * j + s
                    next_w(m, s)
                    act.wait_ge(main_done, m + 1)
                    act.wait_ge(conv_step, 8 * j)
                    nc.scalar.activation(xz[s][:, :, KC - 1:], ps[s][:], ACT.Copy).then_inc(left, 1)
                    act.wait_ge(conv_step, 4 * m + 4)
                    nc.scalar.activation(xc4[:, :, m, :], pre[s][:], ACT.Silu).then_inc(xc_done, 1)
                    act.wait_ge(zeroed, 5)
                    act.wait_ge(xproj_done, m)
                    act.wait_ge(xc_done, m + 1)
                    nc.scalar.activation(xc_hi[s][:], xc4[:, :, m, :], ACT.Copy).then_inc(xc_hi_done, 1)
            next_w(IT, 0)
            gate(IT, 0)
            act.wait_ge(xproj_done, XP_LAST)
            nc.scalar.activation(ssm, ps_xp, ACT.Copy).then_inc(ssm_done, 1)
            nc.scalar.activation(sq, ps_xp, ACT.Square).then_inc(sq_done, 1)
            next_w(IT + 1, 1)
            gate(IT + 1, 1)
            act.wait_ge(ms_done, 1)
            nc.scalar.activation(rms, ps_ms, ACT.Sqrt, bias=eps[:, 0:1]).then_inc(rms_done, 1)

            def exponentials(i):
                act.wait_ge(dt_done, i)
                for s in range(2):
                    bias = dt_b[:, bass.ds(i + s, 1)]
                    act.wait_ge(dt_mm, i + s + 1)
                    nc.scalar.activation(ee[s][:], ps_dt[s][:], ACT.Abs, bias=bias).then_inc(part_done, 1)
                    nc.scalar.activation(rl[s][:], ps_dt[s][:], ACT.Relu, bias=bias).then_inc(part_done, 1)
                for s in range(2):
                    act.wait_ge(part_done, 2 * (i + s) + 2)
                    nc.scalar.activation(ee[s][:], ee[s][:], ACT.Exp, scale=-1.0).then_inc(e_done, 1)

            def logarithms(i):
                for s in range(2):
                    act.wait_ge(e_done, i + s + 1)
                    nc.scalar.activation(ll[s][:], ee[s][:], ACT.Ln, bias=1.0).then_inc(l_done, 1)

            with act.Fori(IT // 2 + 1, IT - 1) as j:
                next_w(2 * j, 0)
                gate(2 * j, 0)
                next_w(2 * j + 1, 1)
                exponentials(2 * j - IT - 2)
                logarithms(2 * j - IT - 2)
                gate(2 * j + 1, 1)
            next_w(NT - 2, 0)
            exponentials(IT - 4)
            logarithms(IT - 4)
            gate(NT - 2, 0)
            exponentials(IT - 2)
            logarithms(IT - 2)
            gate(NT - 1, 1)

        @block.vector
        def _(dve):
            def split_w(s, n):
                dve.wait_ge(w_hi_done, n)
                nc.vector.tensor_tensor(w_lo[s][:], w[s][:], f32(w_hi[s][:]), ALU.subtract).then_inc(w_lo_done, 1)

            for s in range(2):
                nc.vector.memset(xz[s][:, :, 0:KC - 1], 0.0).then_inc(init_done, 1)
            nc.vector.memset(eps[:], RMS_EPS).then_inc(init_done, 1)
            nc.vector.memset(zero[:].bitcast(F32), 0.0).then_inc(zeroed, 1)
            nc.vector.memset(xpw_hi[1][:].bitcast(F32), 0.0).then_inc(zeroed, 1)
            nc.vector.memset(xpw_lo[1][:].bitcast(F32), 0.0).then_inc(zeroed, 1)
            nc.vector.memset(xc_hi[1][:].bitcast(F32), 0.0).then_inc(zeroed, 1)
            nc.vector.memset(xc_lo[1][:].bitcast(F32), 0.0).then_inc(zeroed, 1)
            split_w(0, 1)
            for k in range(HT):
                dve.wait_ge(x_hi_done, k + 1)
                nc.vector.tensor_tensor(x_lo[:, k], x[:, k], f32(x_hi[:, k]), ALU.subtract).then_inc(x_lo_done, 1)
            dve.wait_ge(par_ld, 16 * 8)
            with dve.Fori(0, IT // 2) as j:
                for s in range(2):
                    m = 2 * j + s
                    dve.wait_ge(main_done, m)
                    split_w(1 - s, m + 2)
                    dve.wait_ge(xpw_hi_done, m + 1)
                    nc.vector.tensor_tensor(xpw_lo[s][:], xpw[:, m, :], f32(xpw_hi[s][:]),
                                            ALU.subtract).then_inc(xpw_done, 1)
                    dve.wait_ge(left, m + 2)
                    dve.wait_ge(xc_done, 2 * j)
                    nc.vector.tensor_scalar(acc[s][:], xz[s][:, :, 0:L], cw[:, m, 0:1], cb[:, bass.ds(m, 1)],
                                            ALU.mult, ALU.add).then_inc(conv_step, 1)
                    for t in range(1, KC):
                        a, o = (acc, pre) if t % 2 else (pre, acc)
                        dve.wait_ge(conv_step, 4 * m + t)
                        nc.vector.scalar_tensor_tensor(o[s][:], xz[s][:, :, t:t + L], cw[:, m, t:t + 1], a[s][:],
                                                       ALU.mult, ALU.add).then_inc(conv_step, 1)
                    dve.wait_ge(xc_hi_done, m + 1)
                    nc.vector.tensor_tensor(xc_lo[s][:], xc4[:, :, m, :], f32(xc_hi[s][:]),
                                            ALU.subtract).then_inc(xc_lo_done, 1)
            for s in range(2):
                dve.wait_ge(main_done, IT + s)
                split_w(1 - s, IT + s + 2)
            dve.wait_ge(rms_done, 1)
            nc.vector.reciprocal(sq, rms).then_inc(rr_done, 1)
            dve.wait_ge(rr_done, 1)
            nc.vector.scalar_tensor_tensor(ssm_n, ssm, lnw[:, 0:1], sq, ALU.mult, ALU.mult).then_inc(n_done, 1)

            def softplus(i):
                for s in range(2):
                    dve.wait_ge(e_done, i + s + 1)
                    dve.wait_ge(dt_st[s], 16 * (i // 2))
                    nc.vector.tensor_scalar(dd[s][:], ee[s][:], 1.0, -1.0, ALU.add, ALU.add).then_inc(one_done, 1)
                for s in range(2):
                    dve.wait_ge(one_done, i + s + 1)
                    nc.vector.tensor_tensor(dd[s][:], ee[s][:], dd[s][:], ALU.subtract).then_inc(rest_done, 1)
                for s in range(2):
                    dve.wait_ge(l_done, i + s + 1)
                    dve.wait_ge(rest_done, i + s + 1)
                    nc.vector.tensor_tensor(dd[s][:], dd[s][:], ll[s][:], ALU.add).then_inc(ln_done, 1)
                for s in range(2):
                    dve.wait_ge(ln_done, i + s + 1)
                    nc.vector.tensor_tensor(dd[s][:], dd[s][:], rl[s][:], ALU.add).then_inc(dt_done, 1)

            with dve.Fori(IT // 2 + 1, IT - 1) as j:
                for s in range(2):
                    dve.wait_ge(main_done, 2 * j + s)
                    split_w(1 - s, 2 * j + s + 2)
                softplus(2 * j - IT - 2)
            dve.wait_ge(main_done, NT - 2)
            split_w(1, NT)
            softplus(IT - 4)
            softplus(IT - 2)

        @block.gpsimd
        def _(pool):
            pool.wait_ge(par_ld, 16 * 8)
            pool.wait_ge(zeroed, 5)
            with pool.Fori(0, IT // 2) as j:
                for s in range(2):
                    m = 2 * j + s
                    pool.wait_ge(xproj_done, m)
                    nc.gpsimd.tensor_copy(xpw_hi[s][:], xpw[:, m, :]).then_inc(xpw_hi_done, 1)

        @block.tensor
        def _(pe):
            def main(m, s):
                pe.wait_ge(w_lo_done, m + 1)
                pe.wait_ge(left, m)
                for k in range(HT):
                    pe.wait_ge(x_lo_done, k + 1)
                    for b in range(B):
                        c = slice(b * L, (b + 1) * L)
                        last = three_passes(nc, ps[s][:, b], w_hi[s][:, k], w_lo[s][:, k], x_hi[:, k, c], x_lo[:, k, c],
                                            k == 0, k == HT - 1)
                last.then_inc(main_done, 1)

            def xproj(s, ready, stop=False):
                pe.wait_ge(xc_lo_done, ready)
                pe.wait_ge(xpw_done, ready)
                for b in range(B):
                    last = three_passes(nc, ps_xp[:, b], xpw_hi[s][:], xpw_lo[s][:], xc_hi[s][:, b], xc_lo[s][:, b],
                                        False, stop)
                last.then_inc(xproj_done, 1)

            pe.wait_ge(zeroed, 5)
            pe.wait_ge(x_lo_done, 1)
            for b in range(B):
                nc.tensor.matmul(ps_xp[:, b], zero[:, 0:E], x_hi[:, 0, 0:L], start=True, stop=False)
            with pe.Fori(0, IT // 2) as j:
                for s in range(2):
                    main(2 * j + s, s)
                    xproj(1 - s, 2 * j + s)
            main(IT, 0)
            xproj(1, IT, stop=True)
            main(IT + 1, 1)
            pe.wait_ge(sq_done, 1)
            pe.wait_ge(par_ld, 16 * 8)
            for b in range(B):
                last = nc.tensor.matmul(ps_ms[:, b], meanw[:], sq[:, b], start=True, stop=True)
            last.then_inc(ms_done, 1)

            def dt_products(i):
                pe.wait_ge(n_done, 1)
                pe.wait_ge(part_done, 2 * i)
                for s in range(2):
                    pe.wait_ge(dtw_ld[s], 16 * (i // 2 + 1))
                    for b in range(B):
                        last = nc.tensor.matmul(ps_dt[s][:, b], dtw[s][:], ssm_n[0:R, b], start=True, stop=True)
                    last.then_inc(dt_mm, 1)

            with pe.Fori(IT // 2 + 1, IT - 1) as j:
                main(2 * j, 0)
                dt_products(2 * j - IT - 2)
                main(2 * j + 1, 1)
            for s in range(2):
                dt_products(IT - 4 + 2 * s)
                main(NT - 2 + s, s)


def mamba_scan(nc, res, d, xc):
    sb = Arena(nc, "scan")

    def sem(n):
        return res.sem("scan_" + n)

    NIT = B * IT
    NK = NS // 2
    CH = 4
    SL = 4
    SB = 3
    KW = KV * HD
    KF = KW // P
    KC_TOK = 256
    NC_B = CTX // KC_TOK
    NKC = B * NC_B
    NU = KF * NKC
    assert KF == SB and NU <= NIT - 2
    b_bc = sb("b_bc", [P, NS, L])
    c_bc = sb("c_bc", [P, NS, L])
    dbx = [sb(f"dbx{s}", [P, 2, L]) for s in range(SL)]
    g = [sb(f"g{s}", [P, 2, L]) for s in range(SB)]
    dt = [sb(f"dt{s}", [P, L]) for s in range(SB)]
    u = [sb(f"u{s}", [P, L]) for s in range(SB)]
    sz = [sb(f"sz{s}", [P, L]) for s in range(SB)]
    yb = [sb(f"yb{s}", [P, L]) for s in range(SB)]
    a_neg = sb("a_neg", [P, NIT, NS])
    a_exp = sb("a_exp", [P, NIT, NS])
    d_p = sb("d_p", [P, NIT])
    ident = sb("ident", [P, P])
    d_diag = [sb(f"d_diag{s}", [P, P]) for s in range(SB)]
    wk = sb("wk", [P, HT, KW])
    cx = sb("cx", [P, HT, KC_TOK])
    kb = sb("kb", [P, KC_TOK])
    assert sb.at <= TOP - 4 * NIT * L

    ps_a = [res.bank(f"scan_ps_a{s}", [P, 2, L]) for s in range(SB)]
    ps_y = res.bank("scan_ps_y", [P, L])
    ps_k = res.bank("scan_ps_k", [P, KC_TOK])

    par_ld = sem("par_ld")
    b_ld = [sem(f"b_ld{c}") for c in range(NS // CH)]
    c_ld = [sem(f"c_ld{c}") for c in range(NS // CH)]
    dt_ld = [sem(f"dt_ld{s}") for s in range(SB)]
    sz_ld = [sem(f"sz_ld{s}") for s in range(SB)]
    y_st = [sem(f"y_st{s}") for s in range(SB)]
    a_exp_done, a_done, diag_done, u_done = sem("a_exp_done"), sem("a_done"), sem("diag_done"), sem("u_done")
    a_ready, dbx_ready, epi_done = sem("a_ready"), sem("dbx_ready"), sem("epi_done")
    scanned = sem("scanned")
    g_ready = sem("g_ready")
    summed = sem("summed")
    wk_ld, cx_ld, k_mm, kb_done, k_st = sem("wk_ld"), sem("cx_ld"), sem("k_mm"), sem("kb_done"), sem("k_st")

    def blocks(eng, body):
        body(0, 0, None, None)
        with eng.Fori(0, NKC) as j:
            for s in range(SB):
                body(SB * j + s + 1, (s + 1) % SB, j, s)
        with eng.Fori(NKC, (NIT - 2) // SB) as j:
            for s in range(SB):
                body(SB * j + s + 1, (s + 1) % SB, None, None)
        body(NIT - 1, (NIT - 1) % SB, None, None)

    with nc.Block() as block:
        @block.sync
        def _(sp):
            def load_b(b, c):
                n = c * CH
                sp.dma_start(b_bc[:, n:n + CH], d["bc"][b, n:n + CH].partition_broadcast(P)).then_inc(b_ld[c], 16)

            def load_c(b, c):
                n = c * CH
                sp.dma_start(c_bc[:, n:n + CH], d["bc"][b, NS + n:NS + n + CH].partition_broadcast(P)).then_inc(c_ld[c], 16)

            def load_dt(it, s):
                sp.dma_start(dt[s][:], d["dt"][it]).then_inc(dt_ld[s], 16)

            def load_sz(it, s):
                sp.dma_start(sz[s][:], d["sz"][it]).then_inc(sz_ld[s], 16)

            def store(it, s):
                sp.wait_ge(epi_done, it + 1)
                sp.dma_start(d["y"][it], yb[s][:]).then_inc(y_st[s], 16)

            def body(it, s):
                sp.wait_ge(a_ready, 2 * NK * it)
                sp.wait_ge(u_done, it)
                load_dt(it + 2, (s + 2) % SB)
                store(it - 1, (s + 2) % SB)
                load_sz(it + 1, (s + 1) % SB)

            def load_chunk(c):
                sp.dma_start(cx[:], d["ctx"][c // 2][:, :, bass.ds((c % 2) * KC_TOK, KC_TOK)]).then_inc(cx_ld, 16)

            def three_blocks(j):
                for s in range(SB):
                    body(SB * j + s + 1, (s + 1) % SB)

            def next_chunk(j):
                sp.wait_ge(k_mm, KF * j + KF)
                load_chunk((j + 1) % NKC)

            def blocks_with_keys(first, last):
                with sp.Fori(first, last) as j:
                    three_blocks(j)
                    next_chunk(j)

            def next_batch():
                last = NK * (IT - 1)
                for c in range(NS // CH):
                    sp.wait_ge(dbx_ready, last + (c + 1) * CH // 2)
                    load_b(1, c)
                    if c:
                        sp.wait_ge(g_ready, SB + last + c * CH // 2)
                        load_c(1, c - 1)
                    if c == 1:
                        next_chunk(HALF - 1)
                sp.wait_ge(g_ready, SB + NK * IT)
                load_c(1, NS // CH - 1)

            load_dt(0, 0)
            load_b(0, 0)
            load_c(0, 0)
            load_dt(1, 1)
            for c in range(1, NS // CH):
                load_b(0, c)
                load_c(0, c)
            load_sz(0, 0)
            load_dt(2, 2)
            load_sz(1, 1)
            sp.dma_start(wk[:], d["w_k"]).then_inc(wk_ld, 16)
            load_chunk(0)
            HALF = (IT - 1) // SB
            blocks_with_keys(0, HALF - 1)
            three_blocks(HALF - 1)
            next_batch()
            blocks_with_keys(HALF, NKC)
            with sp.Fori(NKC, (NIT - 2) // SB - 1) as j:
                three_blocks(j)
            for it in range(NIT - 4, NIT):
                if it + 2 < NIT:
                    body(it, it % SB)
                else:
                    store(it - 1, (it - 1) % SB)
                    if it + 1 < NIT:
                        load_sz(it + 1, (it + 1) % SB)
            store(NIT - 1, (NIT - 1) % SB)
            for s in range(SB):
                sp.wait_ge(y_st[s], 16 * len(range(s, NIT, SB)))
            sp.wait_ge(k_st, 16 * NU)
            sp.wait_ge(cx_ld, 16 * (NKC + 1))

        @block.scalar
        def _(act):
            def diagonal(it, s):
                nc.scalar.activation(d_diag[s][:], ident[:], ACT.Copy, scale=d_p[:, bass.ds(it, 1)]).then_inc(diag_done, 1)

            def store_keys(c, i):
                act.wait_ge(k_mm, KF * c + i + 1)
                act.wait_ge(k_st, 16 * (KF * c + i))
                nc.scalar.activation(kb[:], ps_k[:], ACT.Copy).then_inc(kb_done, 1)
                act.wait_ge(kb_done, KF * c + i + 1)
                act.dma_start(d["k"][c // NC_B, i * P:(i + 1) * P, bass.ds((c % NC_B) * KC_TOK, KC_TOK)],
                              kb[:]).then_inc(k_st, 16)

            def body(it, s, chunk, tile):
                act.wait_ge(dt_ld[s], 16 * (it // SB + 1))
                for k in range(NK):
                    n = NK * it + k
                    act.wait_ge(g_ready, n + 1)
                    for h in range(2):
                        nc.scalar.activation(ps_a[(2 * s + k) % SB][:, h], dt[s][:], ACT.Exp,
                                             scale=a_neg[:, it, 2 * k + h:2 * k + h + 1]).then_inc(a_ready, 1)
                    if k == 4 and not (isinstance(it, int) and it == NIT - 1):
                        act.wait_ge(summed, NK * it + 1)
                        diagonal(it + 1, (s + 1) % SB)
                if chunk is not None:
                    store_keys(chunk, tile)

            act.dma_start(a_exp[:, 0:IT, :], d["a_log"]).then_inc(par_ld, 16)
            act.dma_start(a_exp[:, IT:NIT, :], d["a_log"]).then_inc(par_ld, 16)
            for b in range(B):
                act.dma_start(d_p[:, b * IT:(b + 1) * IT], d["d_param"]).then_inc(par_ld, 16)
            act.dma_start(ident[:], d["ident"]).then_inc(par_ld, 16)
            act.wait_ge(par_ld, 16 * 5)
            nc.scalar.activation(a_exp[:], a_exp[:], ACT.Exp).then_inc(a_exp_done, 1)
            act.wait_ge(a_exp_done, 1)
            nc.scalar.activation(a_neg[:], a_exp[:], ACT.Copy, scale=-1.0).then_inc(a_done, 1)
            act.wait_ge(a_done, 1)
            diagonal(0, 0)
            blocks(act, body)

        @block.vector
        def _(dve):
            def times_c(n, s, k):
                dve.wait_ge(scanned, 2 * SL + 2 * n + 2)
                dve.wait_ge(summed, n + 2)
                nc.vector.tensor_tensor(g[s][:], ps_a[s][:], c_bc[:, 2 * k:2 * k + 2], ALU.mult).then_inc(g_ready, 1)

            def after(it, s):
                dve.wait_ge(summed, SB + 1 + NK * it + NK)
                dve.wait_ge(sz_ld[s], 16 * (it // SB + 1))
                dve.wait_ge(y_st[s], 16 * (it // SB))
                nc.vector.tensor_tensor(yb[s][:], ps_y[:], sz[s][:], ALU.mult).then_inc(epi_done, 1)

            def body(it, s, chunk, tile):
                first = isinstance(it, int) and it == 0
                for k in range(NK):
                    n = NK * it + k
                    slot = (2 * s + k) % SB
                    dve.wait_ge(dbx_ready, n + 1)
                    for h in range(2):
                        dve.wait_ge(a_ready, 2 * n + h + 1)
                        nc.vector.tensor_tensor_scan(ps_a[slot][:, h], ps_a[slot][:, h], dbx[k % SL][:, h], 0.0,
                                                     ALU.mult, ALU.add).then_inc(scanned, 1)
                    if k % 2 == 1:
                        dve.wait_ge(c_ld[k // 2], 16 * (it // IT + 1))
                    if not (first and k == 0):
                        times_c(n - 1, (slot - 1) % SB, (k - 1) % NK)
                    if k == 2 and not first:
                        after(it - 1, (s - 1) % SB)

            for free, count in ((scanned, 2 * SL), (g_ready, SB)):
                dve.sem_inc(free, count)
            blocks(dve, body)
            last = NIT - 1
            times_c(NK * NIT - 1, (2 * last + NK - 1) % SB, NK - 1)
            after(last, last % SB)

        @block.gpsimd
        def _(pool):
            def make_u(it, s):
                pool.wait_ge(dt_ld[s], 16 * (it // SB + 1))
                nc.gpsimd.tensor_tensor(u[s][:], dt[s][:], xc[:, it, :], ALU.mult).then_inc(u_done, 1)

            def body(it, s, chunk, tile):
                pool.wait_ge(u_done, it + 1)
                for k in range(NK):
                    if k % 2 == 0:
                        pool.wait_ge(b_ld[k // 2], 16 * (it // IT + 1))
                    pool.wait_ge(scanned, 2 * (NK * it + k) + 2)
                    nc.gpsimd.tensor_tensor(dbx[k % SL][:], u[s][:].unsqueeze(1).to_broadcast([P, 2, L]),
                                            b_bc[:, 2 * k:2 * k + 2], ALU.mult).then_inc(dbx_ready, 1)
                    if k == 4 and not (isinstance(it, int) and it == NIT - 1):
                        pool.wait_ge(dbx_ready, NK * it)
                        make_u(it + 1, (s + 1) % SB)

            make_u(0, 0)
            blocks(pool, body)

        @block.tensor
        def _(pe):
            def body(it, s, chunk, tile):
                def key_product(k):
                    return nc.tensor.matmul(ps_k[:], wk[:, k, tile * P:(tile + 1) * P], cx[:, k], start=k == 0, stop=k == HT - 1)

                if chunk is not None:
                    pe.wait_ge(wk_ld, 16)
                    pe.wait_ge(cx_ld, 16 * (chunk + 1))
                    pe.wait_ge(kb_done, KF * chunk + tile)
                    for k in range(HT // 2):
                        key_product(k)
                pe.wait_ge(epi_done, it)
                pe.wait_ge(diag_done, it + 1)
                nc.tensor.matmul(ps_y[:], d_diag[s][:], xc[:, it], start=True, stop=False)
                for k in range(NK):
                    pe.wait_ge(g_ready, SB + NK * it + k + 1)
                    for h in range(2):
                        last = nc.tensor.matmul(ps_y[:], ident[:], g[(2 * s + k) % SB][:, h], start=False,
                                                stop=k == NK - 1 and h == 1)
                    last.then_inc(summed, 1)
                    if chunk is not None and k < HT // 4:
                        key_product(HT // 2 + 2 * k)
                        last = key_product(HT // 2 + 2 * k + 1)
                        if k == HT // 4 - 1:
                            last.then_inc(k_mm, 1)

            pe.sem_inc(summed, SB + 1)
            pe.wait_ge(par_ld, 16 * 5)
            blocks(pe, body)


class Norm:

    def __init__(self, nc, res, phase, v, mean_w, eps, sq, std, rstd, ps_mean, ps_var, summed=False, shared=0, like=None):
        def sem(n):
            return res.sem(f"{phase}_ln_{n}")

        self.nc, self.v, self.summed = nc, v, summed
        self.mean_w, self.eps = mean_w, eps
        self.sq = sq
        self.std, self.rstd = std, rstd
        self.total, self.sq_total = std, rstd
        self.ps_mean, self.ps_var = ps_mean, ps_var
        self.by_vector = HT - shared
        self.parts = v.shape[2] // L
        self.const_set = like.const_set if like else sem("const_set")
        self.set, self.total_done, self.mean_done = sem("set"), sem("total_done"), sem("mean_done")
        self.c_done, self.sq_done = sem("c_done"), sem("sq_done")
        self.sq_used = sem("sq_used")
        self.var_done, self.std_done, self.rstd_done = sem("var_done"), sem("std_done"), sem("rstd_done")
        self.out_done, self.out_pool, self.stored = sem("out_done"), sem("out_pool"), sem("stored")

    def tile(self, m):
        return self.v[:, m].rearrange("p (b l) -> p b l", b=self.parts)

    def constants(self):
        self.nc.vector.memset(self.mean_w[:], 1.0 / H).then_inc(self.const_set, 1)
        self.nc.vector.memset(self.eps[:, 0:1], LN_EPS).then_inc(self.const_set, 1)

    def setup(self):
        self.nc.vector.memset(self.total[:], 0.0).then_inc(self.set, 1)
        self.nc.vector.memset(self.sq_total[:], 0.0).then_inc(self.set, 1)

    def add(self, dve, m):
        dve.wait_ge(self.set, 2)
        dve.wait_ge(self.total_done, m)
        self.nc.vector.tensor_tensor(self.total[:], self.total[:], self.tile(m), ALU.add).then_inc(self.total_done, 1)

    def mean(self, pe):
        pe.wait_ge(self.const_set, 2)
        pe.wait_ge(self.total_done, HT)
        for b in range(self.parts):
            last = self.nc.tensor.matmul(self.ps_mean[:, b], self.mean_w[:], self.total[:, b], start=True, stop=True)
        last.then_inc(self.mean_done, 1)

    def center(self, dve):
        for m in range(HT):
            self.center_tile(dve, m)
            if self.summed and m:
                self.add_square(dve, m - 1)
        if self.summed:
            self.add_square(dve, HT - 1)

    def center_tile(self, dve, m):
        dve.wait_ge(self.mean_done, 1)
        self.nc.vector.tensor_tensor(self.tile(m), self.tile(m), self.ps_mean, ALU.subtract).then_inc(self.c_done, 1)

    def add_square(self, dve, m):
        dve.wait_ge(self.sq_done, m + 1)
        if m:
            dve.wait_ge(self.sq_used, m)
        self.nc.vector.tensor_tensor(self.sq_total[:], self.sq_total[:], self.sq[m % 2][:], ALU.add).then_inc(self.sq_used, 1)

    def variance(self, pe):
        if self.summed:
            pe.wait_ge(self.sq_used, HT)
            for b in range(self.parts):
                last = self.nc.tensor.matmul(self.ps_var[:, b], self.mean_w[:], self.sq_total[:, b], start=True, stop=True)
        else:
            for m in range(HT):
                pe.wait_ge(self.sq_done, m + 1)
                for b in range(self.parts):
                    last = self.nc.tensor.matmul(self.ps_var[:, b], self.mean_w[:], self.sq[m % 2][:, b],
                                                 start=m == 0, stop=m == HT - 1)
                if m < HT - 1:
                    last.then_inc(self.sq_used, 1)
        last.then_inc(self.var_done, 1)

    def table(self, act):
        act.wait_ge(self.const_set, 2)
        self.nc.scalar.activation(self.eps[:, 1:2], self.eps[:, 0:1], ACT.Sqrt).then_inc(self.const_set, 1)

    def squares(self, act, tiles):
        for m in tiles:
            act.wait_ge(self.c_done, m + 1)
            if m >= 2:
                act.wait_ge(self.sq_used, m - 1)
            self.nc.scalar.activation(self.sq[m % 2][:], self.tile(m), ACT.Square).then_inc(self.sq_done, 1)

    def root(self, act):
        act.wait_ge(self.var_done, 1)
        self.nc.scalar.activation(self.std[:], self.ps_var, ACT.Sqrt, bias=self.eps[:, 0:1]).then_inc(self.std_done, 1)

    def scale(self, dve):
        dve.wait_ge(self.std_done, 1)
        self.nc.vector.reciprocal(self.rstd[:], self.std[:]).then_inc(self.rstd_done, 1)
        dve.wait_ge(self.rstd_done, 1)
        dve.wait_ge(self.sq_done, HT)
        dve.wait_ge(self.c_done, HT)
        for m in range(self.by_vector):
            self.nc.vector.tensor_tensor(self.tile(m), self.tile(m), self.rstd[:], ALU.mult).then_inc(self.out_done, 1)

    def pool(self, pool):
        pool.wait_ge(self.rstd_done, 1)
        pool.wait_ge(self.c_done, HT)
        for m in range(self.by_vector, HT):
            self.nc.gpsimd.tensor_tensor(self.tile(m), self.tile(m), self.rstd[:], ALU.mult).then_inc(self.out_pool, 1)

    def wait_tile(self, eng, m):
        if m < self.by_vector:
            eng.wait_ge(self.out_done, m + 1)
        else:
            eng.wait_ge(self.out_pool, m - self.by_vector + 1)

    def sync(self, sp, out):
        for m in range(HT):
            self.wait_tile(sp, m)
            sp.dma_start(out(m), self.v[:, m]).then_inc(self.stored, 16)

    def wait_stored(self, sp):
        sp.wait_ge(self.stored, 16 * HT)


def project_norm_qkv(nc, res, d):
    sb = Arena(nc, "mid")

    def sem(n):
        return res.sem("mid_" + n)

    KT = IT
    NSTEP = B * KT
    KW = KV * HD
    KF = KW // P
    QF = NH * HD // P
    NCH = B * S // L
    CC = CTX // L
    VT = L // P
    v = sb("v", [P, HT, TOK])
    wk_hi, wk_lo, wv_hi, wv_lo = (sb(n, [P, HT, KW], F32R) for n in ("wk_hi", "wk_lo", "wv_hi", "wv_lo"))
    kb = [sb(f"kb{s}", [P, L]) for s in range(2)]
    vb = [sb(f"vb{s}", [P, KW]) for s in range(2)]
    qb = [sb(f"qb{s}", [P, B, L]) for s in range(2)]
    h = sb("h", [P, HT, L])
    raw_at = Arena(nc, "mid_raw", sb.at)
    wraw = [raw_at(f"w{s}", [P, HT, KW]) for s in range(2)]
    norm_at = Arena(nc, "mid_norm", sb.at)
    wq = [sb(f"wq{s}", [P, HT, P]) for s in range(2)]
    wq_hi = [sb(f"wq_hi{s}", [P, HT, P], F32R) for s in range(2)]
    wq_lo = [sb(f"wq_lo{s}", [P, HT, P], F32R) for s in range(2)]
    mean_w, eps = sb("mean_w", [P, P]), sb("eps", [P, 2])
    sq = [norm_at(f"sq{s}", [P, B, L]) for s in range(2)]
    std, rstd = norm_at("std", [P, B, L]), norm_at("rstd", [P, B, L])
    h_hi0, h_lo0 = sb("h_hi0", [P, HT, L], F32R), sb("h_lo0", [P, HT, L], F32R)
    second = Arena(nc, "mid_second", sb.at)
    h_hi = [h_hi0, second("h_hi1", [P, HT, L], F32R)]
    h_lo = [h_lo0, second("h_lo1", [P, HT, L], F32R)]
    a = [sb(f"a{s}", [P, L]) for s in range(2)]
    a_hi = [sb(f"a_hi{s}", [P, L], F32R) for s in range(2)]
    a_lo = [sb(f"a_lo{s}", [P, L], F32R) for s in range(2)]
    w = [sb(f"w{s}", [P, H]) for s in range(2)]
    w_hi = [sb(f"w_hi{s}", [P, H], F32R) for s in range(2)]
    w_lo = [sb(f"w_lo{s}", [P, H], F32R) for s in range(2)]

    ps = res.bank("mid_ps", [P, 8, L])
    ps_k, ps_v, ps_q = ps[:, 0:2], ps[:, 2:4], ps[:, 4:8].rearrange("p (s b) l -> p s b l", s=2)
    ln = []
    for b in range(B):
        one = slice(b, b + 1)
        ln.append(Norm(nc, res, f"mid{b}", v[:, :, b * L:(b + 1) * L], mean_w, eps, [sq[s][:, one] for s in range(2)],
                       std[:, one], rstd[:, one], ps[:, 4 + b:5 + b], ps[:, 6 + b:7 + b], summed=True,
                       like=ln[0] if b else None))

    a_ld = [sem(f"a_ld{s}") for s in range(2)]
    w_ld = [sem(f"w_ld{s}") for s in range(2)]
    v_ld, h_ld = sem("v_ld"), sem("h_ld")
    wraw_ld = [sem(f"wraw_ld{s}") for s in range(2)]
    wq_ld = [sem(f"wq_ld{s}") for s in range(2)]
    k_st = [sem(f"k_st{s}") for s in range(2)]
    v_st = [sem(f"v_st{s}") for s in range(2)]
    q_st = [sem(f"q_st{s}") for s in range(2)]
    hi_done, lo_done = sem("hi_done"), sem("lo_done")
    used = sem("used")
    v_done = sem("v_done")
    kv_hi_done, kv_lo_done = sem("kv_hi_done"), sem("kv_lo_done")
    wq_hi_done, wq_lo_done = sem("wq_hi_done"), sem("wq_lo_done")
    h_hi_done, h_lo_done = sem("h_hi_done"), sem("h_lo_done")
    k_mm, v_mm, kb_done, vb_done = sem("k_mm"), sem("v_mm"), sem("kb_done"), sem("vb_done")
    q_mm, qb_done = sem("q_mm"), sem("qb_done")
    q_out = d["q"].rearrange("b (m p) l -> m p b l", p=P)

    def steps(eng, body, between):
        for i, (first, last) in enumerate(((0, 3), (3, 5), (5, KT // 2 - 1))):
            with eng.Fori(first, last) as j:
                for s in range(2):
                    body(2 * j + s, s)
            between[i]()
        for n in range(KT - 2, KT + 1):
            body(n, n % 2)
        between[3]()
        body(KT + 1, 1)
        between[4]()
        with eng.Fori(KT // 2 + 1, NSTEP // 2) as j:
            for s in range(2):
                body(2 * j + s, s)

    def nothing():
        pass

    def latent(q):
        b = q - B * CC
        return v[:, :, b * L:(b + 1) * L]

    with nc.Block() as block:
        @block.sync
        def _(sp):
            def load(n, s):
                sp.dma_start(w[s][:], d["w_out"][n % KT]).then_inc(w_ld[s], 16)
                sp.dma_start(a[s][:], d["y"][n]).then_inc(a_ld[s], 16)

            for s in range(2):
                load(s, s)
            def next_steps(first, last):
                with sp.Fori(first, last) as j:
                    for s in range(2):
                        sp.wait_ge(lo_done, 2 * (2 * j + s) + 2)
                        load(2 * j + s + 2, s)

            next_steps(0, 1)
            sp.dma_start(wraw[0][:], d["w_k"]).then_inc(wraw_ld[0], 16)
            next_steps(1, 3)
            sp.dma_start(wraw[1][:], d["w_v"]).then_inc(wraw_ld[1], 16)
            next_steps(3, 5)
            sp.dma_start(h[:], d["ctx"][0]).then_inc(h_ld, 16)
            for m in range(HT):
                if m % 4 == 0:
                    next_steps(5 + m // 4, 6 + m // 4)
                sp.dma_start(v[:, m], d["x_t"][m]).then_inc(v_ld, 16)
            next_steps(7, NSTEP // 2 - 1)
            for q in range(1, B * CC):
                sp.wait_ge(h_lo_done, q)
                sp.dma_start(h[:], d["ctx"][q]).then_inc(h_ld, 16)
            for b in range(B):
                ln[b].sync(sp, lambda m: d["x1"][m, :, b * L:(b + 1) * L])
            sp.wait_ge(kv_lo_done, 2)
            for s in range(2):
                sp.dma_start(wq[s][:], d["w_q"][s]).then_inc(wq_ld[s], 16)

            def store_q(m, s):
                sp.wait_ge(qb_done, m + 3)
                sp.dma_start(q_out[m], qb[s][:]).then_inc(q_st[s], 16)

            with sp.Fori(0, QF // 2 - 1) as j:
                for s in range(2):
                    store_q(2 * j + s, s)
                    sp.wait_ge(wq_lo_done, 2 * j + s + 1)
                    sp.dma_start(wq[s][:], d["w_q"][2 * j + s + 2]).then_inc(wq_ld[s], 16)
            for s in range(2):
                store_q(QF - 2 + s, s)
            for s in range(2):
                sp.wait_ge(q_st[s], 16 * QF // 2)
                sp.wait_ge(k_st[s], 16 * B * KF // 2)
                sp.wait_ge(v_st[s], 16 * NCH * VT // 2)
            for b in range(B):
                ln[b].wait_stored(sp)

        @block.scalar
        def _(act):
            def step(n, s):
                act.wait_ge(used, n)
                act.wait_ge(w_ld[s], 16 * (n // 2 + 1))
                nc.scalar.activation(w_hi[s][:], w[s][:], ACT.Copy).then_inc(hi_done, 1)
                act.wait_ge(a_ld[s], 16 * (n // 2 + 1))
                nc.scalar.activation(a_hi[s][:], a[s][:], ACT.Copy).then_inc(hi_done, 1)

            def split_w(b):
                act.wait_ge(wraw_ld[b], 16)
                nc.scalar.activation((wk_hi, wv_hi)[b][:], wraw[b][:], ACT.Copy).then_inc(kv_hi_done, 1)

            def split(q):
                if q < B * CC:
                    act.wait_ge(h_ld, 16 * (q + 1))
                    src = h[:]
                else:
                    act.wait_ge(ln[q - B * CC].out_done, HT)
                    src = latent(q)
                nc.scalar.activation(h_hi[q % 2][:], src, ACT.Copy).then_inc(h_hi_done, 1)

            def place(q):
                return (q // CC, q % CC * L) if q < B * CC else (q - B * CC, CTX)

            def keys(q):
                b, t0 = place(q)
                for i in range(KF):
                    n = KF * (q - B * CC) + i
                    act.wait_ge(k_mm, n + 1)
                    if n >= 2:
                        act.wait_ge(k_st[n % 2], 16 * (n // 2))
                    nc.scalar.activation(kb[n % 2][:], ps_k[:, n % 2], ACT.Copy).then_inc(kb_done, 1)
                    act.wait_ge(kb_done, n + 3)
                    act.dma_start(d["k"][b, i * P:(i + 1) * P, t0:t0 + L], kb[n % 2][:]).then_inc(k_st[n % 2], 16)

            def values(q):
                b, t0 = place(q)
                for i in range(VT):
                    if q == 2 and i in (1, 3):
                        ln[i // 2].root(act)
                    n = VT * q + i
                    act.wait_ge(v_mm, n + 1)
                    if n >= 2:
                        act.wait_ge(v_st[n % 2], 16 * (n // 2))
                    nc.scalar.activation(vb[n % 2][:], ps_v[:, n % 2, 0:KW], ACT.Copy).then_inc(vb_done, 1)
                    act.wait_ge(vb_done, n + 3)
                    act.dma_start(d["v"][b, :, :, t0 // P + i].rearrange("g p d -> p g d"),
                                  vb[n % 2][:].rearrange("p (g d) -> p g d", g=KV)).then_inc(v_st[n % 2], 16)
                    if q == 1:
                        half = HT // 2 * (i % 2)
                        ln[i // 2].squares(act, range(half, half + HT // 2))

            def split_wq(m, s):
                act.wait_ge(wq_ld[s], 16 * (m // 2) + 16)
                nc.scalar.activation(wq_hi[s][:], wq[s][:], ACT.Copy).then_inc(wq_hi_done, 1)

            def query(m, s):
                act.wait_ge(q_mm, m + 1)
                act.wait_ge(q_st[s], 16 * (m // 2))
                nc.scalar.activation(qb[s][:], ps_q[:, s], ACT.Copy).then_inc(qb_done, 1)

            for free in (kb_done, vb_done, qb_done):
                act.sem_inc(free, 2)
            steps(act, step, (lambda: split_w(0), lambda: split_w(1), lambda: split(0), nothing, nothing))
            act.wait_ge(used, NSTEP + 1)
            split(1)
            ln[0].table(act)
            for q in range(NCH):
                if q >= B * CC:
                    keys(q)
                values(q)
                if q + 2 < NCH:
                    split(q + 2)
                else:
                    split_wq(q - NCH + 2, q - NCH + 2)
            with act.Fori(0, QF // 2 - 1) as j:
                for s in range(2):
                    query(2 * j + s, s)
                    split_wq(2 * j + s + 2, s)
            for s in range(2):
                query(QF - 2 + s, s)

        @block.vector
        def _(dve):
            def step(n, s):
                dve.wait_ge(hi_done, 2 * n + 1)
                nc.vector.tensor_tensor(w_lo[s][:], w[s][:], f32(w_hi[s][:]), ALU.subtract).then_inc(lo_done, 1)
                dve.wait_ge(hi_done, 2 * n + 2)
                nc.vector.tensor_tensor(a_lo[s][:], a[s][:], f32(a_hi[s][:]), ALU.subtract).then_inc(lo_done, 1)

            def split_w(b):
                dve.wait_ge(kv_hi_done, b + 1)
                nc.vector.tensor_tensor((wk_lo, wv_lo)[b][:], wraw[b][:], f32((wk_hi, wv_hi)[b][:]),
                                        ALU.subtract).then_inc(kv_lo_done, 1)

            def split(q):
                dve.wait_ge(h_hi_done, q + 1)
                src = h[:] if q < B * CC else latent(q)
                nc.vector.tensor_tensor(h_lo[q % 2][:], src, f32(h_hi[q % 2][:]), ALU.subtract).then_inc(h_lo_done, 1)

            def add(b):
                dve.wait_ge(used, KT * (b + 1) + 1)
                dve.wait_ge(v_ld, 16 * HT)
                for m in range(HT):
                    c = v[:, m, b * L:(b + 1) * L]
                    nc.vector.tensor_tensor(c, c, ps[:, m], ALU.add).then_inc(v_done, 1)

            def total(b):
                if b == 0:
                    dve.wait_ge(kv_lo_done, 2)
                    ln[0].constants()
                ln[b].setup()
                dve.wait_ge(v_done, HT * (b + 1))
                for m in range(HT):
                    ln[b].add(dve, m)

            steps(dve, step, (lambda: split_w(0), lambda: split_w(1), lambda: split(0), lambda: add(0), lambda: total(0)))
            add(1)
            split(1)
            total(1)
            split(2)
            for b in range(B):
                ln[b].center(dve)
            split(3)
            for b in range(B):
                ln[b].scale(dve)
                split(B * CC + b)
            with dve.Fori(0, QF // 2) as j:
                for s in range(2):
                    dve.wait_ge(wq_hi_done, 2 * j + s + 1)
                    nc.vector.tensor_tensor(wq_lo[s][:], wq[s][:], f32(wq_hi[s][:]), ALU.subtract).then_inc(wq_lo_done, 1)

        @block.tensor
        def _(pe):
            def step(n, s, start=False, stop=False):
                pe.wait_ge(lo_done, 2 * n + 2)
                for m in range(HT):
                    if start and n > 0:
                        pe.wait_ge(v_done, m + 1)
                    c = slice(m * P, (m + 1) * P)
                    last = three_passes(nc, ps[:, m], w_hi[s][:, c], w_lo[s][:, c], a_hi[s][:], a_lo[s][:], start, stop)
                last.then_inc(used, 1)

            def keys(q):
                s = q % 2
                pe.wait_ge(h_lo_done, q + 1)
                for i in range(KF):
                    n = KF * (q - B * CC) + i
                    pe.wait_ge(kb_done, n + 1)
                    c = slice(i * P, (i + 1) * P)
                    for k in range(HT):
                        last = three_passes(nc, ps_k[:, n % 2], wk_hi[:, k, c], wk_lo[:, k, c],
                                            h_hi[s][:, k], h_lo[s][:, k], k == 0, k == HT - 1)
                    last.then_inc(k_mm, 1)

            def values(q, part):
                s = q % 2
                pe.wait_ge(h_lo_done, q + 1)
                for i in part:
                    pe.wait_ge(vb_done, VT * q + i + 1)
                    c = slice(i * P, (i + 1) * P)
                    for k in range(HT):
                        last = three_passes(nc, ps_v[:, i % 2, 0:KW], h_hi[s][:, k, c], h_lo[s][:, k, c],
                                            wv_hi[:, k], wv_lo[:, k], k == 0, k == HT - 1)
                    last.then_inc(v_mm, 1)

            pe.sem_inc(used, 1)
            for b in range(B):
                step(KT * b, 0, start=True)
                step(KT * b + 1, 1)
                with pe.Fori(KT // 2 * b + 1, KT // 2 * (b + 1) - 1) as j:
                    for s in range(2):
                        step(2 * j + s, s)
                step(KT * b + KT - 2, 0)
                step(KT * b + KT - 1, 1, stop=True)
            pe.wait_ge(v_done, HT + 4)
            pe.wait_ge(kv_lo_done, 2)
            values(0, range(VT))
            pe.wait_ge(v_done, B * HT)
            values(1, range(1))
            for b in range(B):
                ln[b].mean(pe)
            values(1, range(1, VT))
            values(2, [0])
            ln[0].variance(pe)
            values(2, [1, 2])
            ln[1].variance(pe)
            values(2, [3])
            for q in range(3, NCH):
                if q >= B * CC:
                    keys(q)
                values(q, range(VT))
            for b in range(B):
                pe.wait_ge(ln[b].std_done, 1)
            with pe.Fori(0, QF // 2) as j:
                for s in range(2):
                    pe.wait_ge(wq_lo_done, 2 * j + s + 1)
                    pe.wait_ge(qb_done, 2 * j + s + 1)
                    for b in range(B):
                        for k in range(HT):
                            last = three_passes(nc, ps_q[:, s, b], wq_hi[s][:, k], wq_lo[s][:, k],
                                                h_hi[b][:, k], h_lo[b][:, k], k == 0, k == HT - 1)
                    last.then_inc(q_mm, 1)


def attention(nc, res, d):
    sb = Arena(nc, "at")

    def sem(n):
        return res.sem("at_" + n)

    NHD = B * NH
    NW = B * KV
    SCALE = 1.0 / float(HD) ** 0.5
    NSL = 6
    NQ = 4
    LAG = 4
    NB1 = P - HD
    k = sb("k", [HD, S])
    v = sb("v", [P, ST, HD])
    q = [sb(f"q{s}", [HD, L]) for s in range(2)]
    k_hi = [sb(f"k_hi{s}", [HD + 1, S], F32R) for s in range(2)]
    k_lo = [sb(f"k_lo{s}", [HD, S], F32R) for s in range(2)]
    v_hi = [sb(f"v_hi{s}", [P, ST, P], F32R) for s in range(2)]
    v_lo = [sb(f"v_lo{s}", [P, ST, P], F32R) for s in range(2)]
    q_hi = [sb(f"q_hi{s}", [HD + 1, L], F32R) for s in range(NQ)]
    q_lo = [sb(f"q_lo{s}", [HD, L], F32R) for s in range(NQ)]
    p = [sb(f"p{s}", [P, L]) for s in range(NSL)]
    p_hi = [sb(f"p_hi{s}", [P, L], F32R) for s in range(NSL)]
    p_lo = [sb(f"p_lo{s}", [P, L], F32R) for s in range(NSL)]
    neg_max = sb("neg_max", [P, QT, HD + 1])
    ident = sb("ident", [P, P])
    rs = sb("rs", [P, L])
    on = [sb(f"on{s}", [HD, L]) for s in range(2)]

    NB = S // L
    ps_mx = res.bank("at_ps_mx", [P, NB, L])
    ps_s = [res.bank(f"at_ps_s{s}", [P, L]) for s in range(2)]
    ps_o = [res.bank(f"at_ps_o{s}", [P, L]) for s in range(2)]
    ps_t = res.bank("at_ps_t", [HD + 1, L])

    q_ld = [sem(f"q_ld{s}") for s in range(2)]
    on_st = [sem(f"on_st{s}") for s in range(2)]
    id_ld, kv_ld = sem("id_ld"), sem("kv_ld")
    set_done, pool_set, before_done = sem("set_done"), sem("pool_set"), sem("before_done")
    kv_hi_done, kv_lo_done = sem("kv_hi_done"), sem("kv_lo_done")
    q_hi_done, q_lo_done = sem("q_hi_done"), sem("q_lo_done")
    mx_mm, max_done, t_mm, row_done = sem("mx_mm"), sem("max_done"), sem("t_mm"), sem("row_done")
    s_mm, p_hi_done, pv_mm = sem("s_mm"), sem("p_hi_done"), sem("pv_mm")
    exp_done = sem("exp_done")
    p_lo_done = sem("p_lo_done")
    rs_done, on_done = sem("rs_done"), sem("on_done")

    def heads(eng, body):
        with eng.Fori(0, NW // 2) as j:
            for s in range(2):
                for g in range(G):
                    body(2 * G * j + G * s + g, 2 * j + s, g, s)

    SET, POOL_SET = 5, 2 + 2 * LAG

    with nc.Block() as block:
        @block.sync
        def _(sp):
            def load_kv(w):
                sp.dma_start(k[:], d["k"].rearrange("b (g e) s -> (b g) e s", g=KV)[w]).then_inc(kv_ld, 16)
                sp.dma_start(v[:], d["v"].rearrange("b g p t d -> (b g) p t d")[w]).then_inc(kv_ld, 16)

            def load_q(hd, s):
                sp.dma_start(q[s][:], d["q"].rearrange("b (h e) l -> (b h) e l", h=NH)[hd % NHD]).then_inc(q_ld[s], 16)

            def store(hd, s):
                sp.wait_ge(on_done, 3 * hd + 3)
                sp.dma_start(d["attn"][hd], on[s][:]).then_inc(on_st[s], 16)

            def body(hd, w, g, s):
                if g == 0:
                    sp.wait_ge(kv_lo_done, 2 * w + 2)
                    load_kv((w + 1) % NW)
                sp.wait_ge(q_lo_done, hd + 2)
                load_q(hd + 3, 1 - g % 2)
                store(hd, g % 2)

            load_q(0, 0)
            load_kv(0)
            load_q(1, 1)
            sp.dma_start(ident[:], d["ident"]).then_inc(id_ld, 16)
            sp.wait_ge(q_lo_done, 1)
            load_q(2, 0)
            heads(sp, body)
            store(NHD, 0)
            sp.wait_ge(on_st[0], 16 * (NHD // 2 + 1))
            sp.wait_ge(on_st[1], 16 * (NHD // 2))
            sp.wait_ge(q_ld[0], 16 * (NHD // 2 + 2))
            sp.wait_ge(q_ld[1], 16 * (NHD // 2 + 1))
            sp.wait_ge(kv_ld, 32 * (NW + 1))

        @block.scalar
        def _(act):
            def split_kv(w, s, part):
                act.wait_ge(kv_ld, 32 * (w + 1))
                if part < 3:
                    c = slice(part * L, (part + 1) * L)
                    nc.scalar.activation(k_hi[s][0:HD, c], k[:, c], ACT.Copy).then_inc(kv_hi_done, 1)
                else:
                    c = slice((part - 3) * ST // 3, (part - 2) * ST // 3)
                    nc.scalar.activation(v_hi[s][:, c, 0:HD], v[:, c], ACT.Copy).then_inc(kv_hi_done, 1)

            def queries(hd, s):
                act.wait_ge(q_ld[s % 2], 16 * (hd // 2 + 1))
                nc.scalar.activation(q_hi[s][0:HD], q[s % 2][:], ACT.Copy).then_inc(q_hi_done, 1)

            def row(hd, s):
                act.wait_ge(t_mm, hd + 1)
                nc.scalar.activation(q_hi[s][HD:HD + 1], ps_t[HD:HD + 1], ACT.Copy).then_inc(row_done, 1)

            def body(hd, w, g, s):
                for t in range(ST):
                    n = ST * hd + t
                    act.wait_ge(s_mm, n + 1)
                    act.wait_ge(p_lo_done, n + 1)
                    nc.scalar.activation(p[t % NSL][:], ps_s[t % 2][:], ACT.Exp, scale=SCALE).then_inc(exp_done, 1)
                    act.wait_ge(exp_done, n + 3)
                    act.wait_ge(pv_mm, n + 1)
                    nc.scalar.activation(p_hi[t % NSL][:], p[t % NSL][:], ACT.Copy).then_inc(p_hi_done, 1)
                    if t == 6:
                        queries(hd + 2, (g + 2) % NQ)
                    if 5 <= t <= 10 and g == 1:
                        act.wait_ge(pv_mm, NSL + ST * G * w)
                        split_kv(w + 1, 1 - s, t - 5)
                    if t == 10:
                        row(hd + 1, (g + 1) % NQ)

            act.sem_inc(exp_done, 2)
            queries(0, 0)
            for part in range(6):
                split_kv(0, 0, part)
            queries(1, 1)
            row(0, 0)
            act.wait_ge(before_done, 1)
            heads(act, body)

        @block.vector
        def _(dve):
            def split_k(w, s):
                dve.wait_ge(kv_hi_done, 6 * w + 6)
                nc.vector.tensor_tensor(k_lo[s][:], k[:], f32(k_hi[s][0:HD]), ALU.subtract).then_inc(kv_lo_done, 1)

            def split_v(w, s):
                dve.wait_ge(kv_hi_done, 6 * w + 6)
                nc.vector.tensor_tensor(v_lo[s][:, :, 0:HD], v[:], f32(v_hi[s][:, :, 0:HD]),
                                        ALU.subtract).then_inc(kv_lo_done, 1)

            def queries(hd, s):
                dve.wait_ge(q_hi_done, hd + 1)
                nc.vector.tensor_tensor(q_lo[s][:], q[s % 2][:], f32(q_hi[s][0:HD]), ALU.subtract).then_inc(q_lo_done, 1)

            def maximum(hd, i):
                dve.wait_ge(mx_mm, QT * hd + i + 1)
                dve.wait_ge(t_mm, hd)
                nc.vector.tensor_reduce(neg_max[:, i, HD:HD + 1], ps_mx[:].rearrange("p n l -> p (n l)"), AX_X,
                                        ALU.max, negate=True).then_inc(max_done, 1)

            def reciprocals(hd, e):
                dve.wait_ge(pv_mm, NSL + ST * hd)
                dve.wait_ge(on_done, 3 * hd)
                nc.vector.reciprocal(rs[HD:P], ps_o[1 - e][HD:P]).then_inc(rs_done, 1)

            def divide(hd, e):
                dve.wait_ge(rs_done, hd + 1)
                dve.wait_ge(on_st[e], 16 * (hd // 2))
                for c in range(0, HD, NB1):
                    nc.vector.tensor_tensor(on[e][c:c + NB1], ps_o[1 - e][c:c + NB1], rs[HD:P], ALU.mult).then_inc(on_done, 1)

            def body(hd, w, g, s):
                maximum(hd + 1, 0)
                maximum(hd + 1, 1)
                reciprocals(hd, g % 2)
                maximum(hd + 1, 2)
                divide(hd, g % 2)
                maximum(hd + 1, 3)
                queries(hd + 2, (g + 2) % NQ)
                if g == 1:
                    split_k(w + 1, 1 - s)
                    split_v(w + 1, 1 - s)

            nc.vector.memset(neg_max[:], 0.0).then_inc(set_done, 1)
            for s in range(2):
                nc.vector.memset(k_hi[s][HD:HD + 1].bitcast(F32), 1.0).then_inc(set_done, 1)
            nc.vector.memset(v_hi[0][:, :, HD:P].bitcast(F32), 1.0).then_inc(set_done, 1)
            nc.vector.memset(v_lo[0][:, :, HD:P].bitcast(F32), 0.0).then_inc(set_done, 1)
            dve.wait_ge(set_done, SET)
            maximum(0, 0)
            queries(0, 0)
            maximum(0, 1)
            split_k(0, 0)
            maximum(0, 2)
            split_v(0, 0)
            maximum(0, 3)
            queries(1, 1)
            heads(dve, body)
            reciprocals(NHD, 0)
            divide(NHD, 0)

        @block.gpsimd
        def _(pool):
            def body(hd, w, g, s):
                for t in range(ST):
                    n = ST * hd + t
                    pool.wait_ge(p_hi_done, n + 1)
                    pool.wait_ge(pv_mm, n + 1)
                    nc.gpsimd.tensor_tensor(p_lo[t % NSL][:], p[t % NSL][:], f32(p_hi[t % NSL][:]),
                                            ALU.subtract).then_inc(p_lo_done, 1)

            for t in range(NSL - LAG, NSL):
                nc.gpsimd.memset(p_hi[t][:].bitcast(F32), 1.0).then_inc(pool_set, 1)
                nc.gpsimd.memset(p_lo[t][:].bitcast(F32), 0.0).then_inc(pool_set, 1)
            nc.gpsimd.memset(v_hi[1][:].bitcast(F32), 1.0).then_inc(pool_set, 1)
            nc.gpsimd.memset(v_lo[1][:].bitcast(F32), 0.0).then_inc(pool_set, 1)
            pool.sem_inc(p_lo_done, NSL)
            heads(pool, body)

        @block.tensor
        def _(pe):
            def maximum(hd, w, e, s, i):
                if i == 0:
                    pe.wait_ge(q_hi_done, hd + 1)
                    pe.wait_ge(kv_hi_done, 6 * w + 3)
                pe.wait_ge(max_done, QT * hd + i)
                for c in range(NB):
                    last = nc.tensor.matmul(ps_mx[:, c], q_hi[e][0:HD, i * P:(i + 1) * P],
                                            k_hi[s][0:HD, c * L:(c + 1) * L], start=True, stop=True)
                last.then_inc(mx_mm, 1)

            def transposes(hd):
                pe.wait_ge(max_done, QT * hd + QT)
                pe.wait_ge(row_done, hd)
                for i in range(QT):
                    last = nc.tensor.transpose(ps_t[0:HD + 1, i * P:(i + 1) * P], neg_max[:, i], ident[:])
                last.then_inc(t_mm, 1)

            def scores(hd, t, e, s):
                pe.wait_ge(exp_done, ST * hd + t + 1)
                c = slice(t * P, (t + 1) * P)
                nc.tensor.matmul(ps_s[t % 2][:], k_hi[s][:, c], q_hi[e][:], start=True, stop=False)
                nc.tensor.matmul(ps_s[t % 2][:], k_hi[s][0:HD, c], q_lo[e][:], start=False, stop=False)
                nc.tensor.matmul(ps_s[t % 2][:], k_lo[s][:, c], q_hi[e][0:HD], start=False, stop=True).then_inc(s_mm, 1)

            def values(bank, t, s):
                three_passes(nc, ps_o[bank][:], v_hi[s][:, t], v_lo[s][:, t], p_hi[t % NSL][:], p_lo[t % NSL][:],
                             t == 0, t == ST - 1).then_inc(pv_mm, 1)

            def body(hd, w, g, s):
                e = g % 2
                pe.wait_ge(row_done, hd + 1)
                pe.wait_ge(q_lo_done, hd + 1)
                if g == 0:
                    pe.wait_ge(kv_lo_done, 2 * w + 2)
                for t in range(ST):
                    scores(hd, t, g, s)
                    pe.wait_ge(p_lo_done, NSL + ST * hd + t - LAG + 1)
                    if t < LAG:
                        values(1 - e, ST + t - LAG, s if g else 1 - s)
                    else:
                        if t == LAG:
                            pe.wait_ge(on_done, 3 * hd)
                        values(e, t - LAG, s)
                    if t in (0, 2, 5, 7):
                        nw = w + 1 if g == G - 1 else w
                        maximum(hd + 1, nw, (g + 1) % NQ, 1 - s if g == G - 1 else s, (0, 2, 5, 7).index(t))
                    if t == 10:
                        transposes(hd + 1)

            for i in range(QT):
                maximum(0, 0, 0, 0, i)
            pe.wait_ge(id_ld, 16)
            pe.wait_ge(set_done, SET)
            pe.wait_ge(pool_set, POOL_SET)
            nc.tensor.matmul(ps_o[1][:], v_hi[1][:, 0], p_hi[NSL - 1][:], start=True, stop=False).then_inc(before_done, 1)
            pe.sem_inc(pv_mm, NSL - LAG)
            transposes(0)
            heads(pe, body)
            for t in range(ST - LAG, ST):
                pe.wait_ge(p_lo_done, NSL + ST * (NHD - 1) + t + 1)
                values(1, t, 1)


def attention_out_feed_forward(nc, res, d, attn, out):
    KT = NH * HD // P
    KH = KT // 2
    NLB = 2 * HT
    sb = Arena(nc, "ff")

    def sem(n):
        return res.sem("ff_" + n)

    attn_at = Arena(nc, "ff_attn", sb.at)
    a_hi, a_lo = zip(*((attn_at(f"a_hi{b}", [P, KT, L], F32R), attn_at(f"a_lo{b}", [P, KT, L], F32R)) for b in range(B)))
    x_hi, x_lo = zip(*((sb(f"x_hi{b}", [P, HT, L], F32R), sb(f"x_lo{b}", [P, HT, L], F32R)) for b in range(B)))
    assert HT <= KT
    h_hi, h_lo = sb("h_hi", [P, CF, B, L], F32R), sb("h_lo", [P, CF, B, L], F32R)
    assert attn_at.at <= sb.at
    y = sb("y", [P, HT, TOK])
    wo_at = Arena(nc, "ff_wo", sb.at)
    wo = [wo_at(f"wo{s}", [P, KH, P]) for s in range(2)]
    wo_hi = [wo_at(f"wo_hi{s}", [P, KH, P], F32R) for s in range(2)]
    wo_lo = [wo_at(f"wo_lo{s}", [P, KH, P], F32R) for s in range(2)]
    w, w_hi, w_lo = [None] * 4, [None] * 4, [None] * 4
    for s in (1, 3, 0, 2):
        if s == 0:
            raw1 = Arena(nc, "ff_raw1", sb.at)("a_raw", [P, KT, L])
        w[s] = sb(f"w{s}", [P, HT, P])
        w_hi[s], w_lo[s] = sb(f"w_hi{s}", [P, HT, P], F32R), sb(f"w_lo{s}", [P, HT, P], F32R)
        assert s != 3 or wo_at.at <= sb.at
    raw_at = sb.at
    w2 = [sb(f"w2_{s}", [P, CF, P]) for s in range(2)]
    w2_hi = [sb(f"w2_hi{s}", [P, CF, P], F32R) for s in range(2)]
    w2_lo = [sb(f"w2_lo{s}", [P, CF, P], F32R) for s in range(2)]
    sg = sb("sg", [P, B, L])
    hf = sb("hf", [P, B, L])
    ps_y = [res.bank(f"ff_ps_y{s}", [P, B, L])[:] for s in range(2)]
    std, rstd = sb("std", [P, B, L]), sb("rstd", [P, B, L])
    raw0 = Arena(nc, "ff_raw0", raw_at)("a_raw", [P, KT, L])
    assert raw_at + 4 * KT * L <= sb.at and KT * L <= 2 * 3 * HT * P
    a_raw = (raw0, raw1)
    scales = [sb(f"scale{n}", [P, FT * HT]) for n in range(3)]
    mean_w, eps = sb("mean_w", [P, P]), sb("eps", [P, 2])

    def norm(name, b, mean_bank, var_bank, **how):
        one = slice(b, b + 1)
        return Norm(nc, res, name, y[:, :, b * L:(b + 1) * L], mean_w, eps, [sg[:, one], hf[:, one]], std[:, one],
                    rstd[:, one], mean_bank, var_bank, **how)

    ps_o = [ps_y[s][:, 0] for s in range(2)]
    ln_x = [norm("ao0", 0, ps_y[0][:, 1:2], ps_y[1][:, 1:2], summed=True, shared=5)]
    ln_x.append(norm("ao1", 1, ps_y[0][:, 0:1], ps_y[1][:, 0:1], shared=3, like=ln_x[0]))
    ln_y = [norm(f"ff{b}", b, ps_y[0][:, b:b + 1], ps_y[1][:, b:b + 1], shared=3, like=ln_x[0]) for b in range(B)]
    ps_g, ps_u = res.bank("ff_ps_g", [P, B, L]), res.bank("ff_ps_u", [P, B, L])

    a_ld = [[sem(f"a_ld{b}_{i}") for i in range(KT // 2)] for b in range(B)]
    wo_ld = [sem(f"wo_ld{s}") for s in range(2)]
    v_ld = [sem(f"v_ld{i}") for i in range(2)]
    a_hi_done, a_lo_done = sem("a_hi_done"), sem("a_lo_done")
    wo_hi_done, wo_lo_done, wo_used = sem("wo_hi_done"), sem("wo_lo_done"), sem("wo_used")
    v_done = sem("v_done")
    sc_ld = sem("sc_ld")
    w_ld = [sem(f"w_ld{s}") for s in range(4)]
    w2_ld = [sem(f"w2_ld{s}") for s in range(2)]
    x_hi_done, x_lo_done = ([sem(f"x_{part}_done{b}") for b in range(B)] for part in ("hi", "lo"))
    ws_done, w_hi_done, w_lo_done = sem("ws_done"), sem("w_hi_done"), sem("w_lo_done")
    w2s_done, w2_hi_done, w2_lo_done = sem("w2s_done"), sem("w2_hi_done"), sem("w2_lo_done")
    g_mm, u_mm, y_mm = sem("g_mm"), sem("u_mm"), sem("y_mm")
    sg_done, hf_done, h_hi_done, h_lo_done, y_done = (sem("sg_done"), sem("hf_done"), sem("h_hi_done"),
                                                      sem("h_lo_done"), sem("y_done"))

    with nc.Block() as block:
        @block.sync
        def _(sp):
            def load_w(f, e):
                for i, name in enumerate(("w_1", "w_3")):
                    sp.dma_start(w[2 * i + e][:], d[name][f]).then_inc(w_ld[2 * i + e], 16)

            def load_a(b, pair):
                c = slice(2 * pair, 2 * pair + 2)
                sp.dma_start(a_raw[b][:, c], attn[c, :, b].rearrange("i p l -> p i l")).then_inc(a_ld[b][pair], 16)

            def load_v(i):
                c = slice(HT // 2 * i, HT // 2 * (i + 1))
                sp.dma_start(y[:, c], d["x1"][c].rearrange("m p t -> p m t")).then_inc(v_ld[i], 16)

            sp.dma_start(wo[0][:], d["w_o"][0]).then_inc(wo_ld[0], 16)
            for i in range(KT // 2):
                load_a(0, i)
            sp.dma_start(wo[1][:], d["w_o"][1]).then_inc(wo_ld[1], 16)
            load_v(0)

            def next_wo(n, s, load):
                sp.wait_ge(wo_lo_done, n - 1)
                sp.dma_start(wo[s][:], d["w_o"][load]).then_inc(wo_ld[s], 16)

            def next_pairs(first, last):
                with sp.Fori(first, last) as j:
                    for s in range(2):
                        next_wo(2 * j + s, s, 2 * j + s)

            next_pairs(1, 2)
            load_v(1)
            for i in range(3):
                next_pairs(i + 2, i + 3)
                load_a(1, 2 * i)
                load_a(1, 2 * i + 1)
            next_pairs(5, NLB // 2)
            for s in range(2):
                next_wo(NLB + s, s, s)
            sp.wait_ge(a_lo_done, KT)
            for n, name in enumerate(("s_1", "s_3", "s_2")):
                sp.dma_start(scales[n][:], d[name].partition_broadcast(P)).then_inc(sc_ld, 16)
            load_w(0, 0)
            for n in range(NLB + 2, B * NLB):
                next_wo(n, n % 2, n % NLB)
            sp.wait_ge(wo_used, B * NLB)
            load_w(1, 1)
            for s in range(2):
                sp.dma_start(w2[s][:], d["w_2"][s]).then_inc(w2_ld[s], 16)
            def chunk(c, tiles, pairs):
                for f in range(tiles):
                    sp.wait_ge(w_lo_done, 2 * (CF * c + f) + 2)
                    load_w(CF * c + f + 2, f % 2)
                with sp.Fori(0, pairs) as j:
                    for s in range(2):
                        sp.wait_ge(w2_lo_done, HT * c + 2 * j + s + 1)
                        sp.dma_start(w2[s][:], d["w_2"][HT * c + 2 * j + s + 2]).then_inc(w2_ld[s], 16)

            with sp.Fori(0, FC - 1) as c:
                chunk(c, CF, HT // 2)
            chunk(FC - 1, CF - 2, HT // 2 - 1)
            for b in range(B):
                ln_y[b].sync(sp, lambda m: out[m, :, b * L:(b + 1) * L])
            for b in range(B):
                ln_y[b].wait_stored(sp)

        @block.scalar
        def _(act):
            def split_w(f, e):
                for i in range(2):
                    n = 2 * f + i
                    act.wait_ge(ws_done, n + 1)
                    act.wait_ge((g_mm, u_mm)[i], f)
                    nc.scalar.activation(w_hi[2 * i + e][:], w[2 * i + e][:], ACT.Copy).then_inc(w_hi_done, 1)

            def split_w2(n, s):
                act.wait_ge(w2s_done, n + 1)
                act.wait_ge(y_mm, n)
                nc.scalar.activation(w2_hi[s][:], w2[s][:], ACT.Copy).then_inc(w2_hi_done, 1)

            def split_wo(n, s):
                act.wait_ge(wo_ld[s], 16 * (n // 2 + 1))
                nc.scalar.activation(wo_hi[s][:], wo[s][:], ACT.Copy).then_inc(wo_hi_done, 1)

            def split_x(b):
                for m in range(HT):
                    ln_x[b].wait_tile(act, m)
                    nc.scalar.activation(x_hi[b][:, m], y[:, m, b * L:(b + 1) * L], ACT.Copy).then_inc(x_hi_done[b], 1)

            def split_a(b, pair):
                c = slice(2 * pair, 2 * pair + 2)
                act.wait_ge(a_ld[b][pair], 16)
                nc.scalar.activation(a_hi[b][:, c], a_raw[b][:, c], ACT.Copy).then_inc(a_hi_done, 1)

            split_wo(0, 0)
            for i in range(KT // 2):
                split_a(0, i)
            split_wo(1, 1)
            for i, (first, last) in enumerate(((0, 4), (4, 6), (6, 8))):
                with act.Fori(first, last) as j:
                    for s in range(2):
                        act.wait_ge(wo_used, 2 * j + s + 1)
                        split_wo(2 * j + s + 2, s)
                split_a(1, 2 * i)
                split_a(1, 2 * i + 1)
            ln_x[0].table(act)
            for n in range(2, NLB):
                act.wait_ge(wo_used, NLB + n - 1)
                split_wo(NLB + n, n % 2)
                if 3 <= n < 3 + HT:
                    ln_x[0].squares(act, [n - 3])
                if n == 3 + HT + 1:
                    ln_x[0].root(act)
            for i in range(2):
                act.wait_ge(ws_done, i + 1)
                nc.scalar.activation(w_hi[2 * i][:], w[2 * i][:], ACT.Copy).then_inc(w_hi_done, 1)
            split_x(0)
            ln_x[1].squares(act, range(HT))
            ln_x[1].root(act)
            split_x(1)

            def chunk(c, last=False):
                for f in range(CF):
                    ff = CF * c + f
                    if f < CF - 1:
                        split_w(ff + 1, 1 - f % 2)
                    else:
                        for s in range(2):
                            split_w2(HT * c + s, s)
                    act.wait_ge(g_mm, ff + 2)
                    act.wait_ge(hf_done, ff)
                    nc.scalar.activation(sg[:], ps_g[:], ACT.Silu).then_inc(sg_done, 1)
                    act.wait_ge(hf_done, ff + 1)
                    act.wait_ge(y_mm, HT * c + 1)
                    nc.scalar.activation(h_hi[:, f], hf[:], ACT.Copy).then_inc(h_hi_done, 1)
                with act.Fori(0, HT // 2 - 1) as j:
                    for s in range(2):
                        split_w2(HT * c + 2 * j + s + 2, s)
                if not last:
                    split_w(CF * c + CF, 0)

            with act.Fori(0, FC - 1) as c:
                chunk(c)
            chunk(FC - 1, last=True)
            ln_y[0].table(act)
            for b in range(B):
                ln_y[b].squares(act, range(HT))
            for b in range(B):
                ln_y[b].root(act)

        @block.vector
        def _(dve):
            def scale_w(f, e):
                for i in range(2):
                    slot = 2 * i + e
                    dve.wait_ge(w_ld[slot], 16 * (f // 2 + 1))
                    sc = scales[i][:, bass.ds(f * HT, HT)].unsqueeze(2).to_broadcast([P, HT, P])
                    nc.vector.tensor_tensor(w[slot][:], w[slot][:], sc, ALU.mult).then_inc(ws_done, 1)

            def rest_w(f, e):
                for i in range(2):
                    slot = 2 * i + e
                    dve.wait_ge(w_hi_done, 2 * f + i + 1)
                    nc.vector.tensor_tensor(w_lo[slot][:], w[slot][:], f32(w_hi[slot][:]),
                                            ALU.subtract).then_inc(w_lo_done, 1)

            def scale_w2(n, s):
                dve.wait_ge(w2_ld[s], 16 * (n // 2 + 1))
                sc = scales[2][:, bass.ds(n * CF, CF)].unsqueeze(2).to_broadcast([P, CF, P])
                nc.vector.tensor_tensor(w2[s][:], w2[s][:], sc, ALU.mult).then_inc(w2s_done, 1)

            def rest_w2(n, s):
                dve.wait_ge(w2_hi_done, n + 1)
                nc.vector.tensor_tensor(w2_lo[s][:], w2[s][:], f32(w2_hi[s][:]), ALU.subtract).then_inc(w2_lo_done, 1)

            def add_y(c, m, s):
                dve.wait_ge(y_mm, HT * c + m + 2)
                c = y[:, m].rearrange("p (b l) -> p b l", b=B)
                nc.vector.tensor_tensor(c, c, ps_y[s], ALU.add).then_inc(y_done, 1)

            def split_wo(n, s):
                dve.wait_ge(wo_hi_done, n + 1)
                nc.vector.tensor_tensor(wo_lo[s][:], wo[s][:], f32(wo_hi[s][:]), ALU.subtract).then_inc(wo_lo_done, 1)

            def add_o(b, m, s):
                dve.wait_ge(wo_used, NLB * b + 2 * m + 2)
                c = ln_x[b].tile(m)
                nc.vector.tensor_tensor(c, c, ps_o[s].unsqueeze(1), ALU.add).then_inc(v_done, 1)
                dve.wait_ge(v_done, HT * b + m + 1)
                ln_x[b].add(dve, m)

            def split_x(b):
                for m in range(HT):
                    dve.wait_ge(x_hi_done[b], m + 1)
                    nc.vector.tensor_tensor(x_lo[b][:, m], y[:, m, b * L:(b + 1) * L], f32(x_hi[b][:, m]),
                                            ALU.subtract).then_inc(x_lo_done[b], 1)

            def split_a(b, pair):
                c = slice(2 * pair, 2 * pair + 2)
                dve.wait_ge(a_hi_done, KT // 2 * b + pair + 1)
                nc.vector.tensor_tensor(a_lo[b][:, c], a_raw[b][:, c], f32(a_hi[b][:, c]), ALU.subtract).then_inc(a_lo_done, 1)

            ln_x[0].constants()
            dve.sem_inc(y_done, 1)
            split_wo(0, 0)
            for i in range(KT // 2):
                split_a(0, i)
            split_wo(1, 1)
            dve.wait_ge(a_lo_done, KT // 2)
            for b in range(B):
                ln_x[b].setup()
            for i, (first, last) in enumerate(((0, 2), (2, 3), (3, 4))):
                if i < 2:
                    dve.wait_ge(v_ld[i], 16)
                with dve.Fori(first, last) as j:
                    for t in range(2):
                        for s in range(2):
                            split_wo(4 * j + 2 * t + s + 2, s)
                        add_o(0, 2 * j + t, t)
                split_a(1, 2 * i)
                split_a(1, 2 * i + 1)
            for n in range(2, NLB):
                split_wo(NLB + n, n % 2)
                if 3 <= n < 3 + HT:
                    ln_x[0].center_tile(dve, n - 3)
                if 4 <= n < 4 + HT:
                    ln_x[0].add_square(dve, n - 4)
                if n % 2:
                    add_o(1, n // 2 - 1, 1 - n // 2 % 2)
                if n == 4 + HT:
                    ln_x[0].scale(dve)
                    dve.wait_ge(sc_ld, 48)
                    scale_w(0, 0)
            rest_w(0, 0)
            split_x(0)
            add_o(1, HT - 1, 1)
            ln_x[1].center(dve)
            ln_x[1].scale(dve)
            split_x(1)

            def chunk(c, last=False):
                for f in range(CF):
                    ff = CF * c + f
                    if f < CF - 1:
                        scale_w(ff + 1, 1 - f % 2)
                        rest_w(ff + 1, 1 - f % 2)
                    else:
                        for s in range(2):
                            scale_w2(HT * c + s, s)
                            rest_w2(HT * c + s, s)
                    dve.wait_ge(sg_done, ff + 1)
                    dve.wait_ge(u_mm, ff + 2)
                    dve.wait_ge(h_lo_done, ff)
                    nc.vector.tensor_tensor(hf[:], sg[:], ps_u[:], ALU.mult).then_inc(hf_done, 1)
                    dve.wait_ge(h_hi_done, ff + 1)
                    nc.vector.tensor_tensor(h_lo[:, f], hf[:], f32(h_hi[:, f]), ALU.subtract).then_inc(h_lo_done, 1)
                if last:
                    for b in range(B):
                        ln_y[b].setup()
                    for m in range(HT):
                        if m + 2 < HT:
                            scale_w2(HT * c + m + 2, m % 2)
                        add_y(c, m, m % 2)
                        if m + 2 < HT:
                            rest_w2(HT * c + m + 2, m % 2)
                        dve.wait_ge(y_done, HT * c + m + 2)
                        for b in range(B):
                            ln_y[b].add(dve, m)
                    return
                with dve.Fori(0, HT // 2 - 1) as j:
                    for s in range(2):
                        n = HT * c + 2 * j + s
                        scale_w2(n + 2, s)
                        add_y(c, 2 * j + s, s)
                        rest_w2(n + 2, s)
                scale_w(CF * c + CF, 0)
                rest_w(CF * c + CF, 0)
                for s in range(2):
                    add_y(c, HT - 2 + s, s)

            with dve.Fori(0, FC - 1) as c:
                chunk(c)
            chunk(FC - 1, last=True)
            for b in range(B):
                ln_y[b].center(dve)
            for b in range(B):
                ln_y[b].scale(dve)

        @block.gpsimd
        def _(pool):
            for ln in (*ln_x, *ln_y):
                ln.pool(pool)

        @block.tensor
        def _(pe):
            def product_o(b, m, bank, s):
                pe.wait_ge(wo_lo_done, NLB * b + 2 * m + s + 1)
                for k in range(KH):
                    kk = s * KH + k
                    pe.wait_ge(a_lo_done, KT // 2 * b + kk // 2 + 1)
                    last = three_passes(nc, ps_o[bank], wo_hi[s][:, k], wo_lo[s][:, k], a_hi[b][:, kk], a_lo[b][:, kk],
                                        kk == 0, kk == KT - 1)
                last.then_inc(wo_used, 1)

            def product(ps, slot, batches=range(B)):
                for k in range(HT):
                    for b in batches:
                        pe.wait_ge(x_lo_done[b], k + 1)
                        last = three_passes(nc, ps[:, b], w_hi[slot][:, k], w_lo[slot][:, k], x_hi[b][:, k],
                                            x_lo[b][:, k], k == 0, k == HT - 1)
                return last

            def down(c, m, s):
                n = HT * c + m
                pe.wait_ge(w2_lo_done, n + 1)
                pe.wait_ge(y_done, n)
                for k in range(CF):
                    pe.wait_ge(h_lo_done, CF * c + k + 1)
                    for b in range(B):
                        last = three_passes(nc, ps_y[s][:, b], w2_hi[s][:, k], w2_lo[s][:, k], h_hi[:, k, b],
                                            h_lo[:, k, b], k == 0, k == CF - 1)
                last.then_inc(y_mm, 1)

            for free in (g_mm, u_mm, y_mm):
                pe.sem_inc(free, 1)
            def chunk(c, tiles):
                for f in tiles:
                    ff = CF * c + f
                    pe.wait_ge(w_lo_done, 2 * ff + 1)
                    pe.wait_ge(sg_done, ff)
                    product(ps_g, f % 2).then_inc(g_mm, 1)
                    pe.wait_ge(w_lo_done, 2 * ff + 2)
                    pe.wait_ge(hf_done, ff)
                    product(ps_u, 2 + f % 2).then_inc(u_mm, 1)
                with pe.Fori(0, HT // 2) as j:
                    for s in range(2):
                        down(c, 2 * j + s, s)

            for m in range(2):
                for s in range(2):
                    product_o(0, m, m, s)
            with pe.Fori(1, HT // 2) as j:
                for t in range(2):
                    pe.wait_ge(v_done, 2 * j + t - 1)
                    for s in range(2):
                        product_o(0, 2 * j + t, t, s)
            for m in range(HT):
                pe.wait_ge(v_done, HT + m - 1)
                for s in range(2):
                    product_o(1, m, m % 2, s)
                    if (m, s) == (0, 1):
                        ln_x[0].mean(pe)
                    if 2 * m + s == 2 + HT:
                        ln_x[0].variance(pe)
            ln_x[1].mean(pe)
            pe.wait_ge(w_lo_done, 1)
            product(ps_g, 0, [0])
            ln_x[1].variance(pe)
            pe.wait_ge(w_lo_done, 2)
            product(ps_u, 2, [0])
            product(ps_g, 0, [1]).then_inc(g_mm, 1)
            product(ps_u, 2, [1]).then_inc(u_mm, 1)
            chunk(0, range(1, CF))
            with pe.Fori(1, FC) as c:
                chunk(c, range(CF))
            for b in range(B):
                ln_y[b].mean(pe)
            for b in range(B):
                ln_y[b].variance(pe)


def decoder_layer(nc, d):
    for name, shape in (("bc", [B, 2 * NS, L]), ("sz", [B * IT, P, L]), ("dt", [B * IT, P, L]), ("y", [B * IT, P, L]), ("x1", [HT, P, TOK]),
                        ("q", [B, NH * HD, L]), ("k", [B, KV * HD, S]), ("v", [B, KV, P, ST, HD]), ("attn", [B * NH + 1, HD, L])):
        d[name] = nc.dram_tensor(name, shape, F32, kind="Internal").ap()
    xc = nc.alloc_sbuf_tensor_at("xc", [P, B * IT, L], F32, offset=TOP - 4 * B * IT * L)
    attn = d["attn"][1:].rearrange("(b h) e l -> b (h e) l", b=B).rearrange("b (i p) l -> i p b l", p=P)

    def phase(f, *args):
        res = Phase(nc)
        f(nc, res, *args)
        res.release()

    phase(mamba_in, d, xc)
    phase(mamba_scan, d, xc)
    phase(project_norm_qkv, d)
    phase(attention, d)
    phase(attention_out_feed_forward, d, attn, d["out"])


def kernel(**inputs):
    import concourse.bacc as bacc
    from concourse.bass_utils import run_bass_kernel_spmd

    a = {n: np.asarray(v) for n, v in inputs.items()}
    m, q, f = "L0_attn_", "L0_xattn_", "L0_ffn_"

    def tiles(w, mt, kt, split=1):
        w = w.reshape(mt, P, split, kt // split, -1).transpose(0, 2, 4, 3, 1)
        return w.reshape(mt * split, w.shape[2], kt // split, P)

    def cols(v):
        return v.reshape(-1, P).T

    x = a["x"].reshape(TOK, H).T
    group = np.repeat([0, 1, 2], [R, NS, NS])
    arrays = {
        "x_t": x.reshape(HT, P, TOK),
        "w_in": tiles(a[m + "in_proj_w"].T, 2 * IT, HT),
        "conv_w": a[m + "conv_w"].reshape(IT, P, KC).transpose(1, 0, 2),
        "conv_b": cols(a[m + "conv_b"]),
        "x_proj": a[m + "x_proj_w"].reshape(E, IT, P).transpose(2, 1, 0),
        "dt_w": a[m + "dt_proj_w"].reshape(IT, P, R).transpose(0, 2, 1),
        "dt_bias": cols(a[m + "dt_bias"]),
        "a_log": a[m + "A_log"].reshape(IT, P, NS).transpose(1, 0, 2),
        "d_param": cols(a[m + "D_param"]),
        "dt_ln": a[m + "dt_ln_w"].reshape(R, 1),
        "b_ln": a[m + "B_ln_w"].reshape(NS, 1),
        "c_ln": a[m + "C_ln_w"].reshape(NS, 1),
        "w_out": a[m + "out_proj_w"].T.reshape(IT, P, H),
        "ctx": a["ctx_4096"].reshape(B, CTX // L, L, HT, P).transpose(0, 1, 4, 3, 2).reshape(-1, P, HT, L),
        "w_q": tiles(a[q + "Wq"], NH * HD // P, HT),
        "w_k": a[q + "Wk"].reshape(KV * HD, HT, P).transpose(2, 1, 0),
        "w_v": a[q + "Wv"].reshape(KV * HD, HT, P).transpose(2, 1, 0),
        "w_o": tiles(a[q + "Wo"], HT, NH * HD // P, split=2),
        "w_1": tiles(a[f + "w1"], FT, HT),
        "w_3": tiles(a[f + "w3"], FT, HT),
        "w_2": a[f + "w2"].reshape(HT, P, FC, CF, P).transpose(2, 0, 4, 3, 1).reshape(FC * HT, P, CF, P),
        "s_1": a[f + "w1_scale"].reshape(-1),
        "s_3": a[f + "w3_scale"].reshape(-1),
        "s_2": a[f + "w2_scale"].reshape(HT, FC, CF).transpose(1, 0, 2).reshape(-1),
        "ident": np.eye(P, dtype=np.float32),
        "mean_w": ((group[:, None] == group[None, :]) / np.repeat([R, NS, NS], [R, NS, NS])[:, None]).astype(np.float32),
    }
    nc = bacc.Bacc("TRN2", target_bir_lowering=False, num_devices=1)
    arrays = {f"in_{n}": np.ascontiguousarray(v) for n, v in arrays.items()}
    d = {n[3:]: nc.dram_tensor(n, v.shape, F32, kind="ExternalInput").ap() for n, v in arrays.items()}
    d["out"] = nc.dram_tensor("out", (HT, P, TOK), F32, kind="ExternalOutput").ap()
    decoder_layer(nc, d)
    r = run_bass_kernel_spmd(nc, [arrays], core_ids=[0])
    return r.results[0]["out"].reshape(H, TOK).T.reshape(B, L, H)
```
